# Optimizing a Trainium2 kernel written in Bass

```python
import numpy as np
import jax
import jax.numpy as jnp

def _softmax(x, axis=-1):
    return jax.nn.softmax(x, axis=axis)

def _gelu(x):
    return jax.nn.gelu(x, approximate=True)

def _silu(x):
    return jax.nn.silu(x)

def _sigmoid(x):
    return jax.nn.sigmoid(x)

def _layernorm(x, axis=-1, eps=1e-05):
    m = jnp.mean(x, axis=axis, keepdims=True)
    v = jnp.var(x, axis=axis, keepdims=True)
    return (x - m) / jnp.sqrt(v + eps)

def _scatter_add(tgt, idx, src, axis=0):
    return tgt.at[idx].add(src)

def _segment_sum(src, seg, n):
    return jax.ops.segment_sum(src, seg, n)
kernel_name = 'mk_hybrid_d1_jaxref_r8_d0d799'

def setup_inputs(seed: int=0):
    np.random.seed(seed)
    _w = jnp.asarray

    def _L0_attn_a_setup():
        import jax, jax.numpy as jnp
        import numpy as np
        D_MODEL = 256
        N_HEAD = 16
        SEM_DIM = 128
        GEO_DIM = 128
        ATTN_DIM = 256
        ROPE_BASE = 10000.0

        def _rope(x, base=ROPE_BASE):
            S, d = (x.shape[-2], x.shape[-1])
            inv_freq = 1.0 / base ** (jnp.arange(0, d, 2, dtype=jnp.float32) / d)
            t = jnp.arange(S, dtype=jnp.float32)
            freqs = jnp.einsum('s,f->sf', t, inv_freq)
            cos, sin = (jnp.cos(freqs), jnp.sin(freqs))
            x1, x2 = (x[..., :d // 2], x[..., d // 2:])
            return jnp.concatenate([x1 * cos - x2 * sin, x1 * sin + x2 * cos], axis=-1).astype(x.dtype)

        def _split_heads(y, H):
            B, S, dim = y.shape
            return y.reshape(B, S, H, dim // H).transpose(0, 2, 1, 3)
        key = jax.random.key(seed)
        ks = jax.random.split(key, 7)
        B, S = (2, 256)
        sd = 0.02
        return {'x': jax.random.normal(ks[0], (B, S, D_MODEL), dtype=jnp.float32), 'Wq_sem': jax.random.normal(ks[1], (SEM_DIM, D_MODEL), dtype=jnp.float32) * sd, 'Wk_sem': jax.random.normal(ks[2], (SEM_DIM, D_MODEL), dtype=jnp.float32) * sd, 'Wq_geo': jax.random.normal(ks[3], (GEO_DIM, D_MODEL), dtype=jnp.float32) * sd, 'Wk_geo': jax.random.normal(ks[4], (GEO_DIM, D_MODEL), dtype=jnp.float32) * sd, 'Wv': jax.random.normal(ks[5], (ATTN_DIM, D_MODEL), dtype=jnp.float32) * sd, 'Wo': jax.random.normal(ks[6], (D_MODEL, ATTN_DIM), dtype=jnp.float32) * sd}
    _L0_attn_a_in = _L0_attn_a_setup()

    def _L0_attn_b_setup():
        import jax, jax.numpy as jnp
        import numpy as np
        B, N, DIM = (2, 256, 256)
        H, DK, DV = (16, 64, 128)
        DIM_INNER = (DK + DV) * H
        EPS = 1e-12

        def l2norm(t):
            n = jnp.linalg.norm(t, axis=-1, keepdims=True)
            return t / jnp.maximum(n, EPS)

        def tanh_norm(t):
            n = jnp.linalg.norm(t, axis=-1, keepdims=True)
            return jnp.tanh(n) * (t / jnp.maximum(n, EPS))

        def _split_heads(t):
            b, n, _ = t.shape
            return t.reshape(b, n, H, -1).transpose(0, 2, 1, 3)
        key = jax.random.key(seed)
        k1, k2, k3, k4 = jax.random.split(key, 4)
        tokens = jax.random.normal(k1, (B, N, DIM), dtype=jnp.float32)
        Wqg = jax.random.normal(k2, (DIM, DIM_INNER), dtype=jnp.float32) * DIM ** (-0.5)
        Wkv = jax.random.normal(k3, (DIM, DIM_INNER), dtype=jnp.float32) * DIM ** (-0.5)
        Wo = jax.random.normal(k4, (DV * H, DIM), dtype=jnp.float32) * (DV * H) ** (-0.5)
        ls_iaw = jnp.zeros((H,), dtype=jnp.float32)
        ls_hws = jnp.zeros((H,), dtype=jnp.float32)
        return {'tokens': tokens, 'Wqg': Wqg, 'Wkv': Wkv, 'Wo': Wo, 'ls_iaw': ls_iaw, 'ls_hws': ls_hws}
    _L0_attn_b_in = _L0_attn_b_setup()

    def _L0_ffn_setup():
        import jax, jax.numpy as jnp
        import numpy as np
        EPS = 1e-08

        def _quantize(w):
            gamma = jnp.mean(jnp.abs(w))
            return jnp.clip(jnp.round(w / (gamma + EPS)), -1.0, 1.0)

        def _bitlinear(x, w):
            return jnp.matmul(x, _quantize(w).T)
        key = jax.random.key(seed)
        k1, k2, k3, k4 = jax.random.split(key, 4)
        d, h = (256, 704)
        x = jax.random.normal(k1, (4, 256, d), dtype=jnp.float32)
        w1 = jax.random.normal(k2, (h, d), dtype=jnp.float32)
        w2 = jax.random.normal(k3, (h, d), dtype=jnp.float32)
        w3 = jax.random.normal(k4, (d, h), dtype=jnp.float32)
        return {'x': x, 'w1': w1, 'w2': w2, 'w3': w3}
    _L0_ffn_in = _L0_ffn_setup()
    _d = {'L0_attn_a_x': _L0_attn_a_in['x'], 'L0_attn_a_Wq_sem': _L0_attn_a_in['Wq_sem'], 'L0_attn_a_Wk_sem': _L0_attn_a_in['Wk_sem'], 'L0_attn_a_Wq_geo': _L0_attn_a_in['Wq_geo'], 'L0_attn_a_Wk_geo': _L0_attn_a_in['Wk_geo'], 'L0_attn_a_Wv': _L0_attn_a_in['Wv'], 'L0_attn_a_Wo': _L0_attn_a_in['Wo'], 'L0_attn_b_Wqg': _L0_attn_b_in['Wqg'], 'L0_attn_b_Wkv': _L0_attn_b_in['Wkv'], 'L0_attn_b_Wo': _L0_attn_b_in['Wo'], 'L0_attn_b_ls_iaw': _L0_attn_b_in['ls_iaw'], 'L0_attn_b_ls_hws': _L0_attn_b_in['ls_hws'], 'L0_ffn_w1': _L0_ffn_in['w1'], 'L0_ffn_w2': _L0_ffn_in['w2'], 'L0_ffn_w3': _L0_ffn_in['w3']}
    _x0 = _d['L0_attn_a_x']
    _d['L0_attn_a_x'] = jax.random.normal(jax.random.fold_in(jax.random.key(seed), 1), (4, 512, 256), dtype=_x0.dtype)
    del _x0
    return _d

def reference(L0_attn_a_x, L0_attn_a_Wq_sem, L0_attn_a_Wk_sem, L0_attn_a_Wq_geo, L0_attn_a_Wk_geo, L0_attn_a_Wv, L0_attn_a_Wo, L0_attn_b_Wqg, L0_attn_b_Wkv, L0_attn_b_Wo, L0_attn_b_ls_iaw, L0_attn_b_ls_hws, L0_ffn_w1, L0_ffn_w2, L0_ffn_w3):

    def _L0_attn_a_ref(x, Wq_sem, Wk_sem, Wq_geo, Wk_geo, Wv, Wo):
        import jax, jax.numpy as jnp
        import numpy as np
        D_MODEL = 256
        N_HEAD = 16
        SEM_DIM = 128
        GEO_DIM = 128
        ATTN_DIM = 256
        ROPE_BASE = 10000.0

        def _rope(x, base=ROPE_BASE):
            S, d = (x.shape[-2], x.shape[-1])
            inv_freq = 1.0 / base ** (jnp.arange(0, d, 2, dtype=jnp.float32) / d)
            t = jnp.arange(S, dtype=jnp.float32)
            freqs = jnp.einsum('s,f->sf', t, inv_freq)
            cos, sin = (jnp.cos(freqs), jnp.sin(freqs))
            x1, x2 = (x[..., :d // 2], x[..., d // 2:])
            return jnp.concatenate([x1 * cos - x2 * sin, x1 * sin + x2 * cos], axis=-1).astype(x.dtype)

        def _split_heads(y, H):
            B, S, dim = y.shape
            return y.reshape(B, S, H, dim // H).transpose(0, 2, 1, 3)
        B, S, _ = x.shape
        H = N_HEAD
        q_sem = _split_heads(x @ Wq_sem.T, H)
        k_sem = _split_heads(x @ Wk_sem.T, H)
        q_geo = _rope(_split_heads(x @ Wq_geo.T, H))
        k_geo = _rope(_split_heads(x @ Wk_geo.T, H))
        v = _split_heads(x @ Wv.T, H)
        q = jnp.concatenate([q_sem, q_geo], axis=-1)
        k = jnp.concatenate([k_sem, k_geo], axis=-1)
        scale = 1.0 / jnp.sqrt(jnp.asarray(q.shape[-1], dtype=jnp.float32))
        scores = jnp.einsum('bhqd,bhkd->bhqk', q, k).astype(jnp.float32) * scale
        causal = jnp.tril(jnp.ones((S, S), dtype=bool))
        scores = jnp.where(causal, scores, jnp.finfo(jnp.float32).min)
        attn = jax.nn.softmax(scores, axis=-1).astype(v.dtype)
        out = jnp.einsum('bhqk,bhkd->bhqd', attn, v)
        out = out.transpose(0, 2, 1, 3).reshape(B, S, ATTN_DIM)
        return out @ Wo.T

    def _L0_attn_b_ref(tokens, Wqg, Wkv, Wo, ls_iaw, ls_hws):
        import jax, jax.numpy as jnp
        import numpy as np
        B, N, DIM = (2, 256, 256)
        H, DK, DV = (16, 64, 128)
        DIM_INNER = (DK + DV) * H
        EPS = 1e-12

        def l2norm(t):
            n = jnp.linalg.norm(t, axis=-1, keepdims=True)
            return t / jnp.maximum(n, EPS)

        def tanh_norm(t):
            n = jnp.linalg.norm(t, axis=-1, keepdims=True)
            return jnp.tanh(n) * (t / jnp.maximum(n, EPS))

        def _split_heads(t):
            b, n, _ = t.shape
            return t.reshape(b, n, H, -1).transpose(0, 2, 1, 3)
        qg = _split_heads(tokens @ Wqg)
        kv = _split_heads(tokens @ Wkv)
        queries, gates = (qg[..., :DK], qg[..., DK:])
        keys, values = (kv[..., :DK], kv[..., DK:])
        queries, keys, values = (l2norm(queries), l2norm(keys), l2norm(values))
        sim = jnp.einsum('bhid,bhjd->bhij', queries, keys)
        r = 1.0 / (jnp.exp(ls_iaw) + 1.0)[None, :, None, None]
        attn = jnp.square(jax.nn.relu(1.0 - r * (1.0 - sim)))
        aggr = jnp.einsum('bhij,bhjd->bhid', attn, values)
        out = tanh_norm(aggr) * jnp.tanh(jax.nn.silu(gates))
        out = out * jnp.exp(ls_hws)[None, :, None, None]
        out = out.transpose(0, 2, 1, 3).reshape(tokens.shape[0], tokens.shape[1], H * DV)
        return out @ Wo

    def _L0_ffn_ref(x, w1, w2, w3):
        import jax, jax.numpy as jnp
        import numpy as np
        EPS = 1e-08

        def _quantize(w):
            gamma = jnp.mean(jnp.abs(w))
            return jnp.clip(jnp.round(w / (gamma + EPS)), -1.0, 1.0)

        def _bitlinear(x, w):
            return jnp.matmul(x, _quantize(w).T)
        x1 = _bitlinear(x, w1)
        x2 = _bitlinear(x, w2)
        hidden = jax.nn.sigmoid(x1) * x2
        return _bitlinear(hidden, w3)
    x = L0_attn_a_x
    x = x + _L0_attn_a_ref(_layernorm(x, axis=-1), L0_attn_a_Wq_sem, L0_attn_a_Wk_sem, L0_attn_a_Wq_geo, L0_attn_a_Wk_geo, L0_attn_a_Wv, L0_attn_a_Wo)
    x = x + _L0_ffn_ref(_layernorm(x, axis=-1), L0_ffn_w1, L0_ffn_w2, L0_ffn_w3)
    x = x + _L0_attn_b_ref(_layernorm(x, axis=-1), L0_attn_b_Wqg, L0_attn_b_Wkv, L0_attn_b_Wo, L0_attn_b_ls_iaw, L0_attn_b_ls_hws)
    x = x + _L0_ffn_ref(_layernorm(x, axis=-1), L0_ffn_w1, L0_ffn_w2, L0_ffn_w3)
    return x

_drawn_inputs = setup_inputs


def setup_inputs(seed=0):
    import zlib

    import numpy as np

    out = dict(_drawn_inputs(seed))
    spreads = {'L0_attn_b_ls_iaw': (0.0, 2.0), 'L0_attn_b_ls_hws': (0.0, 2.0)}
    factors = {'L0_attn_a_Wq_sem': 8.0,
     'L0_attn_a_Wk_sem': 8.0,
     'L0_attn_a_Wq_geo': 8.0,
     'L0_attn_a_Wk_geo': 8.0,
     'L0_attn_b_Wqg': 62.744,
     'L0_attn_b_Wkv': 52.681,
     'L0_attn_b_Wo': 52.014}
    for name, (base, spread) in spreads.items():
        noise = np.random.default_rng([zlib.crc32(name.encode()), seed]).standard_normal(out[name].shape)
        drawn = base * np.exp(spread * noise) if base else spread * noise
        out[name] = jnp.asarray(drawn.astype(out[name].dtype))
    for name, factor in factors.items():
        out[name] = (out[name] * factor).astype(out[name].dtype)
    return out
```

```python
from contextlib import ExitStack

import concourse.bass as bass
from concourse import mybir

F32 = mybir.dt.float32
F32R = mybir.dt.float32r
BF16 = mybir.dt.bfloat16
F16 = mybir.dt.float16
ALU = mybir.AluOpType
ACT = mybir.ActivationFunctionType
AX = mybir.AxisListType

P = 128
B, S, DM = 4, 512, 256
TOK = B * S
NT = TOK // P
TB = S // P
KD = DM // P
H = 16
DH = 16
NG = B * H // 4
SLOTS = 6
KROWS = SLOTS * DH
MROWS = 3
DK, DV = 64, 128
HW = 2 * DK + 2 * DV
FF = 704
NF = -(-FF // P)
FP = NF * P
LN_EPS, Q_EPS, NORM_EPS = 1e-5, 1e-8, 1e-12
MASKED = -1e30


def at(start, n):
    return slice(start, start + n) if isinstance(start, int) else bass.ds(start, n)


def known(v):
    return isinstance(v, int)


def program(nc, x, consts, wqk, wv, wo_a, w12, w3, wb, wo_b, ls, out):
    scratch = nc.dram_tensor("qk_parts", (2, 3, 2 * P, TOK), BF16, kind="Internal").ap()
    mscratch = nc.dram_tensor("max_parts", (2, MROWS, 4 * S), BF16, kind="Internal").ap()
    ctx = ExitStack()
    with ctx:
        def sb(name, shape, dt=F32):
            return ctx.enter_context(nc.sbuf_tensor(name, shape, dt))

        def sem(name):
            return ctx.enter_context(nc.semaphore(name))

        xres = sb("xres", [P, NT, DM])
        xT_hi = sb("xT_hi", [P, KD, TOK], F32R)
        xT_lo = sb("xT_lo", [P, KD, TOK], F32R)
        big_hi = sb("big_hi", [P, 1536], F32R)
        big_lo = sb("big_lo", [P, 1536], F32R)
        wv_hi = sb("wv_hi", [P, KD, DM], F32R)
        wv_lo = sb("wv_lo", [P, KD, DM], F32R)
        w12q = sb("w12q", [P, 2, KD, FP], F32R)
        w3q = sb("w3q", [P, NF, DM], F32R)
        woa = sb("woa", [P, 4, DM])
        cst = sb("cst", [P, 5, P])
        ident, mask32, sel, ones = (cst[:, i, :] for i in range(4))
        ident_b = sb("ident_b", [P, P], BF16)
        mask_b = sb("mask_b", [P, P], BF16)
        stats = sb("stats", [P, TB, 6])
        mv = sb("mv", [P, TB, 2])
        lnw = sb("lnw", [P, 3, TB])
        neghalf = sb("neghalf", [P, 16])
        eps = sb("eps", [P, TB])
        hold = sb("hold", [P, 1])
        xn = sb("xn", [P, TB, DM])
        ident_h = sb("ident_h", [P, P], F16)
        region = ExitStack()

        def sa(name, shape, dt=F32):
            return region.enter_context(nc.sbuf_tensor(name, shape, dt))

        U1 = sa("U1", [P, 11264])
        wqk_raw = U1[:, 4096:5632]
        wv_raw = U1[:, 5632:6144]
        rot = U1[:, 6144:8192].rearrange("p (b y t) -> p b y t", b=2, y=2)
        parts = U1[:, 8192:11264].bitcast(BF16).rearrange("p (b a y t) -> p b a y t", b=2, a=3, y=2)
        PT = U1[:, 0:10240].rearrange("p (b g c) -> p b g c", b=2, g=4)
        U2 = sa("U2", [P, 8192])
        qs = U2[:, 0:4096].bitcast(BF16).rearrange("p (r g t) -> p r g t", r=4, g=4)
        ks = U2[:, 4096:8192].bitcast(BF16).rearrange("p (r g t) -> p r g t", r=4, g=4)
        w12_raw = U2[:, 0:2 * KD * FP].rearrange("p (w k f) -> p w k f", w=2, k=KD)
        w3_raw = U2[:, 3072:3072 + NF * DM].rearrange("p (f c) -> p f c", f=NF)
        below = U2[:, 4608:4608 + KD * FP]
        junk = U2[:, 6144:6144 + KD * FP]
        trig = sa("trig", [P, 2, S])
        v_all = sa("v_all", [P, NG, TB, 4 * DH])
        vg = [sa(f"vg{i}", [P, TB, 4, 2 * DH]) for i in range(2)]
        OTs = sa("OTs", [P, S])
        rden = sa("rden", [P, S])
        aoT = sa("aoT", [P, S])
        mx = sa("mx", [P, 16])
        mxr = sa("mxr", [P, 16])
        m3 = sa("m3", [P, P], BF16)
        mT = sa("mT", [MROWS * 16, P], BF16)
        asum = sa("asum", [P, 3])
        thr = sa("thr", [P, 3, 3])
        region.close()
        wob = sb("wob", [P, H, DM])
        wb_raw = sb("wb_raw", [P, KD, HW])
        ls_sb = sb("ls_sb", [P, 2, H])
        bias = sb("bias", [P, TB])
        head = sb("head", [P, 4, H])
        sq = sb("sq", [P, TB, 2 * DV])
        ss = sb("ss", [P, 16])
        rs = sb("rs", [P, 16])
        qk = sb("qk", [P, TB, 2, DK])
        qk16 = sb("qk16", [P, TB, 6, DK], F16)
        kqT = [sb(f"kqT{i}", [P, 2, S], F16) for i in range(2)]
        qlT = [sb(f"qlT{i}", [P, S], F16) for i in range(2)]
        vn = [sb(f"vn{i}", [P, TB, DV]) for i in range(2)]
        relu = sb("relu", [P, 2, S])
        attn = sb("attn", [P, TB, S])
        sig = sb("sig", [P, S])
        silu = sb("silu", [P, S])
        gate = [sb(f"gate{i}", [P, S]) for i in range(2)]
        agg2 = sb("agg2", [P, S])
        gated = sb("gated", [P, S])
        norm = sb("norm", [P, 3, TB])
        fsig = sb("fsig", [P, 2, S])
        hid = sb("hid", [P, 2, S])
        psum = ctx.enter_context(nc.psum_tensor("psum", [P, 8 * 512], F32))
        bank = [psum[:, i * 512:(i + 1) * 512] for i in range(8)]

        x_in, const_in, wqk_in, wv_in, woa_in, ffn_in = (sem(n) for n in (
            "x_in", "const_in", "wqk_in", "wv_in", "woa_in", "ffn_in"))
        half_set, bf_const, wa_hi, wa_lo = (sem(n) for n in ("half_set", "bf_const", "wa_hi", "wa_lo"))
        as_done, as_tot, thr_set, below_set, wq_set = (sem(n) for n in (
            "as_done", "as_tot", "thr_set", "below_set", "wq_set"))
        ln_stats, ln_mv, ln_eps, ln_rstd, ln_nmr, ln_xn, ln_tp, ln_hi, ln_lo = (sem(n) for n in (
            "ln_stats", "ln_mv", "ln_eps", "ln_rstd", "ln_nmr", "ln_xn", "ln_tp", "ln_hi", "ln_lo"))
        pj_mm, pj_sem, pj_t, pj_rot, pj_p1, pj_r1, pj_p2, pj_p3, pj_out, v_mm, v_out = (sem(n) for n in (
            "pj_mm", "pj_sem", "pj_t", "pj_rot", "pj_p1", "pj_r1", "pj_p2", "pj_p3", "pj_out", "v_mm", "v_out"))
        ks_ones, vg_pad, vg_set, stack_in = (sem(n) for n in ("ks_ones", "vg_pad", "vg_set", "stack_in"))
        p1_mm, p1_red, m_split, m_tr, m_copied, m_out, m_in = (sem(n) for n in (
            "p1_mm", "p1_red", "m_split", "m_tr", "m_copied", "m_out", "m_in"))
        p2_mm, p2_exp, pv_mm, ot_copied, den_mm, den_inv, ao_set, oa_mm, x_a = (sem(n) for n in (
            "p2_mm", "p2_exp", "pv_mm", "ot_copied", "den_mm", "den_inv", "ao_set", "oa_mm", "x_a"))
        y_out = sem("y_out")
        m3_zero = sem("m3_zero")
        up_mm, sig_set, hid_set, hi_set, lo_set, dn_mm, x_f = (sem(n) for n in (
            "up_mm", "sig_set", "hid_set", "hi_set", "lo_set", "dn_mm", "x_f"))
        wob_in, wb_in, ls_in, ss_one, ls_exp, r_set, wb_hi, wb_lo = (sem(n) for n in (
            "wob_in", "wb_in", "ls_in", "ss_one", "ls_exp", "r_set", "wb_hi", "wb_lo"))
        kqv_mm, sq_set, red_set, ss_set, rs_set, rq_set, qk_set, vn_set, q_hi, q_lo, q_dup = (sem(n) for n in (
            "kqv_mm", "sq_set", "red_set", "ss_set", "rs_set", "rq_set", "qk_set", "vn_set", "q_hi", "q_lo", "q_dup"))
        tr_mm, tr_out, trl_mm, trl_out, gate_mm, gsig_set, silu_set, gate_set = (sem(n) for n in (
            "tr_mm", "tr_out", "trl_mm", "trl_out", "gate_mm", "gsig_set", "silu_set", "gate_set"))
        sim_mm, relu_set, attn_set, av_mm, agg2_set, gated_set, ssum_mm, ssum_out = (sem(n) for n in (
            "sim_mm", "relu_set", "attn_set", "av_mm", "agg2_set", "gated_set", "ssum_mm", "ssum_out"))
        red_set0, bias_set = sem("kq_red_set"), sem("bias_set")
        norm_set, tanh_set, factor_set, ob_mm, x_b = (sem(n) for n in (
            "norm_set", "tanh_set", "factor_set", "ob_mm", "x_b"))

        block = ctx.enter_context(nc.Block())

        P1_BANKS = [(3,), (0, 2), (1,)]
        P2_BANKS = [(0,), (1, 3), (2,)]
        P2_AT = [0, 512, 1024, 896]

        @block.sync
        def _(sp):
            for b in range(B):
                sp.dma_start(xres[:, b * TB:(b + 1) * TB, :],
                             x[b * S:(b + 1) * S, :].rearrange("(t p) c -> p t c", p=P)).then_inc(x_in, 16)
            sp.dma_start(cst[:, 0:4, :], consts[:, 0:4 * P].rearrange("p (i c) -> p i c", i=4)).then_inc(const_in, 16)
            sp.dma_start(trig[:, :, :], consts[:, 4 * P:4 * P + 2 * S].rearrange("p (i c) -> p i c", i=2)).then_inc(const_in, 16)
            sp.dma_start(wqk_raw.rearrange("p (k c) -> p k c", k=KD),
                         wqk.rearrange("(k p) c -> p k c", p=P)).then_inc(wqk_in, 16)
            sp.dma_start(wv_raw.rearrange("p (k c) -> p k c", k=KD),
                         wv.rearrange("(k p) c -> p k c", p=P)).then_inc(wv_in, 16)
            for w in range(2):
                sp.dma_start(w12_raw[:, w], w12[w].rearrange("(k p) f -> p k f", p=P)).then_inc(ffn_in, 16)
            sp.dma_start(w3_raw, w3.rearrange("(f p) c -> p f c", p=P)).then_inc(ffn_in, 16)
            sp.dma_start(woa[:, :, :], wo_a).then_inc(woa_in, 16)
            with sp.Fori(0, B) as b:
                tokens = sp.snap(b * S)
                for s in range(2):
                    sp.wait_ge(pj_p3, 2 * b + s + 1)
                    for a in range(3):
                        sp.dma_start(scratch[s, a].rearrange("(y p) t -> p y t", p=P)[:, :, at(tokens, S)],
                                     parts[:, s, a]).then_inc(pj_out, 16)
            sp.wait_ge(pj_out, B * 2 * 3 * 16)

            def load_stack(k):
                slot_at, head_at, token_at, read, loaded = (
                    v if known(k) else sp.snap(v) for v in (k % 4, (k % 4) * 4, (k // 4) * S, 12 * (k - 3), k * 12 * 16))
                if not known(k) or k >= 4:
                    sp.wait_ge(p2_mm, read)
                if not known(k) or k >= 1:
                    sp.wait_ge(stack_in, loaded)
                for s, dst, which in ((0, qs, (0, 0, 1, 0, 2, 1)), (1, ks, (0, 1, 0, 2, 0, 1))):
                    for slot, a in enumerate(which):
                        src = scratch[s, a].rearrange("(r h) t -> r h t", h=H)
                        sp.dma_start(dst[slot * DH:(slot + 1) * DH, at(slot_at, 1), :, :].rearrange("p r g t -> p (r g) t"),
                                     src[:, at(head_at, 4), at(token_at, S)]).then_inc(stack_in, 16)

            def move_max(k):
                half_at, slot_at, copied, written, read = (
                    v if known(k) else sp.snap(v) for v in (k % 2, k % 4, k + 1, (k + 1) * MROWS * 16, k * 16))
                sp.wait_ge(m_copied, copied)
                for a in range(MROWS):
                    if a == 1 and (not known(k) or k >= 1):
                        sp.wait_ge(m_in, read)
                    sp.dma_start(mscratch[at(half_at, 1), a, :].rearrange("o (r c) -> (o r) c", c=P),
                                 mT[a * 16:(a + 1) * 16, :]).then_inc(m_out, 16)
                sp.wait_ge(m_out, written)
                sp.dma_start(qs[KROWS:KROWS + MROWS, at(slot_at, 1), :, :].rearrange("p r g t -> p (r g t)"),
                             mscratch[at(half_at, 1), :, :].rearrange("o a n -> (o a) n")).then_inc(m_in, 16)

            sp.wait_ge(wq_set, 3)
            load_stack(0)
            load_stack(1)
            load_stack(2)
            move_max(0)
            load_stack(3)
            with sp.Fori(1, NG - 3) as k:
                move_max(k)
                load_stack(k + 3)
            move_max(NG - 3)
            move_max(NG - 2)
            move_max(NG - 1)

            sp.wait_ge(x_a, 2 * NG)
            sp.dma_start(wob[:, :, :], wo_b.rearrange("(h p) c -> p h c", p=P)).then_inc(wob_in, 16)
            sp.dma_start(ls_sb[:, :, :], ls).then_inc(ls_in, 16)

            def load_head(h):
                if not known(h) or h:
                    sp.wait_ge(wb_lo, h)
                sp.dma_start(wb_raw[:, :, :], wb[:, at(h, 1), :].rearrange("(k p) o c -> p k (o c)", p=P)).then_inc(wb_in, 16)

            load_head(0)
            with sp.Fori(1, H) as h:
                load_head(h)

            sp.wait_ge(x_f, 4 * B)
            for b in range(B):
                sp.dma_start(out[b * S:(b + 1) * S, :].rearrange("(t p) c -> p t c", p=P),
                             xres[:, b * TB:(b + 1) * TB, :]).then_inc(y_out, 16)
            sp.wait_ge(y_out, B * 16)

        @block.gpsimd
        def _(pool):
            pool.memset(neghalf[:, :], -0.5).then_inc(half_set, 1)
            pool.memset(eps[:, :], LN_EPS).then_inc(half_set, 1)
            for i in range(2):
                pool.memset(vg[i][:, :, :, :], 0.0).then_inc(vg_pad, 1)
            pool.wait_ge(vg_pad, 2)
            for i in range(2):
                pool.memset(vg[i][:, :, :, DH:DH + 1], 1.0).then_inc(vg_pad, 1)

            def ln_rstd_of(u):
                pool.wait_ge(ln_mv, TB * (u + 1))
                pool.tensor_tensor(lnw[:, 0, :], mv[:, :, 1], eps[:, :], ALU.add).then_inc(ln_eps, 1)
                pool.wait_ge(ln_eps, u + 1)
                pool.tensor_tensor(lnw[:, 1, :], lnw[:, 0, :], neghalf[:, 0:TB], ALU.pow).then_inc(ln_rstd, 1)

            pool.wait_ge(half_set, 2)
            for u in range(B):
                ln_rstd_of(u)
            pool.wait_ge(wq_set, 3)
            pool.memset(ks[KROWS:KROWS + MROWS, :, :, :], 1.0).then_inc(ks_ones, 1)
            pool.wait_ge(ks_ones, 1)
            pool.wait_ge(v_out, NT)
            pool.wait_ge(vg_pad, 4)

            def fill_vg(k, i):
                if not known(k) or k >= 2:
                    pool.wait_ge(pv_mm, k - 1)
                pool.tensor_copy(vg[i][:, :, :, 0:DH],
                                 v_all[:, at(k, 1), :, :].rearrange("p o j (g d) -> p (o j) g d", g=4)).then_inc(vg_set, 1)

            fill_vg(0, 0)
            fill_vg(1, 1)
            with pool.Fori(1, NG // 2) as i:
                fill_vg(2 * i, 0)
                fill_vg(2 * i + 1, 1)

            with pool.Fori(B, 3 * B) as u:
                ln_rstd_of(u)
            pool.wait_ge(ss_one, 1)
            for i in range(3):
                pool.wait_ge(ss_set, i + 1)
                if i:
                    pool.wait_ge(vn_set, i)
                pool.tensor_tensor(rs[:, :], ss[:, :], neghalf[:, :], ALU.pow).then_inc(rs_set, 1)
            with pool.Fori(3, B * H) as i:
                pool.wait_ge(ss_set, i + 1)
                pool.wait_ge(vn_set, i)
                pool.wait_ge(factor_set, i - 2)
                pool.tensor_tensor(rs[:, :], ss[:, :], neghalf[:, :], ALU.pow).then_inc(rs_set, 1)
            for i in range(B * H, B * H + 2):
                pool.wait_ge(ss_set, i + 1)
                pool.wait_ge(vn_set, B * H)
                pool.wait_ge(factor_set, i - 2)
                pool.tensor_tensor(rs[:, :], ss[:, :], neghalf[:, :], ALU.pow).then_inc(rs_set, 1)
            with pool.Fori(3 * B, 4 * B) as u:
                ln_rstd_of(u)

        @block.scalar
        def _(act):
            act.preload_act_table(ACT.Exp)
            act.wait_ge(const_in, 32)
            act.activation(ident_b[:, :], ident, ACT.Copy).then_inc(bf_const, 1)
            act.activation(mask_b[:, :], mask32, ACT.Copy).then_inc(bf_const, 1)
            act.activation(ident_h[:, :], ident, ACT.Copy).then_inc(bf_const, 1)
            act.wait_ge(wqk_in, 16)
            act.activation(big_hi[:, :], wqk_raw, ACT.Copy).then_inc(wa_hi, 1)
            act.wait_ge(wv_in, 16)
            act.activation(wv_hi[:, :, :].rearrange("p k c -> p (k c)"), wv_raw, ACT.Copy).then_inc(wa_hi, 1)

            def ln_high(u, b):
                for k in range(KD):
                    act.wait_ge(ln_tp, 2 * u + k + 1)
                    act.activation(xT_hi[:, k, at(b * S, S)], bank[6 + k], ACT.Copy).then_inc(ln_hi, 1)

            for b in range(B):
                ln_high(b, b)
            act.wait_ge(ffn_in, 3 * 16)
            for w in range(2):
                act.activation(junk.rearrange("p (k f) -> p k f", k=KD), w12_raw[:, w], ACT.Abs,
                               accum_out=asum[:, w:w + 1]).then_inc(as_done, 1)
                act.wait_ge(as_done, w + 1)
            act.activation(junk.rearrange("p (f c) -> p f c", c=DM), w3_raw, ACT.Abs, accum_out=asum[:, 2:3]).then_inc(as_done, 1)

            def parts_act(b):
                for s in range(2):
                    n = 2 * b + s
                    act.wait_ge(pj_mm, 3 * n + 1)
                    if not known(b) or b >= 1:
                        act.wait_ge(pj_p3, 2 * b)
                    act.activation(rot[:, s, 0], bank[2 + 3 * s][:, :], ACT.Copy).then_inc(pj_sem, 1)
                    act.wait_ge(pj_rot, n + 1)
                    act.wait_ge(pj_sem, n + 1)
                    if not known(b) or b >= 1:
                        act.wait_ge(pj_out, b * 96)
                    act.activation(parts[:, s, 0], rot[:, s], ACT.Copy).then_inc(pj_p1, 1)
                    act.wait_ge(pj_r1, n + 1)
                    act.activation(parts[:, s, 1], rot[:, s], ACT.Copy).then_inc(pj_p2, 1)

            parts_act(0)
            with act.Fori(1, B) as b:
                parts_act(b)
            with act.Fori(0, B) as b:
                for t in range(TB):
                    act.wait_ge(v_mm, TB * b + t + 1)
                    act.activation(v_all[:, at(4 * b, 4), t, :], bank[t % 2][:, 0:DM].rearrange("p (g c) -> p g c", g=4),
                                   ACT.Copy).then_inc(v_out, 1)

            def ot_out(k):
                act.wait_ge(pv_mm, k + 1)
                if not known(k) or k >= 1:
                    act.wait_ge(ao_set, 2 * k)
                act.activation(OTs[:, :], bank[5][:, :], ACT.Copy).then_inc(ot_copied, 1)

            def exps(k, i, g):
                for j in range(3):
                    act.wait_ge(p2_mm, 12 * k + 3 * g + j + 1)
                    if g == 0 and j == 0 and (not known(k) or k >= 2):
                        act.wait_ge(pv_mm, k - 1)
                    n = (512, 512, 256)[j]
                    act.activation(PT[:, i, g, 512 * j:512 * j + n], bank[2 + j][:, 0:n], ACT.Exp,
                                   scale=float(DH) ** -0.5).then_inc(p2_exp, 1)

            def max_out(k):
                act.wait_ge(m_tr, k + 1)
                if not known(k) or k >= 1:
                    act.wait_ge(m_out, k * MROWS * 16)
                act.activation(mT[:, :], bank[6].bitcast(BF16)[0:MROWS * 16, 0:P], ACT.Copy).then_inc(m_copied, 1)

            def act_group(k, i, p1=True, p2=True, tail=True):
                if tail:
                    ot_out(k - 2)
                if p2:
                    exps(k, i, 0)
                    for g in range(1, 4):
                        exps(k, i, g)
                if p1:
                    max_out(k + 2)

            act_group(-2, 0, p2=False, tail=False)
            act_group(-1, 1, p2=False, tail=False)
            act_group(0, 0, tail=False)
            act_group(1, 1, tail=False)
            act_group(2, 0)
            act_group(3, 1)
            with act.Fori(2, NG // 2 - 1) as i:
                act_group(2 * i, 0)
                act_group(2 * i + 1, 1)
            act_group(NG - 2, 0, p1=False)
            act_group(NG - 1, 1, p1=False)
            act_group(NG, 0, p1=False, p2=False)
            act_group(NG + 1, 1, p1=False, p2=False)

            def ffn_high(f, n):
                act.wait_ge(hid_set, n + 1)
                if not known(n) or n >= 3:
                    act.wait_ge(dn_mm, n - 2)
                act.activation(big_hi[:, (f % 3) * S:(f % 3 + 1) * S], hid[:, f % 2], ACT.Copy).then_inc(hi_set, 1)

            def ffn_act(v, u, b, ln):
                for f in range(NF):
                    n = NF * v + f
                    act.wait_ge(up_mm, 2 * n + 1)
                    if not known(n) or n >= 2:
                        act.wait_ge(hid_set, n - 1)
                    act.activation(fsig[:, f % 2], bank[f % 2][:, :], ACT.Sigmoid).then_inc(sig_set, 1)
                    if f:
                        ffn_high(f - 1, n - 1)
                    if ln and f == 4:
                        ln_high(u + 1, b + 1)
                ffn_high(NF - 1, NF * v + NF - 1)

            def ffn_act_all(first, u):
                act.preload_act_table(ACT.Sigmoid)
                ln_high(u, 0)
                ffn_act(first, u, 0, True)
                with act.Fori(1, B - 1) as b:
                    ffn_act(first + b, u + b, b, True)
                ffn_act(first + B - 1, u + B - 1, B - 1, False)

            ffn_act_all(0, B)

            def att_act(h, b, nxt, cur, prv, split):
                u, p = B * h + b, b % 2
                if prv:
                    act.wait_ge(av_mm, u)
                    if not known(u) or u >= 2:
                        act.wait_ge(ssum_mm, u - 1)
                    act.activation(agg2[:, :], bank[5], ACT.Square).then_inc(agg2_set, 1)
                if nxt:
                    act.wait_ge(kqv_mm, u + 2)
                    if not known(u) or u >= 0:
                        act.wait_ge(red_set, u + 1)
                    act.activation(sq[:, :, :].rearrange("p t c -> p (t c)"), psum[:, 0:1024], ACT.Square).then_inc(sq_set, 1)
                if cur:
                    act.wait_ge(trl_mm, u + 1)
                    if not known(u) or u >= 2:
                        act.wait_ge(sim_mm, 4 * (u - 1))
                    act.activation(qlT[p][:, :], bank[7].bitcast(F16)[:, 0:S], ACT.Copy).then_inc(trl_out, 1)
                if nxt:
                    act.wait_ge(gate_mm, u + 2)
                    if not known(u) or u >= 0:
                        act.wait_ge(silu_set, u + 1)
                    act.activation(sig[:, :], bank[2], ACT.Sigmoid).then_inc(gsig_set, 1)
                if cur:
                    act.wait_ge(bias_set, u + 1)
                for j in range(TB):
                    if cur:
                        n = TB * u + j
                        act.wait_ge(sim_mm, n + 1)
                        if not known(n) or n >= 2:
                            act.wait_ge(attn_set, n - 1)
                        act.activation(relu[:, j % 2], bank[3 + j % 2], ACT.Relu, bias=bias[:, b:b + 1]).then_inc(relu_set, 1)
                    if prv and j == 2:
                        act.wait_ge(norm_set, u)
                        act.activation(norm[:, 1, :], norm[:, 0, :], ACT.Tanh).then_inc(tanh_set, 1)
                    if nxt and j == 2:
                        act.wait_ge(silu_set, u + 2)
                        if not known(u) or u >= 1:
                            act.wait_ge(gated_set, u)
                        act.activation(gate[1 - p][:, :], silu[:, :], ACT.Tanh).then_inc(gate_set, 1)
                if split:
                    head_high(h + 1)
                if nxt:
                    act.wait_ge(qk_set, u + 2)
                    if not known(u) or u >= 0:
                        act.wait_ge(trl_mm, u + 1)
                    act.activation(qk16[:, :, 0:4:2, :], qk[:, :, :, :], ACT.Copy).then_inc(q_hi, 1)
                    act.wait_ge(tr_mm, u + 2)
                    if not known(u) or u >= 1:
                        act.wait_ge(sim_mm, 4 * u)
                    act.activation(kqT[1 - p][:, :, :].rearrange("p a t -> p (a t)"), bank[7].bitcast(F16), ACT.Copy).then_inc(tr_out, 1)

            def head_high(h):
                act.wait_ge(wb_in, 16 * (h + 1))
                if not known(h) or h >= 1:
                    act.wait_ge(gate_mm, B * h)
                act.activation(big_hi[:, 0:KD * HW], wb_raw[:, :, :].rearrange("p k c -> p (k c)"),
                               ACT.Copy).then_inc(wb_hi, 1)

            act.wait_ge(ls_in, 16)
            act.preload_act_table(ACT.Exp)
            act.activation(head[:, 0, :], ls_sb[:, 0, :], ACT.Exp).then_inc(ls_exp, 1)
            act.activation(head[:, 3, :], ls_sb[:, 1, :], ACT.Exp).then_inc(ls_exp, 1)
            act.preload_act_table(ACT.Sigmoid)
            with act.Fori(0, B) as b:
                ln_high(2 * B + b, b)
            act.wait_ge(r_set, 3)
            act.wait_ge(dn_mm, NF * B)
            head_high(0)
            att_act(-1, 3, True, False, False, False)
            for b in range(B):
                att_act(0, b, True, True, b > 0, b == 2)
            with act.Fori(1, H - 1) as h:
                for b in range(B):
                    att_act(h, b, True, True, True, b == 2)
            for b in range(B):
                att_act(H - 1, b, b < 3, True, True, False)
            att_act(H, 0, False, False, True, False)
            ffn_act_all(B, 3 * B)

        @block.vector
        def _(dve):
            dve.memset(m3[:, :], 0.0).then_inc(m3_zero, 1)

            def ln_stat(u, b):
                for t in range(TB):
                    dve.bn_stats(stats[:, t, :], xres[:, at(b * TB + t, 1), :].rearrange("p o c -> p (o c)")).then_inc(ln_stats, 1)
                dve.wait_ge(ln_stats, TB * (u + 1))
                if not known(u):
                    dve.memset(hold[:, :], 0.0)
                for t in range(TB):
                    dve.bn_aggr(mv[:, t, :], stats[:, t, :]).then_inc(ln_mv, 1)

            def ln_norm(u, b):
                dve.wait_ge(ln_rstd, u + 1)
                dve.scalar_tensor_tensor(lnw[:, 2, :], mv[:, :, 0], -1.0, lnw[:, 1, :], ALU.mult, ALU.mult).then_inc(ln_nmr, 1)
                dve.wait_ge(ln_nmr, u + 1)
                if not known(u) or u >= 1:
                    dve.wait_ge(ln_tp, 2 * u)
                for t in range(TB):
                    dve.tensor_scalar(xn[:, t, :], xres[:, at(b * TB + t, 1), :].rearrange("p o c -> p (o c)"),
                                      lnw[:, 1, t:t + 1], lnw[:, 2, t:t + 1], ALU.mult, ALU.add).then_inc(ln_xn, 1)

            def ln_low(u, b):
                for k in range(KD):
                    dve.wait_ge(ln_hi, 2 * u + k + 1)
                    dve.tensor_tensor(xT_lo[:, k, at(b * S, S)], bank[6 + k],
                                      xT_hi[:, k, at(b * S, S)].bitcast(F32), ALU.subtract).then_inc(ln_lo, 1)

            def ln_all(u):
                ln_stat(u, 0)
                with dve.Fori(0, B - 1) as b:
                    ln_norm(u + b, b)
                    ln_stat(u + b + 1, b + 1)
                    ln_low(u + b, b)
                ln_norm(u + B - 1, B - 1)
                ln_low(u + B - 1, B - 1)

            dve.wait_ge(x_in, B * 16)
            ln_stat(0, 0)
            for b in range(B):
                ln_norm(b, b)
                if b < B - 1:
                    ln_stat(b + 1, b + 1)
                ln_low(b, b)
            dve.wait_ge(wa_hi, 1)
            dve.tensor_tensor(big_lo[:, :], wqk_raw, big_hi[:, :].bitcast(F32), ALU.subtract).then_inc(wa_lo, 1)
            dve.wait_ge(wa_hi, 2)
            dve.tensor_tensor(wv_lo[:, :, :].rearrange("p k c -> p (k c)"), wv_raw,
                              wv_hi[:, :, :].rearrange("p k c -> p (k c)").bitcast(F32), ALU.subtract).then_inc(wa_lo, 1)

            dve.wait_ge(as_tot, 1)
            dve.tensor_scalar(thr[:, 0, :], bank[1][:, 0:3], 1.0 / (FF * DM), Q_EPS, ALU.mult, ALU.add).then_inc(thr_set, 1)
            dve.wait_ge(thr_set, 1)
            dve.tensor_scalar(thr[:, 1, :], thr[:, 0, :], 0.5, None, ALU.mult).then_inc(thr_set, 1)
            dve.tensor_scalar(thr[:, 2, :], thr[:, 0, :], -0.5, None, ALU.mult).then_inc(thr_set, 1)
            dve.wait_ge(thr_set, 3)
            for w in range(3):
                q = w12q[:, w] if w < 2 else w3q[:, :, :]
                raw = w12_raw[:, w] if w < 2 else w3_raw
                low = below.rearrange("p (k f) -> p k f", k=KD) if w < 2 else below.rearrange("p (f c) -> p f c", c=DM)
                dve.tensor_scalar(low, raw, thr[:, 2, w:w + 1], None, ALU.is_lt).then_inc(below_set, 1)
                dve.wait_ge(below_set, w + 1)
                dve.scalar_tensor_tensor(q, raw, thr[:, 1, w:w + 1], low, ALU.is_gt, ALU.subtract).then_inc(wq_set, 1)
                dve.wait_ge(wq_set, w + 1)

            dve.wait_ge(const_in, 32)
            with dve.Fori(0, B) as b:
                for s in range(2):
                    n = 2 * b + s
                    dve.wait_ge(pj_mm, 3 * n + 2)
                    dve.tensor_tensor(rot[:, s, 1], bank[3 + 3 * s][:, :], trig[:, 0], ALU.mult).then_inc(pj_t, 1)
                    dve.wait_ge(pj_mm, 3 * n + 3)
                    dve.tensor_tensor(OTs[:, :], bank[4 + 3 * s][:, :], trig[:, 1], ALU.mult).then_inc(pj_t, 1)
                    dve.wait_ge(pj_t, 2 * n + 2)
                    dve.tensor_tensor(rot[:, s, 1], rot[:, s, 1], OTs[:, :], ALU.add).then_inc(pj_rot, 1)
                    dve.wait_ge(pj_p1, n + 1)
                    dve.tensor_tensor(rot[:, s], rot[:, s], parts[:, s, 0], ALU.subtract).then_inc(pj_r1, 1)
                    dve.wait_ge(pj_p2, n + 1)
                    dve.tensor_tensor(parts[:, s, 2], rot[:, s], parts[:, s, 1], ALU.subtract).then_inc(pj_p3, 1)

            def row_max(k, g):
                for j, its in enumerate(P1_BANKS):
                    n = 12 * k + 3 * g + j
                    dve.wait_ge(p1_mm, n + 1)
                    if g == 0 and j == 0 and (not known(k) or k >= 1):
                        dve.wait_ge(m_split, 4 * k)
                    c = 0
                    for it in its:
                        last = dve.reduce_max(mx[:, 4 * g + it:4 * g + it + 1],
                                              bank[(3 * g + j) % 2][:, c:c + (it + 1) * P], AX.X)
                        c += (it + 1) * P
                    last.then_inc(p1_red, 1)

            def split_max(k):
                dve.wait_ge(p1_red, 12 * k + 12)
                if not known(k) or k >= 1:
                    dve.wait_ge(m_tr, k)
                dve.tensor_scalar(m3[:, 0:16], mx[:, :], -1.0, None, ALU.mult).then_inc(m_split, 1)
                dve.wait_ge(m_split, 4 * k + 1)
                dve.scalar_tensor_tensor(mxr[:, :], mx[:, :], -1.0, m3[:, 0:16], ALU.mult, ALU.subtract).then_inc(m_split, 1)
                dve.wait_ge(m_split, 4 * k + 2)
                dve.tensor_copy(m3[:, 16:32], mxr[:, :]).then_inc(m_split, 1)
                dve.wait_ge(m_split, 4 * k + 3)
                dve.tensor_tensor(m3[:, 32:48], mxr[:, :], m3[:, 16:32], ALU.subtract).then_inc(m_split, 1)

            def normalise(k, r):
                q = slice(r * S // 2, (r + 1) * S // 2)
                if r == 0:
                    dve.wait_ge(den_mm, k + 1)
                dve.reciprocal(rden[:, q], bank[6][:, q]).then_inc(den_inv, 1)
                dve.wait_ge(den_inv, 2 * k + r + 1)
                if not known(k) or k >= 1:
                    dve.wait_ge(oa_mm, 2 * k - 1 + r)
                dve.tensor_tensor(aoT[:, q], OTs[:, q], rden[:, q], ALU.mult).then_inc(ao_set, 1)

            def add_out(k, r):
                dve.wait_ge(oa_mm, 2 * k + r + 1)
                if not known(k) or 2 * k + r >= 1:
                    dve.wait_ge(x_a, 2 * k + r)
                rows = xres[:, at((k // 4) * TB + 2 * r, 2), :]
                dve.tensor_tensor(rows, bank[7][:, :].rearrange("p (t c) -> p t c", t=2), rows, ALU.add).then_inc(x_a, 1)

            def dve_group(k, p1=True, tail=True):
                if p1:
                    row_max(k + 2, 0)
                if tail:
                    normalise(k - 2, 0)
                if p1:
                    row_max(k + 2, 1)
                if tail:
                    normalise(k - 2, 1)
                if p1:
                    row_max(k + 2, 2)
                if tail:
                    add_out(k - 2, 0)
                if p1:
                    row_max(k + 2, 3)
                    split_max(k + 2)
                if tail:
                    add_out(k - 2, 1)

            dve_group(-2, tail=False)
            dve_group(-1, tail=False)
            dve_group(0, tail=False)
            dve_group(1, tail=False)
            dve_group(2)
            with dve.Fori(3, NG - 2) as k:
                dve_group(k)
            dve_group(NG - 2, p1=False)
            dve_group(NG - 1, p1=False)
            dve_group(NG, p1=False)
            dve_group(NG + 1, p1=False)

            def ffn_low(f, n):
                dve.wait_ge(hi_set, n + 1)
                dve.tensor_tensor(big_lo[:, (f % 3) * S:(f % 3 + 1) * S], hid[:, f % 2],
                                  big_hi[:, (f % 3) * S:(f % 3 + 1) * S].bitcast(F32), ALU.subtract).then_inc(lo_set, 1)

            def ffn_add(v, b):
                dve.wait_ge(dn_mm, NF * (v + 1))
                for r in range(2):
                    rows = xres[:, at(b * TB + 2 * r, 2), :]
                    dve.tensor_tensor(rows, bank[4 + r].rearrange("p (t c) -> p t c", t=2), rows, ALU.add).then_inc(x_f, 1)

            def ffn_dve(v, u, b, ln, add):
                if ln:
                    ln_stat(u + 1, b + 1)
                for f in range(NF):
                    n = NF * v + f
                    dve.wait_ge(sig_set, n + 1)
                    dve.wait_ge(up_mm, 2 * n + 2)
                    if not known(n) or n >= 2:
                        dve.wait_ge(lo_set, n - 1)
                    dve.tensor_tensor(hid[:, f % 2], bank[2 + f % 2][:, :], fsig[:, f % 2], ALU.mult).then_inc(hid_set, 1)
                    if f == 1 and add:
                        ffn_add(v - 1, b - 1)
                    if f:
                        ffn_low(f - 1, n - 1)
                    if ln and f == 3:
                        ln_norm(u + 1, b + 1)
                    if ln and f == 5:
                        ln_low(u + 1, b + 1)
                ffn_low(NF - 1, NF * v + NF - 1)

            def ffn_dve_all(first, u):
                ln_stat(u, 0)
                ln_norm(u, 0)
                ln_low(u, 0)
                ffn_dve(first, u, 0, True, False)
                with dve.Fori(1, B - 1) as b:
                    ffn_dve(first + b, u + b, b, True, True)
                ffn_dve(first + B - 1, u + B - 1, B - 1, False, True)
                ffn_add(first + B - 1, B - 1)

            dve.wait_ge(x_a, 2 * NG)
            ffn_dve_all(0, B)

            def head_low(h):
                dve.wait_ge(wb_hi, h + 1)
                dve.tensor_tensor(big_lo[:, 0:KD * HW], wb_raw[:, :, :].rearrange("p k c -> p (k c)"),
                                  big_hi[:, 0:KD * HW].bitcast(F32), ALU.subtract).then_inc(wb_lo, 1)

            proj = psum[:, 0:1024].rearrange("p (t c) -> p t c", t=TB)

            def att_dve(h, b, nxt, cur, prv, split):
                u, p = B * h + b, b % 2
                i = u + 1
                if cur:
                    dve.tensor_copy(bias[:, b:b + 1], head[:, 2, at(h, 1)]).then_inc(bias_set, 1)
                first_n, first_c = (known(u) and u < 0), (known(u) and u < 1)
                if prv:
                    dve.wait_ge(agg2_set, u)
                    dve.wait_ge(gate_set, u)
                    if not known(u) or u >= 2:
                        dve.wait_ge(ob_mm, 2 * (u - 1))
                    dve.tensor_tensor(gated[:, :], bank[5], gate[1 - p][:, :], ALU.mult).then_inc(gated_set, 1)
                if nxt:
                    dve.wait_ge(sq_set, u + 2)
                if i is not None and not (known(i) and i < 1):
                    dve.wait_ge(rs_set, i)
                if nxt:
                    dve.tensor_reduce(ss[:, 0:8].rearrange("p (t a) -> p t a", t=TB),
                                      sq[:, :, 0:2 * DK].rearrange("p t (a d) -> p t a d", a=2), AX.X, ALU.add).then_inc(red_set0, 1)
                    dve.tensor_reduce(ss[:, 8:12], sq[:, :, 2 * DK:], AX.X, ALU.add).then_inc(red_set, 1)
                if prv:
                    dve.wait_ge(ssum_mm, u)
                    last = dve.tensor_scalar(ss[:, 12:16], bank[6][:, 0:4], NORM_EPS ** 2, None, ALU.max)
                    last.then_inc(ssum_out, 1)
                if nxt:
                    dve.wait_ge(red_set, u + 2)
                    dve.tensor_scalar(ss[:, 0:12], ss[:, 0:12], NORM_EPS ** 2, None, ALU.max).then_inc(ss_set, 1)
                else:
                    dve.wait_ge(ssum_out, u)
                    dve.tensor_scalar(ss[:, 0:12], ss[:, 0:12], NORM_EPS ** 2, None, ALU.max).then_inc(ss_set, 1)
                if nxt:
                    dve.wait_ge(gsig_set, u + 2)
                    if not first_n:
                        dve.wait_ge(gate_set, u + 1)
                    dve.tensor_tensor(silu[:, :], bank[2], sig[:, :], ALU.mult).then_inc(silu_set, 1)
                for j in range(TB):
                    if cur:
                        n = TB * u + j
                        dve.wait_ge(relu_set, n + 1)
                        if j == 0 and not first_c:
                            dve.wait_ge(av_mm, u)
                        dve.tensor_tensor(attn[:, j], relu[:, j % 2], relu[:, j % 2], ALU.mult).then_inc(attn_set, 1)
                    if j == 1:
                        if prv:
                            dve.wait_ge(rs_set, i + 1)
                            dve.tensor_tensor(norm[:, 0, :], ss[:, 12:16], rs[:, 12:16], ALU.mult).then_inc(norm_set, 1)
                        if nxt:
                            hn = h + (b + 1) // 4
                            dve.wait_ge(rs_set, i + 1)
                            inv_q = rs[:, 0:8].rearrange("p (t a) -> p t a", t=TB)[:, :, 1]
                            dve.tensor_scalar(inv_q, inv_q, head[:, 1, at(hn, 1)], None, ALU.mult).then_inc(rq_set, 1)
                            dve.wait_ge(rq_set, u + 2)
                            dve.tensor_tensor(qk[:, :, :, :], proj[:, :, 0:2 * DK].rearrange("p t (a d) -> p t a d", a=2),
                                              rs[:, 0:8].rearrange("p (t a o) -> p t a o", t=TB, o=1).broadcast_to([P, TB, 2, DK]),
                                              ALU.mult).then_inc(qk_set, 1)
                            if not (known(u) and u < 1):
                                dve.wait_ge(av_mm, u)
                            dve.tensor_tensor(vn[1 - p][:, :, :], proj[:, :, 2 * DK:],
                                              rs[:, 8:12].rearrange("p (t o) -> p t o", o=1).broadcast_to([P, TB, DV]),
                                              ALU.mult).then_inc(vn_set, 1)
                    if prv and j >= 2:
                        r = j - 2
                        hp = h - (1 if b == 0 else 0)
                        if r == 0:
                            dve.wait_ge(tanh_set, u)
                            dve.scalar_tensor_tensor(norm[:, 2, :], norm[:, 1, :], head[:, 3, at(hp, 1)], rs[:, 12:16],
                                                     ALU.mult, ALU.mult).then_inc(factor_set, 1)
                            dve.wait_ge(factor_set, u)
                        dve.wait_ge(ob_mm, 2 * (u - 1) + r + 1)
                        for t in range(2):
                            row = xres[:, ((b - 1) % B) * TB + 2 * r + t, :]
                            last = dve.scalar_tensor_tensor(row, bank[6][:, t * DM:(t + 1) * DM], norm[:, 2, 2 * r + t:2 * r + t + 1], row,
                                                            ALU.mult, ALU.add)
                        last.then_inc(x_b, 1)
                if nxt:
                    dve.wait_ge(q_hi, u + 2)
                    dve.tensor_tensor(qk16[:, :, 1:5:3, :], qk[:, :, :, :], qk16[:, :, 0:4:2, :], ALU.subtract).then_inc(q_lo, 1)
                    dve.wait_ge(q_lo, u + 2)
                    dve.tensor_copy(qk16[:, :, 3:6:2, :], qk16[:, :, 2:5:2, :]).then_inc(q_dup, 1)
                if split:
                    head_low(h + 1)

            dve.memset(ss[:, :], 1.0).then_inc(ss_one, 1)
            dve.wait_ge(ss_one, 1)
            dve.wait_ge(x_f, 2 * B)
            ln_all(2 * B)
            dve.wait_ge(ls_exp, 2)
            dve.tensor_scalar(head[:, 0, :], head[:, 0, :], 1.0, None, ALU.add).then_inc(r_set, 1)
            dve.wait_ge(r_set, 1)
            dve.reciprocal(head[:, 1, :], head[:, 0, :]).then_inc(r_set, 1)
            dve.wait_ge(r_set, 2)
            dve.tensor_scalar(head[:, 2, :], head[:, 1, :], -1.0, 1.0, ALU.mult, ALU.add).then_inc(r_set, 1)
            dve.wait_ge(r_set, 3)
            head_low(0)
            att_dve(-1, 3, True, False, False, False)
            for b in range(B):
                att_dve(0, b, True, True, b > 0, b == 2)
            with dve.Fori(1, H - 1) as h:
                for b in range(B):
                    att_dve(h, b, True, True, True, b == 2)
            for b in range(B):
                att_dve(H - 1, b, b < 3, True, True, False)
            att_dve(H, 0, False, False, True, False)
            dve.wait_ge(x_b, 2 * B * H)
            ffn_dve_all(B, 3 * B)

        @block.tensor
        def _(pe):
            def ln_transpose(u):
                for k in range(KD):
                    pe.wait_ge(ln_xn, TB * (u + 1))
                    if not known(u) or u >= 1:
                        pe.wait_ge(ln_lo, 2 * u - 1 + k)
                    for t in range(TB):
                        last = pe.transpose(bank[6 + k][:, t * P:(t + 1) * P], xn[:, t, k * P:(k + 1) * P], ident)
                    last.then_inc(ln_tp, 1)

            pe.wait_ge(const_in, 32)
            for u in range(B):
                ln_transpose(u)
            pe.wait_ge(as_done, 3)
            pe.wait_ge(ln_lo, B * KD)
            pe.matmul(bank[1][:, 0:3], ones, asum[:, :], start=True, stop=True).then_inc(as_tot, 1)

            pe.wait_ge(wa_lo, 1)
            def project_qk(b):
                for s in range(2):
                    if not known(b) or b >= 1:
                        pe.wait_ge(pj_rot, 2 * b)
                        pe.wait_ge(pj_sem, 2 * b)
                    for m in range(3):
                        c = (3 * s + m) * P
                        for i, (w, xt) in enumerate(((big_hi, xT_hi), (big_hi, xT_lo), (big_lo, xT_hi))):
                            for k in range(KD):
                                last = pe.matmul(bank[2 + 3 * s + m][:, :], w[:, k * 768 + c:k * 768 + c + P],
                                                 xt[:, k, at(b * S, S)], start=(i == 0 and k == 0), stop=(i == 2 and k == KD - 1))
                        last.then_inc(pj_mm, 1)

            project_qk(0)
            with pe.Fori(1, B) as b:
                project_qk(b)
            pe.wait_ge(wa_lo, 2)
            pe.wait_ge(thr_set, 1)
            for t in range(NT):
                if t >= 2:
                    pe.wait_ge(v_out, t - 1)
                for i, (xt, w) in enumerate(((xT_hi, wv_hi), (xT_hi, wv_lo), (xT_lo, wv_hi))):
                    for k in range(KD):
                        last = pe.matmul(bank[t % 2][:, 0:DM], xt[:, k, t * P:(t + 1) * P], w[:, k, :],
                                         start=(i == 0 and k == 0), stop=(i == 2 and k == KD - 1))
                last.then_inc(v_mm, 1)

            pe.wait_ge(bf_const, 2)
            pe.wait_ge(ks_ones, 1)
            pe.wait_ge(m3_zero, 1)

            def scores1(k, g):
                if g == 0:
                    pe.wait_ge(stack_in, (k + 1) * 12 * 16)
                r = at(k % 4, 1)
                for j, its in enumerate(P1_BANKS):
                    n = 12 * k + 3 * g + j
                    if not known(k) or n >= 2:
                        pe.wait_ge(p1_red, n - 1)
                    to, c = bank[(3 * g + j) % 2], 0
                    for it in its:
                        pe.matmul(to[:, c:c + (it + 1) * P], qs[0:KROWS, r, g, it * P:(it + 1) * P].rearrange("p o c -> p (o c)"),
                                  ks[0:KROWS, r, g, 0:(it + 1) * P].rearrange("p o c -> p (o c)"), start=True, stop=False,
                                  skip_group_check=True)
                        last = pe.matmul(to[:, c + it * P:c + (it + 1) * P], ident_b[:, :], mask_b[:, :], start=False, stop=True,
                                         skip_group_check=True)
                        c += (it + 1) * P
                    last.then_inc(p1_mm, 1)

            def scores2(k, g):
                if g == 0:
                    pe.wait_ge(m_in, (k + 1) * 16)
                r = at(k % 4, 1)
                for j, jts in enumerate(P2_BANKS):
                    n = 12 * k + 3 * g + j
                    if not known(k) or n >= 3:
                        pe.wait_ge(p2_exp, n - 2)
                    to, c = bank[2 + j], 0
                    for jt in jts:
                        w = S - jt * P
                        pe.matmul(to[:, c:c + w], ks[0:KROWS + MROWS, r, g, jt * P:(jt + 1) * P].rearrange("p o c -> p (o c)"),
                                  qs[0:KROWS + MROWS, r, g, jt * P:S].rearrange("p o c -> p (o c)"), start=True, stop=False,
                                  skip_group_check=True)
                        last = pe.matmul(to[:, c:c + P], mask_b[:, :], ident_b[:, :], start=False, stop=True,
                                         skip_group_check=True)
                        c += w
                    last.then_inc(p2_mm, 1)

            def values(k, i, jt, heads):
                if jt == 0 and heads[0] == 0:
                    pe.wait_ge(p2_exp, 12 * k + 12)
                    pe.wait_ge(vg_set, k + 1)
                    if not known(k) or k >= 1:
                        pe.wait_ge(ot_copied, k)
                for g in heads:
                    w = S - jt * P
                    last = pe.matmul(bank[5][2 * DH * g:2 * DH * (g + 1), jt * P:S], vg[i][:, jt, g, :],
                                     PT[:, i, g, P2_AT[jt]:P2_AT[jt] + w], start=(jt == 0), stop=(jt == TB - 1),
                                     skip_group_check=True)
                if jt == TB - 1 and heads[-1] == 3:
                    last.then_inc(pv_mm, 1)

            def denominators(k):
                pe.wait_ge(ot_copied, k + 1)
                pe.wait_ge(m_copied, min(k + 4, NG) if known(k) else k + 4)
                pe.matmul(bank[6][:, :], sel, OTs[:, :], start=True, stop=True).then_inc(den_mm, 1)

            def transpose_max(k):
                if not known(k) or k >= 1:
                    pe.wait_ge(m_copied, k)
                pe.wait_ge(m_split, 4 * k + 4)
                if not known(k) or k >= 4:
                    pe.wait_ge(den_inv, 2 * (k - 3))
                pe.transpose(bank[6].bitcast(BF16)[:, 0:P], m3[:, :], ident_b[:, :]).then_inc(m_tr, 1)

            def project_out(k, r):
                pe.wait_ge(ao_set, 2 * k + r + 1)
                if not known(k) or 2 * k + r >= 1:
                    pe.wait_ge(x_a, 2 * k + r)
                for t in range(2):
                    last = pe.matmul(bank[7][:, t * DM:(t + 1) * DM], aoT[:, (2 * r + t) * P:(2 * r + t + 1) * P],
                                     woa[:, at(k % 4, 1), :].rearrange("p o c -> p (o c)"), start=True, stop=True)
                last.then_inc(oa_mm, 1)

            def pe_group(k, i, p1=True, p2=True, pv=True, tail=True):
                for step in range(8):
                    g = step // 2
                    if p1 and step % 2 == 0:
                        scores1(k + 2, g)
                    if tail and step == 0:
                        denominators(k - 2)
                    if p2 and step % 2 == 1:
                        scores2(k, g)
                    if pv:
                        values(k - 1, 1 - i, step // 2, (0, 1) if step % 2 == 0 else (2, 3))
                    if tail and step in (4, 6):
                        project_out(k - 2, step // 2 - 2)
                if p1:
                    transpose_max(k + 2)

            pe.wait_ge(v_out, NT)
            pe.wait_ge(pj_rot, 2 * B)
            pe.wait_ge(woa_in, 16)
            pe_group(-2, 0, p2=False, pv=False, tail=False)
            pe_group(-1, 1, p2=False, pv=False, tail=False)
            pe_group(0, 0, pv=False, tail=False)
            pe_group(1, 1, tail=False)
            pe_group(2, 0)
            pe_group(3, 1)
            with pe.Fori(2, NG // 2 - 1) as i:
                pe_group(2 * i, 0)
                pe_group(2 * i + 1, 1)
            pe_group(NG - 2, 0, p1=False)
            pe_group(NG - 1, 1, p1=False)
            pe_group(NG, 0, p1=False, p2=False)
            pe_group(NG + 1, 1, p1=False, p2=False, pv=False)

            def ffn_up(f, n, b):
                if not known(n) or n >= 2:
                    pe.wait_ge(hid_set, n - 1)
                for w in range(2):
                    for i, xt in enumerate((xT_hi, xT_lo)):
                        for k in range(KD):
                            last = pe.matmul(bank[2 * w + f % 2][:, :], w12q[:, w, k, f * P:(f + 1) * P], xt[:, k, at(b * S, S)],
                                             start=(i == 0 and k == 0), stop=(i == 1 and k == KD - 1))
                    last.then_inc(up_mm, 1)

            def ffn_down(f, n, v):
                pe.wait_ge(lo_set, n + 1)
                if f == 0 and (not known(v) or v >= 1):
                    pe.wait_ge(x_f, 2 * v)
                for t in range(TB):
                    for i, part in enumerate((big_hi, big_lo)):
                        last = pe.matmul(bank[4 + t // 2][:, (t % 2) * DM:(t % 2 + 1) * DM],
                                         part[:, (f % 3) * S + t * P:(f % 3) * S + (t + 1) * P], w3q[:, f, :],
                                         start=(f == 0 and t % 2 == 0 and i == 0), stop=(f == NF - 1 and i == 1), skip_group_check=True)
                last.then_inc(dn_mm, 1)

            def ffn_pe(v, u, b, ln):
                pe.wait_ge(ln_lo, 2 * (u + 1))
                for f in range(NF):
                    ffn_up(f, NF * v + f, b)
                    if f:
                        ffn_down(f - 1, NF * v + f - 1, v)
                    if ln and f == 4:
                        ln_transpose(u + 1)
                ffn_down(NF - 1, NF * v + NF - 1, v)

            def ffn_pe_all(first, u):
                ln_transpose(u)
                ffn_pe(first, u, 0, True)
                with pe.Fori(1, B - 1) as b:
                    ffn_pe(first + b, u + b, b, True)
                ffn_pe(first + B - 1, u + B - 1, B - 1, False)

            ffn_pe_all(0, B)

            def att_pe(h, b, nxt, cur, prv):
                u, p = B * h + b, b % 2
                bn = (b + 1) % B
                first_n = known(u) and u < 0
                if nxt:
                    if bn == 0:
                        pe.wait_ge(wb_lo, h + 2)
                    if not first_n:
                        pe.wait_ge(vn_set, u + 1)
                    for t in range(TB):
                        tok = slice(bn * S + t * P, bn * S + (t + 1) * P)
                        for i, (xt, w) in enumerate(((xT_hi, big_hi), (xT_hi, big_lo), (xT_lo, big_hi))):
                            for k in range(KD):
                                last = pe.matmul(psum[:, t * 2 * DV:(t + 1) * 2 * DV], xt[:, k, tok], w[:, k * HW:k * HW + 2 * DV],
                                                 start=(i == 0 and k == 0), stop=(i == 2 and k == KD - 1))
                    last.then_inc(kqv_mm, 1)
                if cur:
                    pe.wait_ge(tr_out, u + 1)
                    for t in range(TB):
                        last = pe.transpose(bank[7].bitcast(F16)[:, t * P:(t + 1) * P],
                                            qk16[:, t, 4:6, :].rearrange("p a d -> p (a d)"), ident_h[:, :])
                    last.then_inc(trl_mm, 1)
                if nxt:
                    if not first_n:
                        pe.wait_ge(silu_set, u + 1)
                    for i, (w, xt) in enumerate(((big_hi, xT_hi), (big_lo, xT_hi), (big_hi, xT_lo))):
                        for k in range(KD):
                            last = pe.matmul(bank[2], w[:, k * HW + 2 * DV:(k + 1) * HW], xt[:, k, bn * S:(bn + 1) * S],
                                             start=(i == 0 and k == 0), stop=(i == 2 and k == KD - 1))
                    last.then_inc(gate_mm, 1)
                if prv:
                    pe.wait_ge(agg2_set, u)
                    if not known(u) or u >= 2:
                        pe.wait_ge(x_b, 2 * (u - 1))
                    for t in range(TB):
                        last = pe.matmul(bank[6][:, t:t + 1], agg2[:, t * P:(t + 1) * P], ones[:, 0:1], start=True, stop=True)
                    last.then_inc(ssum_mm, 1)

                def similarities(j):
                    n = TB * u + j
                    if j == 0:
                        pe.wait_ge(trl_out, u + 1)
                    if not known(n) or n >= 2:
                        pe.wait_ge(relu_set, n - 1)
                    k_t = kqT[p][:, 0, j * P:(j + 1) * P]
                    pe.matmul(bank[3 + j % 2], k_t, kqT[p][:, 1, :], start=True, stop=False)
                    pe.matmul(bank[3 + j % 2], k_t, qlT[p][:, :], start=False, stop=True).then_inc(sim_mm, 1)

                def aggregate(j):
                    pe.wait_ge(attn_set, TB * u + j + 1)
                    if j == 0:
                        pe.wait_ge(vn_set, u + 1)
                        if not known(u) or u >= 1:
                            pe.wait_ge(gated_set, u)
                    last = pe.matmul(bank[5], vn[p][:, j, :], attn[:, j], start=(j == 0), stop=(j == TB - 1))
                    if j == TB - 1:
                        last.then_inc(av_mm, 1)

                def project(r):
                    hp = h - (1 if b == 0 else 0)
                    pe.wait_ge(gated_set, u)
                    if r == 0:
                        pe.wait_ge(ssum_out, u)
                    else:
                        pe.wait_ge(x_b, 2 * (u - 1) + 1)
                    for t in range(2):
                        last = pe.matmul(bank[6][:, t * DM:(t + 1) * DM], gated[:, (2 * r + t) * P:(2 * r + t + 1) * P],
                                         wob[:, at(hp, 1), :].rearrange("p o c -> p (o c)"), start=True, stop=True)
                    last.then_inc(ob_mm, 1)

                if cur:
                    similarities(0)
                    similarities(1)
                    aggregate(0)
                    similarities(2)
                if prv:
                    project(0)
                if cur:
                    aggregate(1)
                    similarities(3)
                    aggregate(2)
                if prv:
                    project(1)
                if cur:
                    aggregate(3)
                if nxt:
                    pe.wait_ge(q_dup, u + 2)
                    if not first_n:
                        pe.wait_ge(trl_out, u + 1)
                    for a in range(2):
                        for t in range(TB):
                            last = pe.transpose(bank[7].bitcast(F16)[:, (a * TB + t) * P:(a * TB + t + 1) * P],
                                                qk16[:, t, 2 * a:2 * a + 2, :].rearrange("p a d -> p (a d)"), ident_h[:, :])
                    last.then_inc(tr_mm, 1)

            with pe.Fori(0, B) as b:
                ln_transpose(2 * B + b)
            pe.wait_ge(ln_lo, 2 * 3 * B)
            pe.wait_ge(bf_const, 3)
            pe.wait_ge(wob_in, 16)
            att_pe(-1, 3, True, False, False)
            for b in range(B):
                att_pe(0, b, True, True, b > 0)
            with pe.Fori(1, H - 1) as h:
                for b in range(B):
                    att_pe(h, b, True, True, True)
            for b in range(B):
                att_pe(H - 1, b, b < 3, True, True)
            att_pe(H, 0, False, False, True)
            ffn_pe_all(B, 3 * B)


def laid_out(inputs):
    import numpy as np

    a = {k: np.asarray(v) for k, v in inputs.items()}
    half = DH // 2
    dim_major = np.array([h * half + d for d in range(half) for h in range(H)])
    swapped = np.array([h * half + (d + half // 2) % half for d in range(half) for h in range(H)])
    wqk = np.concatenate([a["L0_attn_a_Wq_sem"].T[:, dim_major], a["L0_attn_a_Wq_geo"].T[:, dim_major],
                          a["L0_attn_a_Wq_geo"].T[:, swapped], a["L0_attn_a_Wk_sem"].T[:, dim_major],
                          a["L0_attn_a_Wk_geo"].T[:, dim_major], a["L0_attn_a_Wk_geo"].T[:, swapped]], axis=1)
    wo = a["L0_attn_a_Wo"].T.reshape(4, 4, DH, DM)
    wo_a = np.zeros((4, 4, 2 * DH, DM), np.float32)
    wo_a[:, :, :DH] = wo
    wo_a = wo_a.reshape(4, P, DM).transpose(1, 0, 2)
    qg = a["L0_attn_b_Wqg"].reshape(DM, H, DK + DV)
    kv = a["L0_attn_b_Wkv"].reshape(DM, H, DK + DV)
    wb = np.concatenate([kv[:, :, :DK], qg[:, :, :DK], kv[:, :, DK:], qg[:, :, DK:]], axis=2)
    ls = np.broadcast_to(np.stack([a["L0_attn_b_ls_iaw"], a["L0_attn_b_ls_hws"]])[None], (P, 2, H))

    d = np.arange(P) // H
    inv_freq = (np.float32(1.0) / np.float32(10000.0) ** (np.arange(0, half, 2, dtype=np.float32) / np.float32(half))).astype(np.float32)
    angle = (np.arange(S, dtype=np.float32)[None, :] * inv_freq[d % (half // 2)][:, None]).astype(np.float32)
    sign = np.where(d < half // 2, -1.0, 1.0)[:, None]
    i = np.arange(P)
    sel = ((i[:, None] % 32 == DH) & (i[:, None] // 32 == i[None, :] // 32))
    consts = np.concatenate([np.eye(P), np.where(i[None, :] > i[:, None], MASKED, 0.0), sel, np.ones((P, P)),
                             np.cos(angle), np.sin(angle) * sign], axis=1)
    w12 = np.zeros((2, DM, FP), np.float32)
    w12[:, :, :FF] = a["L0_ffn_w1"].T, a["L0_ffn_w2"].T
    w3 = np.zeros((FP, DM), np.float32)
    w3[:FF] = a["L0_ffn_w3"].T
    arrays = {
        "x": a["L0_attn_a_x"].reshape(TOK, DM), "consts": consts.astype(np.float32), "wqk": wqk,
        "wv": a["L0_attn_a_Wv"].T, "wo_a": wo_a, "w12": w12,
        "w3": w3, "wb": wb, "wo_b": a["L0_attn_b_Wo"], "ls": ls,
    }
    return {k: np.ascontiguousarray(v) for k, v in arrays.items()}


def kernel(**inputs):
    import concourse.bacc as bacc
    from concourse.bass_utils import run_bass_kernel_spmd

    arrays = laid_out(inputs)
    nc = bacc.Bacc("TRN2", target_bir_lowering=False, num_devices=1)
    args = {k: nc.dram_tensor("in_" + k, v.shape, mybir.dt.from_np(v.dtype), kind="ExternalInput").ap() for k, v in arrays.items()}
    out = nc.dram_tensor("out_x", (TOK, DM), F32, kind="ExternalOutput").ap()
    program(nc, out=out, **args)
    r = run_bass_kernel_spmd(nc, [{"in_" + k: v for k, v in arrays.items()}], core_ids=[0])
    return r.results[0]["out_x"].reshape(B, S, DM)
```

```python
from contextlib import ExitStack

import concourse.bass as bass
from concourse import mybir

F32 = mybir.dt.float32
F32R = mybir.dt.float32r
BF16 = mybir.dt.bfloat16
F16 = mybir.dt.float16
ALU = mybir.AluOpType
ACT = mybir.ActivationFunctionType
AX = mybir.AxisListType

P = 128
B, S, DM = 4, 512, 256
TOK = B * S
NT = TOK // P
TB = S // P
KD = DM // P
H = 16
DH = 16
NG = B * H // 4
SLOTS = 6
KROWS = SLOTS * DH
MROWS = 3
DK, DV = 64, 128
HW = 2 * DK + 2 * DV
FF = 704
NF = -(-FF // P)
FP = NF * P
LN_EPS, Q_EPS, NORM_EPS = 1e-5, 1e-8, 1e-12
MASKED = -1e30


def at(start, n):
    return slice(start, start + n) if isinstance(start, int) else bass.ds(start, n)


def known(v):
    return isinstance(v, int)


def stage(k, behind):
    return not known(k) or 0 <= k - behind < NG


def program(nc, x, consts, wqk, wv, wo_a, w12, w3, wb, wo_b, ls, out):
    scratch = nc.dram_tensor("qk_parts", (2, 3, 2 * P, TOK), BF16, kind="Internal").ap()
    mscratch = nc.dram_tensor("max_parts", (2, MROWS, 4 * S), BF16, kind="Internal").ap()
    dscratch = nc.dram_tensor("denominators", (2, 2, 4, S), F32, kind="Internal").ap()
    ctx = ExitStack()
    with ctx:
        def sb(name, shape, dt=F32):
            return ctx.enter_context(nc.sbuf_tensor(name, shape, dt))

        def sem(name):
            return ctx.enter_context(nc.semaphore(name))

        xres = sb("xres", [P, NT, DM])
        xT_hi = sb("xT_hi", [P, KD, TOK], F32R)
        xT_lo = sb("xT_lo", [P, KD, TOK], F32R)
        big_hi = sb("big_hi", [P, 1536], F32R)
        big_lo = sb("big_lo", [P, 1536], F32R)
        wv_hi = sb("wv_hi", [P, KD, DM], F32R)
        wv_lo = sb("wv_lo", [P, KD, DM], F32R)
        w12q = sb("w12q", [P, 2, KD, FP], F32R)
        w3q = sb("w3q", [P, NF, DM], F32R)
        woa = sb("woa", [P, 4, DM])
        cst = sb("cst", [P, 5, P])
        ident, mask32, sel, ones = (cst[:, i, :] for i in range(4))
        ident_b = sb("ident_b", [P, P], BF16)
        mask_b = sb("mask_b", [P, P], BF16)
        stats = sb("stats", [P, TB, 6])
        mv = sb("mv", [P, TB, 2])
        lnw = sb("lnw", [P, 3, TB])
        neghalf = sb("neghalf", [P, 16])
        eps = sb("eps", [P, TB])
        hold = sb("hold", [P, 1])
        xn = sb("xn", [P, TB, DM])
        ident_h = sb("ident_h", [P, P], F16)
        region = ExitStack()

        def sa(name, shape, dt=F32):
            return region.enter_context(nc.sbuf_tensor(name, shape, dt))

        U1 = sa("U1", [P, 11264])
        wqk_raw = U1[:, 4096:5632]
        wv_raw = U1[:, 5632:6144]
        rot = U1[:, 6144:8192].rearrange("p (b y t) -> p b y t", b=2, y=2)
        parts = U1[:, 8192:11264].bitcast(BF16).rearrange("p (b a y t) -> p b a y t", b=2, a=3, y=2)
        PT = U1[:, 0:10240].rearrange("p (b g c) -> p b g c", b=2, g=4)
        U2 = sa("U2", [P, 8192])
        qs = U2[:, 0:4096].bitcast(BF16).rearrange("p (r g t) -> p r g t", r=4, g=4)
        ks = U2[:, 4096:8192].bitcast(BF16).rearrange("p (r g t) -> p r g t", r=4, g=4)
        w12_raw = U2[:, 0:2 * KD * FP].rearrange("p (w k f) -> p w k f", w=2, k=KD)
        w3_raw = U2[:, 3072:3072 + NF * DM].rearrange("p (f c) -> p f c", f=NF)
        raw = (w12_raw[:, 0], w12_raw[:, 1], w3_raw)
        below = [U2[:, 4608 + i * KD * FP:4608 + (i + 1) * KD * FP] for i in range(2)]
        junk = [below[1].rearrange("p (k f) -> p k f", k=raw[w].shape[1]) for w in range(3)]
        below = [below[w % 2].rearrange("p (k f) -> p k f", k=raw[w].shape[1]) for w in range(3)]
        trig = sa("trig", [P, 2, S])
        v_all = sa("v_all", [P, NG, TB, 4 * DH])
        vg = [sa(f"vg{i}", [P, TB, 4, 2 * DH]) for i in range(2)]
        OTs = sa("OTs", [P, 2, S])
        den = sa("den", [P, 4 * S // P])
        rden = sa("rden", [P, 4 * S // P])
        aoT = sa("aoT", [P, S])
        mx = sa("mx", [P, 16])
        mxr = sa("mxr", [P, 16])
        m3 = sa("m3", [P, P], BF16)
        mT = sa("mT", [MROWS * 16, P], BF16)
        asum = sa("asum", [P, 3])
        total = sa("total", [P, 3])
        thr = sa("thr", [P, 3, 3])
        region.close()
        wob = sb("wob", [P, H, DM])
        wb_raw = sb("wb_raw", [P, KD, HW])
        ls_sb = sb("ls_sb", [P, 2, H])
        bias = sb("bias", [P, TB])
        head = sb("head", [P, 4, H])
        sq = sb("sq", [P, TB, 2 * DV])
        ss = sb("ss", [P, 3 * TB])
        rs = sb("rs", [P, 3 * TB])
        sa2 = sb("sa2", [P, TB])
        ra = sb("ra", [P, TB])
        qk = sb("qk", [P, TB, 2, DK])
        qk16 = sb("qk16", [P, TB, 6, DK], F16)
        kqT = [sb(f"kqT{i}", [P, 2, S], F16) for i in range(2)]
        qlT = [sb(f"qlT{i}", [P, S], F16) for i in range(2)]
        vn = [sb(f"vn{i}", [P, TB, DV]) for i in range(2)]
        relu = sb("relu", [P, 2, S])
        attn = sb("attn", [P, TB, S])
        sig = sb("sig", [P, S])
        silu = sb("silu", [P, S])
        gate = [sb(f"gate{i}", [P, S]) for i in range(2)]
        agg2 = sb("agg2", [P, S])
        gated = sb("gated", [P, S])
        norm = sb("norm", [P, 3, TB])
        fsig = sb("fsig", [P, 2, S])
        hid = sb("hid", [P, 2, S])
        psum = ctx.enter_context(nc.psum_tensor("psum", [P, 8 * 512], F32))
        bank = [psum[:, i * 512:(i + 1) * 512] for i in range(8)]

        x_in, const_in, wqk_in, wv_in, woa_in, ffn_in = (sem(n) for n in (
            "x_in", "const_in", "wqk_in", "wv_in", "woa_in", "ffn_in"))
        half_set, bf_const, wa_hi, wa_lo = (sem(n) for n in ("half_set", "bf_const", "wa_hi", "wa_lo"))
        as_done, as_tot, tot_out, thr_set, below_set, wq_set = (sem(n) for n in (
            "as_done", "as_tot", "tot_out", "thr_set", "below_set", "wq_set"))
        ln_stats, ln_mv, ln_eps, ln_rstd, ln_nmr, ln_xn, ln_tp, ln_hi, ln_lo = (sem(n) for n in (
            "ln_stats", "ln_mv", "ln_eps", "ln_rstd", "ln_nmr", "ln_xn", "ln_tp", "ln_hi", "ln_lo"))
        pj_mm, pj_sem, pj_t, pj_rot, pj_p1, pj_r1, pj_p2, pj_p3, v_mm, v_out = (sem(n) for n in (
            "pj_mm", "pj_sem", "pj_t", "pj_rot", "pj_p1", "pj_r1", "pj_p2", "pj_p3", "v_mm", "v_out"))
        pj_out = [sem(f"pj_out{i}") for i in range(2)]
        ks_ones, vg_pad, vg_set, stack_in = (sem(n) for n in ("ks_ones", "vg_pad", "vg_set", "stack_in"))
        p1_mm, p1_red, m_split, m_tr, m_copied, m_out, m_in = (sem(n) for n in (
            "p1_mm", "p1_red", "m_split", "m_tr", "m_copied", "m_out", "m_in"))
        p2_mm, p2_exp, pv_mm, ot_copied, den_out, den_in, den_inv, inv_out, inv_in, inv_mm, ao_set, oa_mm, x_a = (sem(n) for n in (
            "p2_mm", "p2_exp", "pv_mm", "ot_copied", "den_out", "den_in", "den_inv", "inv_out", "inv_in", "inv_mm", "ao_set", "oa_mm", "x_a"))
        y_out = sem("y_out")
        m3_zero = sem("m3_zero")
        up_mm, sig_set, hid_set, hi_set, lo_set, dn_mm, x_f = (sem(n) for n in (
            "up_mm", "sig_set", "hid_set", "hi_set", "lo_set", "dn_mm", "x_f"))
        wob_in, wb_in, ls_in, ra_set, ls_exp, r_set, wb_hi, wb_lo = (sem(n) for n in (
            "wob_in", "wb_in", "ls_in", "ra_set", "ls_exp", "r_set", "wb_hi", "wb_lo"))
        kqv_mm, sq_set, red_set, ss_set, rs_set, rq_set, qk_set, vn_set, q_hi, q_lo, q_dup = (sem(n) for n in (
            "kqv_mm", "sq_set", "red_set", "ss_set", "rs_set", "rq_set", "qk_set", "vn_set", "q_hi", "q_lo", "q_dup"))
        tr_mm, tr_out, trl_mm, trl_out, gate_mm, gsig_set, silu_set, gate_set = (sem(n) for n in (
            "tr_mm", "tr_out", "trl_mm", "trl_out", "gate_mm", "gsig_set", "silu_set", "gate_set"))
        sim_mm, relu_set, attn_set, av_mm, agg2_set, gated_set, ssum_mm, ssum_out = (sem(n) for n in (
            "sim_mm", "relu_set", "attn_set", "av_mm", "agg2_set", "gated_set", "ssum_mm", "ssum_out"))
        red_set0, bias_set = sem("kq_red_set"), sem("bias_set")
        norm_set, tanh_set, factor_set, ob_mm, x_b = (sem(n) for n in (
            "norm_set", "tanh_set", "factor_set", "ob_mm", "x_b"))

        block = ctx.enter_context(nc.Block())

        P1_BANKS = [(0, (3,)), (1, (0, 2)), (6, (1,))]
        P2_BANKS = [(2, (0,)), (3, (1, 3)), (4, (2,))]
        V_BANKS = [2, 3]
        P2_AT = [0, 512, 1024, 896]

        @block.sync
        def _(sp):
            for b in range(B):
                sp.dma_start(xres[:, b * TB:(b + 1) * TB, :],
                             x[b * S:(b + 1) * S, :].rearrange("(t p) c -> p t c", p=P)).then_inc(x_in, 16)
            sp.dma_start(cst[:, 0:4, :], consts[:, 0:4 * P].rearrange("p (i c) -> p i c", i=4)).then_inc(const_in, 16)
            sp.dma_start(trig[:, :, :], consts[:, 4 * P:4 * P + 2 * S].rearrange("p (i c) -> p i c", i=2)).then_inc(const_in, 16)
            sp.dma_start(wqk_raw.rearrange("p (k c) -> p k c", k=KD),
                         wqk.rearrange("(k p) c -> p k c", p=P)).then_inc(wqk_in, 16)
            sp.dma_start(wv_raw.rearrange("p (k c) -> p k c", k=KD),
                         wv.rearrange("(k p) c -> p k c", p=P)).then_inc(wv_in, 16)
            for w in range(2):
                sp.dma_start(w12_raw[:, w], w12[w].rearrange("(k p) f -> p k f", p=P)).then_inc(ffn_in, 16)
            sp.dma_start(w3_raw, w3.rearrange("(f p) c -> p f c", p=P)).then_inc(ffn_in, 16)
            sp.dma_start(woa[:, :, :], wo_a).then_inc(woa_in, 16)
            def parts_out(b):
                for s in range(2):
                    sp.wait_ge(pj_p3, 2 * b + s + 1)
                    for a in range(3):
                        sp.dma_start(scratch[s, a].rearrange("(y p) t -> p y t", p=P)[:, :, b * S:(b + 1) * S],
                                     parts[:, s, a]).then_inc(pj_out[s], 16)

            def parts_written(b):
                for s in range(2):
                    sp.wait_ge(pj_out[s], (b + 1) * 3 * 16)

            def load_stack(k):
                slot_at, head_at, token_at, read, loaded = (
                    v if known(k) else sp.snap(v) for v in (k % 4, (k % 4) * 4, (k // 4) * S, 12 * (k - 3), k * 12 * 16))
                if not known(k) or k >= 4:
                    sp.wait_ge(p2_mm, read)
                if not known(k) or k >= 1:
                    sp.wait_ge(stack_in, loaded)
                for s, dst, which in ((0, qs, (0, 0, 1, 0, 2, 1)), (1, ks, (0, 1, 0, 2, 0, 1))):
                    for slot, a in enumerate(which):
                        src = scratch[s, a].rearrange("(r h) t -> r h t", h=H)
                        sp.dma_start(dst[slot * DH:(slot + 1) * DH, at(slot_at, 1), :, :].rearrange("p r g t -> p (r g) t"),
                                     src[:, at(head_at, 4), at(token_at, S)]).then_inc(stack_in, 16)

            def move_max(k):
                half_at, slot_at, copied, written, read = (
                    v if known(k) else sp.snap(v) for v in (k % 2, k % 4, k + 1, (k + 1) * MROWS * 16, k * 16))
                sp.wait_ge(m_copied, copied)
                for a in range(MROWS):
                    if a == 1 and (not known(k) or k >= 1):
                        sp.wait_ge(m_in, read)
                    sp.dma_start(mscratch[at(half_at, 1), a, :].rearrange("o (r c) -> (o r) c", c=P),
                                 mT[a * 16:(a + 1) * 16, :]).then_inc(m_out, 16)
                sp.wait_ge(m_out, written)
                sp.dma_start(qs[KROWS:KROWS + MROWS, at(slot_at, 1), :, :].rearrange("p r g t -> p (r g t)"),
                             mscratch[at(half_at, 1), :, :].rearrange("o a n -> (o a) n")).then_inc(m_in, 16)

            parts_out(0)
            parts_written(0)
            parts_out(1)
            sp.wait_ge(wq_set, 3)
            load_stack(0)
            for b in range(2, B):
                parts_out(b)
                load_stack(b - 1)
            parts_written(B - 1)
            move_max(0)
            load_stack(3)
            with sp.Fori(1, NG - 3) as k:
                move_max(k)
                load_stack(k + 3)
            move_max(NG - 3)
            move_max(NG - 2)
            move_max(NG - 1)

            sp.wait_ge(x_a, 2 * NG)
            sp.dma_start(wob[:, :, :], wo_b.rearrange("(h p) c -> p h c", p=P)).then_inc(wob_in, 16)
            sp.dma_start(ls_sb[:, :, :], ls).then_inc(ls_in, 16)

            def load_head(h):
                if not known(h) or h:
                    sp.wait_ge(wb_lo, h)
                sp.dma_start(wb_raw[:, :, :], wb[:, at(h, 1), :].rearrange("(k p) o c -> p k (o c)", p=P)).then_inc(wb_in, 16)

            load_head(0)
            with sp.Fori(1, H) as h:
                load_head(h)

            sp.wait_ge(x_f, 4 * B)
            for b in range(B):
                sp.dma_start(out[b * S:(b + 1) * S, :].rearrange("(t p) c -> p t c", p=P),
                             xres[:, b * TB:(b + 1) * TB, :]).then_inc(y_out, 16)
            sp.wait_ge(y_out, B * 16)

        @block.gpsimd
        def _(pool):
            pool.memset(neghalf[:, :], -0.5).then_inc(half_set, 1)
            pool.memset(eps[:, :], LN_EPS).then_inc(half_set, 1)
            for i in range(2):
                pool.memset(vg[i][:, :, :, :], 0.0).then_inc(vg_pad, 1)
            pool.wait_ge(vg_pad, 2)
            for i in range(2):
                pool.memset(vg[i][:, :, :, DH:DH + 1], 1.0).then_inc(vg_pad, 1)

            def ln_rstd_of(u):
                pool.wait_ge(ln_mv, TB * (u + 1))
                pool.tensor_tensor(lnw[:, 0, :], mv[:, :, 1], eps[:, :], ALU.add).then_inc(ln_eps, 1)
                pool.wait_ge(ln_eps, u + 1)
                pool.tensor_tensor(lnw[:, 1, :], lnw[:, 0, :], neghalf[:, 0:TB], ALU.pow).then_inc(ln_rstd, 1)

            pool.wait_ge(half_set, 2)
            for u in range(B):
                ln_rstd_of(u)

            pool.wait_ge(tot_out, 1)
            pool.tensor_scalar(thr[:, 0, :], total[:, :], 1.0 / (FF * DM), Q_EPS, ALU.mult, ALU.add).then_inc(thr_set, 1)
            pool.wait_ge(thr_set, 1)
            pool.tensor_scalar(thr[:, 1, :], thr[:, 0, :], 0.5, None, ALU.mult).then_inc(thr_set, 1)
            pool.tensor_scalar(thr[:, 2, :], thr[:, 0, :], -0.5, None, ALU.mult).then_inc(thr_set, 1)
            pool.wait_ge(thr_set, 3)
            for w in range(3):
                if w == 2:
                    pool.wait_ge(wq_set, 1)
                pool.tensor_scalar(below[w], raw[w], thr[:, 2, w:w + 1], None, ALU.is_lt).then_inc(below_set, 1)
            pool.wait_ge(wq_set, 3)
            pool.memset(ks[KROWS:KROWS + MROWS, :, :, :], 1.0).then_inc(ks_ones, 1)
            pool.wait_ge(ks_ones, 1)
            pool.wait_ge(v_out, NT)
            pool.wait_ge(vg_pad, 4)

            def fill_vg(k, i):
                if not known(k) or k >= 2:
                    pool.wait_ge(pv_mm, k - 1)
                pool.tensor_copy(vg[i][:, :, :, 0:DH],
                                 v_all[:, at(k, 1), :, :].rearrange("p o j (g d) -> p (o j) g d", g=4)).then_inc(vg_set, 1)

            fill_vg(0, 0)
            fill_vg(1, 1)
            with pool.Fori(1, NG // 2) as j:
                fill_vg(2 * j, 0)
                fill_vg(2 * j + 1, 1)

            with pool.Fori(B, 3 * B) as u:
                ln_rstd_of(u)
            def inverse_norms(v):
                pool.wait_ge(ss_set, v + 1)
                if not known(v) or v >= 1:
                    pool.wait_ge(vn_set, v)
                pool.tensor_tensor(rs[:, :], ss[:, :], neghalf[:, 0:3 * TB], ALU.pow).then_inc(rs_set, 1)

            def inverse_aggregate(v):
                pool.wait_ge(ssum_out, v + 1)
                if not known(v) or v >= 1:
                    pool.wait_ge(factor_set, v)
                pool.tensor_tensor(ra[:, :], sa2[:, :], neghalf[:, 0:TB], ALU.pow).then_inc(ra_set, 1)

            inverse_norms(0)
            inverse_norms(1)
            inverse_aggregate(0)
            inverse_norms(2)
            with pool.Fori(2, B * H - 1) as u:
                inverse_aggregate(u - 1)
                inverse_norms(u + 1)
            inverse_aggregate(B * H - 2)
            inverse_aggregate(B * H - 1)
            with pool.Fori(3 * B, 4 * B) as u:
                ln_rstd_of(u)

        @block.scalar
        def _(act):
            act.preload_act_table(ACT.Exp)
            act.wait_ge(const_in, 32)
            act.activation(ident_b[:, :], ident, ACT.Copy).then_inc(bf_const, 1)
            act.activation(mask_b[:, :], mask32, ACT.Copy).then_inc(bf_const, 1)
            act.activation(ident_h[:, :], ident, ACT.Copy).then_inc(bf_const, 1)
            act.wait_ge(wqk_in, 16)
            act.activation(big_hi[:, :], wqk_raw, ACT.Copy).then_inc(wa_hi, 1)
            act.wait_ge(wv_in, 16)
            act.activation(wv_hi[:, :, :].rearrange("p k c -> p (k c)"), wv_raw, ACT.Copy).then_inc(wa_hi, 1)

            def ln_high(u, b):
                for k in range(KD):
                    act.wait_ge(ln_tp, 2 * u + k + 1)
                    act.activation(xT_hi[:, k, at(b * S, S)], bank[6 + k], ACT.Copy).then_inc(ln_hi, 1)

            for b in range(B):
                ln_high(b, b)
                if b == 0:
                    act.wait_ge(ffn_in, 3 * 16)
                if b < 3:
                    act.activation(junk[b], raw[b], ACT.Abs, accum_out=asum[:, b:b + 1]).then_inc(as_done, 1)
                    act.wait_ge(as_done, b + 1)

            act.wait_ge(as_tot, 1)
            act.activation(total[:, :], bank[1][:, 0:3], ACT.Copy).then_inc(tot_out, 1)

            def parts_act(b):
                for s in range(2):
                    n = 2 * b + s
                    act.wait_ge(pj_mm, 3 * n + 1)
                    if not known(b) or b >= 1:
                        act.wait_ge(pj_p3, n - 1)
                    act.activation(rot[:, s, 0], bank[2 + 3 * s][:, :], ACT.Copy).then_inc(pj_sem, 1)
                    act.wait_ge(pj_rot, n + 1)
                    act.wait_ge(pj_sem, n + 1)
                    if not known(b) or b >= 1:
                        act.wait_ge(pj_out[s], b * 3 * 16)
                    act.activation(parts[:, s, 0], rot[:, s], ACT.Copy).then_inc(pj_p1, 1)
                    act.wait_ge(pj_r1, n + 1)
                    act.activation(parts[:, s, 1], rot[:, s], ACT.Copy).then_inc(pj_p2, 1)

            parts_act(0)
            with act.Fori(1, B) as b:
                parts_act(b)

            def values_out(first):
                for t in range(first, first + NT // 2):
                    act.wait_ge(v_mm, t + 1)
                    act.activation(v_all[:, t // TB * 4:t // TB * 4 + 4, t % TB, :],
                                   bank[V_BANKS[t % 2]][:, 0:DM].rearrange("p (g c) -> p g c", g=4), ACT.Copy).then_inc(v_out, 1)

            def ot_out(k, i):
                act.wait_ge(pv_mm, k + 1)
                if not known(k) or k >= 2:
                    act.wait_ge(ao_set, k - 1)
                act.activation(OTs[:, i], bank[5][:, :], ACT.Copy).then_inc(ot_copied, 1)

            def exps(k, i, g):
                for j in range(3):
                    act.wait_ge(p2_mm, 12 * k + 3 * g + j + 1)
                    if g == 0 and j == 0 and (not known(k) or k >= 2):
                        act.wait_ge(pv_mm, k - 1)
                    n = (512, 512, 256)[j]
                    act.activation(PT[:, i, g, 512 * j:512 * j + n], bank[2 + j][:, 0:n], ACT.Exp,
                                   scale=float(DH) ** -0.5).then_inc(p2_exp, 1)

            def max_out(k):
                act.wait_ge(m_tr, k + 1)
                if not known(k) or k >= 1:
                    act.wait_ge(m_out, k * MROWS * 16)
                act.activation(mT[:, :], bank[7].bitcast(BF16)[0:MROWS * 16, 0:P], ACT.Copy).then_inc(m_copied, 1)

            def spread(k, i, step):
                rows = OTs[DH:P:2 * DH, i, :]
                if step == 0:
                    act.wait_ge(ot_copied, k + 1)
                    act.dma_start(dscratch[i, 0], rows).then_inc(den_out, 16)
                elif step == 1:
                    act.wait_ge(den_out, 16 * (k + 1))
                    act.dma_start(den[:, :], dscratch[i, 0].rearrange("g (c w) -> (g c) w", c=2 * DH)).then_inc(den_in, 16)
                elif step == 2:
                    act.wait_ge(den_inv, k + 1)
                    act.dma_start(dscratch[i, 1].rearrange("g (c w) -> (g c) w", c=2 * DH), rden[:, :]).then_inc(inv_out, 16)
                else:
                    act.wait_ge(inv_out, 16 * (k + 1))
                    act.dma_start(rows, dscratch[i, 1]).then_inc(inv_in, 16)

            def act_group(k, i):
                if stage(k, 2):
                    ot_out(k - 2, i)
                    spread(k - 2, i, 0)
                if stage(k, -1):
                    max_out(k + 1)
                for g in range(4):
                    if stage(k, 0):
                        exps(k, i, g)
                    if stage(k, 2) and g:
                        spread(k - 2, i, g)

            values_out(0)
            values_out(NT // 2)
            for k in range(-1, 4):
                act_group(k, k % 2)
            with act.Fori(2, NG // 2 - 1) as j:
                act_group(2 * j, 0)
                act_group(2 * j + 1, 1)
            for k in range(NG - 2, NG + 2):
                act_group(k, k % 2)

            def ffn_high(f, n):
                act.wait_ge(hid_set, n + 1)
                if not known(n) or n >= 3:
                    act.wait_ge(dn_mm, n - 2)
                act.activation(big_hi[:, (f % 3) * S:(f % 3 + 1) * S], hid[:, f % 2], ACT.Copy).then_inc(hi_set, 1)

            def ffn_act(v, u, b, ln):
                for f in range(NF):
                    n = NF * v + f
                    act.wait_ge(up_mm, 2 * n + 1)
                    if not known(n) or n >= 2:
                        act.wait_ge(hid_set, n - 1)
                    act.activation(fsig[:, f % 2], bank[f % 2][:, :], ACT.Sigmoid).then_inc(sig_set, 1)
                    if f or not known(b) or b:
                        ffn_high((f - 1) % NF, n - 1)
                    if ln and f == 3:
                        ln_high(u + 1, b + 1)
                if not ln:
                    ffn_high(NF - 1, n)

            def ffn_act_all(first, u):
                act.preload_act_table(ACT.Sigmoid)
                ln_high(u, 0)
                ffn_act(first, u, 0, True)
                with act.Fori(1, B - 1) as b:
                    ffn_act(first + b, u + b, b, True)
                ffn_act(first + B - 1, u + B - 1, B - 1, False)

            ffn_act_all(0, B)

            def att_act(h, b, nxt, cur, prv, split):
                u, p = B * h + b, b % 2

                def scores_relu(j):
                    n = TB * u + j
                    act.wait_ge(sim_mm, n + 1)
                    if not known(n) or n >= 2:
                        act.wait_ge(attn_set, n - 1)
                    act.activation(relu[:, j % 2], bank[3 + j % 2], ACT.Relu, bias=bias[:, b:b + 1]).then_inc(relu_set, 1)

                if prv:
                    act.wait_ge(norm_set, u)
                    act.activation(norm[:, 1, :], norm[:, 0, :], ACT.Tanh).then_inc(tanh_set, 1)
                if nxt:
                    act.wait_ge(kqv_mm, u + 2)
                    if not known(u) or u >= 0:
                        act.wait_ge(red_set, u + 1)
                    act.activation(sq[:, :, :].rearrange("p t c -> p (t c)"), psum[:, 0:1024], ACT.Square).then_inc(sq_set, 1)
                if cur:
                    act.wait_ge(bias_set, u + 1)
                    scores_relu(0)
                    scores_relu(1)
                if nxt:
                    act.wait_ge(gate_mm, u + 2)
                    if not known(u) or u >= 0:
                        act.wait_ge(silu_set, u + 1)
                    act.activation(sig[:, :], bank[2], ACT.Sigmoid).then_inc(gsig_set, 1)
                if split:
                    head_high(h + 1)
                if cur:
                    scores_relu(2)
                if nxt:
                    act.wait_ge(silu_set, u + 2)
                    if not known(u) or u >= 1:
                        act.wait_ge(gated_set, u)
                    act.activation(gate[1 - p][:, :], silu[:, :], ACT.Tanh).then_inc(gate_set, 1)
                if cur:
                    scores_relu(3)
                if nxt:
                    act.wait_ge(qk_set, u + 2)
                    if not known(u) or u >= 0:
                        act.wait_ge(trl_mm, u + 1)
                    act.activation(qk16[:, :, 0:4:2, :], qk[:, :, :, :], ACT.Copy).then_inc(q_hi, 1)
                if cur:
                    act.wait_ge(av_mm, u + 1)
                    if not known(u) or u >= 1:
                        act.wait_ge(ssum_mm, u)
                    act.activation(agg2[:, :], bank[5], ACT.Square).then_inc(agg2_set, 1)
                if nxt:
                    act.wait_ge(tr_mm, u + 2)
                    if not known(u) or u >= 1:
                        act.wait_ge(sim_mm, 4 * u)
                    act.activation(kqT[1 - p][:, :, :].rearrange("p a t -> p (a t)"), bank[7].bitcast(F16), ACT.Copy).then_inc(tr_out, 1)
                    act.wait_ge(trl_mm, u + 2)
                    act.activation(qlT[1 - p][:, :], bank[2].bitcast(F16)[:, 0:S], ACT.Copy).then_inc(trl_out, 1)

            def head_high(h):
                act.wait_ge(wb_in, 16 * (h + 1))
                if not known(h) or h >= 1:
                    act.wait_ge(gate_mm, B * h)
                act.activation(big_hi[:, 0:KD * HW], wb_raw[:, :, :].rearrange("p k c -> p (k c)"),
                               ACT.Copy).then_inc(wb_hi, 1)

            act.wait_ge(ls_in, 16)
            act.preload_act_table(ACT.Exp)
            act.activation(head[:, 0, :], ls_sb[:, 0, :], ACT.Exp).then_inc(ls_exp, 1)
            act.activation(head[:, 3, :], ls_sb[:, 1, :], ACT.Exp).then_inc(ls_exp, 1)
            act.preload_act_table(ACT.Sigmoid)
            with act.Fori(0, B) as b:
                ln_high(2 * B + b, b)
            act.wait_ge(r_set, 3)
            act.wait_ge(dn_mm, NF * B)
            head_high(0)
            att_act(-1, 3, True, False, False, False)
            for b in range(B):
                att_act(0, b, True, True, b > 0, b == 2)
            with act.Fori(1, H - 1) as h:
                for b in range(B):
                    att_act(h, b, True, True, True, b == 2)
            for b in range(B):
                att_act(H - 1, b, b < 3, True, True, False)
            att_act(H, 0, False, False, True, False)
            ffn_act_all(B, 3 * B)

        @block.vector
        def _(dve):
            dve.memset(m3[:, :], 0.0).then_inc(m3_zero, 1)

            def ln_stat(u, b):
                for t in range(TB):
                    dve.bn_stats(stats[:, t, :], xres[:, at(b * TB + t, 1), :].rearrange("p o c -> p (o c)")).then_inc(ln_stats, 1)
                dve.wait_ge(ln_stats, TB * (u + 1))
                if not known(u):
                    dve.memset(hold[:, :], 0.0)
                for t in range(TB):
                    dve.bn_aggr(mv[:, t, :], stats[:, t, :]).then_inc(ln_mv, 1)

            def ln_norm(u, b):
                dve.wait_ge(ln_rstd, u + 1)
                dve.scalar_tensor_tensor(lnw[:, 2, :], mv[:, :, 0], -1.0, lnw[:, 1, :], ALU.mult, ALU.mult).then_inc(ln_nmr, 1)
                dve.wait_ge(ln_nmr, u + 1)
                if not known(u) or u >= 1:
                    dve.wait_ge(ln_tp, 2 * u)
                for t in range(TB):
                    dve.tensor_scalar(xn[:, t, :], xres[:, at(b * TB + t, 1), :].rearrange("p o c -> p (o c)"),
                                      lnw[:, 1, t:t + 1], lnw[:, 2, t:t + 1], ALU.mult, ALU.add).then_inc(ln_xn, 1)

            def ln_low(u, b):
                for k in range(KD):
                    dve.wait_ge(ln_hi, 2 * u + k + 1)
                    dve.tensor_tensor(xT_lo[:, k, at(b * S, S)], bank[6 + k],
                                      xT_hi[:, k, at(b * S, S)].bitcast(F32), ALU.subtract).then_inc(ln_lo, 1)

            def ln_all(u):
                ln_stat(u, 0)
                with dve.Fori(0, B - 1) as b:
                    ln_norm(u + b, b)
                    ln_stat(u + b + 1, b + 1)
                    ln_low(u + b, b)
                ln_norm(u + B - 1, B - 1)
                ln_low(u + B - 1, B - 1)

            def weights_low():
                dve.wait_ge(wa_hi, 1)
                dve.tensor_tensor(big_lo[:, :], wqk_raw, big_hi[:, :].bitcast(F32), ALU.subtract).then_inc(wa_lo, 1)
                dve.wait_ge(wa_hi, 2)
                dve.tensor_tensor(wv_lo[:, :, :].rearrange("p k c -> p (k c)"), wv_raw,
                                  wv_hi[:, :, :].rearrange("p k c -> p (k c)").bitcast(F32), ALU.subtract).then_inc(wa_lo, 1)

            dve.wait_ge(x_in, B * 16)
            ln_stat(0, 0)
            for b in range(B):
                ln_norm(b, b)
                if b < B - 1:
                    ln_stat(b + 1, b + 1)
                if b == 0:
                    weights_low()
                ln_low(b, b)

            dve.wait_ge(const_in, 32)

            def third_part(n, s):
                dve.wait_ge(pj_p2, n + 1)
                dve.tensor_tensor(parts[:, s, 2], rot[:, s], parts[:, s, 1], ALU.subtract).then_inc(pj_p3, 1)

            def rope_and_parts(b):
                for s in range(2):
                    n = 2 * b + s
                    if not known(b) or b >= 1:
                        dve.wait_ge(pj_p3, n - 1)
                    dve.wait_ge(pj_mm, 3 * n + 2)
                    dve.tensor_tensor(rot[:, s, 1], bank[3 + 3 * s][:, :], trig[:, 0], ALU.mult).then_inc(pj_t, 1)
                    dve.wait_ge(pj_mm, 3 * n + 3)
                    dve.tensor_tensor(OTs[:, 0], bank[4 + 3 * s][:, :], trig[:, 1], ALU.mult).then_inc(pj_t, 1)
                    dve.wait_ge(pj_t, 2 * n + 2)
                    dve.tensor_tensor(rot[:, s, 1], rot[:, s, 1], OTs[:, 0], ALU.add).then_inc(pj_rot, 1)
                    if not known(b) or n >= 1:
                        third_part(n - 1, 1 - s)
                    dve.wait_ge(pj_p1, n + 1)
                    dve.tensor_tensor(rot[:, s], rot[:, s], parts[:, s, 0], ALU.subtract).then_inc(pj_r1, 1)

            rope_and_parts(0)
            for w, q in enumerate((w12q[:, 0], w12q[:, 1], w3q[:, :, :])):
                dve.wait_ge(below_set, w + 1)
                dve.scalar_tensor_tensor(q, raw[w], thr[:, 1, w:w + 1], below[w], ALU.is_gt, ALU.subtract).then_inc(wq_set, 1)
            with dve.Fori(1, B) as b:
                rope_and_parts(b)
            third_part(2 * B - 1, 1)

            def row_max(k, g):
                for j, (to, its) in enumerate(P1_BANKS):
                    n = 12 * k + 3 * g + j
                    dve.wait_ge(p1_mm, n + 1)
                    if g == 0 and j == 0 and (not known(k) or k >= 1):
                        dve.wait_ge(m_split, 4 * k)
                    c = 0
                    for it in its:
                        last = dve.reduce_max(mx[:, 4 * g + it:4 * g + it + 1],
                                              bank[to][:, c:c + (it + 1) * P], AX.X)
                        c += (it + 1) * P
                    last.then_inc(p1_red, 1)

            def split_max(k):
                dve.wait_ge(p1_red, 12 * k + 12)
                if not known(k) or k >= 1:
                    dve.wait_ge(m_tr, k)
                dve.tensor_scalar(m3[:, 0:16], mx[:, :], -1.0, None, ALU.mult).then_inc(m_split, 1)
                dve.wait_ge(m_split, 4 * k + 1)
                dve.scalar_tensor_tensor(mxr[:, :], mx[:, :], -1.0, m3[:, 0:16], ALU.mult, ALU.subtract).then_inc(m_split, 1)
                dve.wait_ge(m_split, 4 * k + 2)
                dve.tensor_copy(m3[:, 16:32], mxr[:, :]).then_inc(m_split, 1)
                dve.wait_ge(m_split, 4 * k + 3)
                dve.tensor_tensor(m3[:, 32:48], mxr[:, :], m3[:, 16:32], ALU.subtract).then_inc(m_split, 1)

            def invert(k):
                dve.wait_ge(den_in, 16 * (k + 1))
                if not known(k) or k >= 1:
                    dve.wait_ge(inv_out, 16 * k)
                dve.reciprocal(rden[:, :], den[:, :]).then_inc(den_inv, 1)

            def normalise(k, i):
                dve.wait_ge(inv_mm, k + 1)
                if not known(k) or k >= 1:
                    dve.wait_ge(oa_mm, 2 * k)
                dve.tensor_tensor(aoT[:, :], OTs[:, i], bank[7][:, :], ALU.mult).then_inc(ao_set, 1)

            def add_out(k, r):
                dve.wait_ge(oa_mm, 2 * k + r + 1)
                if not known(k) or 2 * k + r >= 1:
                    dve.wait_ge(x_a, 2 * k + r)
                rows = xres[:, at((k // 4) * TB + 2 * r, 2), :]
                dve.tensor_tensor(rows, bank[7][:, :].rearrange("p (t c) -> p t c", t=2), rows, ALU.add).then_inc(x_a, 1)

            def dve_group(k, i):
                if stage(k, -2):
                    row_max(k + 2, 0)
                    row_max(k + 2, 1)
                if stage(k, 3):
                    normalise(k - 3, 1 - i)
                if stage(k, -2):
                    row_max(k + 2, 2)
                if stage(k, 3):
                    add_out(k - 3, 0)
                if stage(k, 2):
                    invert(k - 2)
                if stage(k, -2):
                    row_max(k + 2, 3)
                    split_max(k + 2)
                if stage(k, 3):
                    add_out(k - 3, 1)

            for k in range(-2, 4):
                dve_group(k, k % 2)
            with dve.Fori(2, NG // 2 - 1) as j:
                dve_group(2 * j, 0)
                dve_group(2 * j + 1, 1)
            for k in range(NG - 2, NG + 3):
                dve_group(k, k % 2)

            def ffn_low(f, n):
                dve.wait_ge(hi_set, n + 1)
                dve.tensor_tensor(big_lo[:, (f % 3) * S:(f % 3 + 1) * S], hid[:, f % 2],
                                  big_hi[:, (f % 3) * S:(f % 3 + 1) * S].bitcast(F32), ALU.subtract).then_inc(lo_set, 1)

            def ffn_add(v, b):
                dve.wait_ge(dn_mm, NF * (v + 1))
                for r in range(2):
                    rows = xres[:, at(b * TB + 2 * r, 2), :]
                    dve.tensor_tensor(rows, bank[4 + r].rearrange("p (t c) -> p t c", t=2), rows, ALU.add).then_inc(x_f, 1)

            def ffn_dve(v, u, b, ln, add):
                if ln:
                    ln_stat(u + 1, b + 1)
                for f in range(NF):
                    n = NF * v + f
                    dve.wait_ge(sig_set, n + 1)
                    dve.wait_ge(up_mm, 2 * n + 2)
                    if not known(n) or n >= 2:
                        dve.wait_ge(lo_set, n - 1)
                    dve.tensor_tensor(hid[:, f % 2], bank[2 + f % 2][:, :], fsig[:, f % 2], ALU.mult).then_inc(hid_set, 1)
                    if f or not known(b) or b:
                        ffn_low((f - 1) % NF, n - 1)
                    if f == 1 and add:
                        ffn_add(v - 1, b - 1)
                    if ln and f == 2:
                        ln_norm(u + 1, b + 1)
                    if ln and f == 4:
                        ln_low(u + 1, b + 1)
                if not ln:
                    ffn_low(NF - 1, n)

            def ffn_dve_all(first, u):
                ln_stat(u, 0)
                ln_norm(u, 0)
                ln_low(u, 0)
                ffn_dve(first, u, 0, True, False)
                with dve.Fori(1, B - 1) as b:
                    ffn_dve(first + b, u + b, b, True, True)
                ffn_dve(first + B - 1, u + B - 1, B - 1, False, True)
                ffn_add(first + B - 1, B - 1)

            dve.wait_ge(x_a, 2 * NG)
            ffn_dve_all(0, B)

            def head_low(h):
                dve.wait_ge(wb_hi, h + 1)
                dve.tensor_tensor(big_lo[:, 0:KD * HW], wb_raw[:, :, :].rearrange("p k c -> p (k c)"),
                                  big_hi[:, 0:KD * HW].bitcast(F32), ALU.subtract).then_inc(wb_lo, 1)

            proj = psum[:, 0:1024].rearrange("p (t c) -> p t c", t=TB)

            def att_dve(h, b, nxt, cur, prv, split):
                u, p = B * h + b, b % 2
                past = lambda n: not known(u) or u >= n

                def square(j):
                    dve.wait_ge(relu_set, TB * u + j + 1)
                    if j == 0 and past(1):
                        dve.wait_ge(av_mm, u)
                    dve.tensor_tensor(attn[:, j], relu[:, j % 2], relu[:, j % 2], ALU.mult).then_inc(attn_set, 1)

                def add_head(r):
                    dve.wait_ge(ob_mm, 2 * (u - 1) + r + 1)
                    for t in range(2):
                        row = xres[:, ((b - 1) % B) * TB + 2 * r + t, :]
                        last = dve.scalar_tensor_tensor(row, bank[6][:, t * DM:(t + 1) * DM], norm[:, 2, 2 * r + t:2 * r + t + 1],
                                                        row, ALU.mult, ALU.add)
                    last.then_inc(x_b, 1)

                if cur:
                    dve.tensor_copy(bias[:, b:b + 1], head[:, 2, at(h, 1)]).then_inc(bias_set, 1)
                if prv:
                    hp = h - (1 if b == 0 else 0)
                    dve.wait_ge(ra_set, u)
                    dve.tensor_tensor(norm[:, 0, :], sa2[:, :], ra[:, :], ALU.mult).then_inc(norm_set, 1)
                    dve.wait_ge(tanh_set, u)
                    dve.scalar_tensor_tensor(norm[:, 2, :], norm[:, 1, :], head[:, 3, at(hp, 1)], ra[:, :],
                                             ALU.mult, ALU.mult).then_inc(factor_set, 1)
                    dve.wait_ge(factor_set, u)
                if nxt:
                    dve.wait_ge(sq_set, u + 2)
                    if past(0):
                        dve.wait_ge(rs_set, u + 1)
                    dve.tensor_reduce(ss[:, 0:8].rearrange("p (t a) -> p t a", t=TB),
                                      sq[:, :, 0:2 * DK].rearrange("p t (a d) -> p t a d", a=2), AX.X, ALU.add).then_inc(red_set0, 1)
                if cur:
                    square(0)
                if nxt:
                    dve.tensor_reduce(ss[:, 8:12], sq[:, :, 2 * DK:], AX.X, ALU.add).then_inc(red_set, 1)
                    dve.wait_ge(red_set, u + 2)
                    dve.tensor_scalar(ss[:, :], ss[:, :], NORM_EPS ** 2, None, ALU.max).then_inc(ss_set, 1)
                if cur:
                    square(1)
                if nxt:
                    dve.wait_ge(gsig_set, u + 2)
                    if past(0):
                        dve.wait_ge(gate_set, u + 1)
                    dve.tensor_tensor(silu[:, :], bank[2], sig[:, :], ALU.mult).then_inc(silu_set, 1)
                if prv:
                    add_head(0)
                if cur:
                    square(2)
                if nxt:
                    hn = h + (b + 1) // 4
                    dve.wait_ge(rs_set, u + 2)
                    inv_q = rs[:, 0:8].rearrange("p (t a) -> p t a", t=TB)[:, :, 1]
                    dve.tensor_scalar(inv_q, inv_q, head[:, 1, at(hn, 1)], None, ALU.mult).then_inc(rq_set, 1)
                    dve.wait_ge(rq_set, u + 2)
                    dve.tensor_tensor(qk[:, :, :, :], proj[:, :, 0:2 * DK].rearrange("p t (a d) -> p t a d", a=2),
                                      rs[:, 0:8].rearrange("p (t a o) -> p t a o", t=TB, o=1).broadcast_to([P, TB, 2, DK]),
                                      ALU.mult).then_inc(qk_set, 1)
                if cur:
                    square(3)
                if nxt:
                    dve.wait_ge(q_hi, u + 2)
                    dve.tensor_tensor(qk16[:, :, 1:5:3, :], qk[:, :, :, :], qk16[:, :, 0:4:2, :], ALU.subtract).then_inc(q_lo, 1)
                    dve.wait_ge(q_lo, u + 2)
                    dve.tensor_copy(qk16[:, :, 3:6:2, :], qk16[:, :, 2:5:2, :]).then_inc(q_dup, 1)
                    dve.tensor_tensor(vn[1 - p][:, :, :], proj[:, :, 2 * DK:],
                                      rs[:, 8:12].rearrange("p (t o) -> p t o", o=1).broadcast_to([P, TB, DV]),
                                      ALU.mult).then_inc(vn_set, 1)
                if split:
                    head_low(h + 1)
                if prv:
                    add_head(1)
                if cur:
                    dve.wait_ge(agg2_set, u + 1)
                    dve.wait_ge(gate_set, u + 1)
                    if past(1):
                        dve.wait_ge(ob_mm, 2 * u)
                    dve.tensor_tensor(gated[:, :], bank[5], gate[p][:, :], ALU.mult).then_inc(gated_set, 1)
                    dve.wait_ge(ssum_mm, u + 1)
                    dve.tensor_scalar(sa2[:, :], bank[3][:, 0:TB], NORM_EPS ** 2, None, ALU.max).then_inc(ssum_out, 1)

            dve.wait_ge(x_f, 2 * B)
            ln_all(2 * B)
            dve.wait_ge(ls_exp, 2)
            dve.tensor_scalar(head[:, 0, :], head[:, 0, :], 1.0, None, ALU.add).then_inc(r_set, 1)
            dve.wait_ge(r_set, 1)
            dve.reciprocal(head[:, 1, :], head[:, 0, :]).then_inc(r_set, 1)
            dve.wait_ge(r_set, 2)
            dve.tensor_scalar(head[:, 2, :], head[:, 1, :], -1.0, 1.0, ALU.mult, ALU.add).then_inc(r_set, 1)
            dve.wait_ge(r_set, 3)
            head_low(0)
            att_dve(-1, 3, True, False, False, False)
            for b in range(B):
                att_dve(0, b, True, True, b > 0, b == 2)
            with dve.Fori(1, H - 1) as h:
                for b in range(B):
                    att_dve(h, b, True, True, True, b == 2)
            for b in range(B):
                att_dve(H - 1, b, b < 3, True, True, False)
            att_dve(H, 0, False, False, True, False)
            dve.wait_ge(x_b, 2 * B * H)
            ffn_dve_all(B, 3 * B)

        @block.tensor
        def _(pe):
            def ln_transpose(u):
                for k in range(KD):
                    pe.wait_ge(ln_xn, TB * (u + 1))
                    if not known(u) or u >= 1:
                        pe.wait_ge(ln_lo, 2 * u - 1 + k)
                    for t in range(TB):
                        last = pe.transpose(bank[6 + k][:, t * P:(t + 1) * P], xn[:, t, k * P:(k + 1) * P], ident)
                    last.then_inc(ln_tp, 1)

            def project_qk(b, s):
                n = 2 * b + s
                if not known(b) or b >= 1:
                    pe.wait_ge(pj_rot, n - 1)
                    pe.wait_ge(pj_sem, n - 1)
                for m in range(3):
                    c = (3 * s + m) * P
                    for i, (w, xt) in enumerate(((big_hi, xT_hi), (big_hi, xT_lo), (big_lo, xT_hi))):
                        for k in range(KD):
                            last = pe.matmul(bank[2 + 3 * s + m][:, :], w[:, k * 768 + c:k * 768 + c + P],
                                             xt[:, k, at(b * S, S)], start=(i == 0 and k == 0), stop=(i == 2 and k == KD - 1))
                    last.then_inc(pj_mm, 1)

            pe.wait_ge(const_in, 32)
            for u in range(B - 1):
                ln_transpose(u)
            pe.wait_ge(wa_lo, 1)
            project_qk(0, 0)
            ln_transpose(B - 1)
            pe.wait_ge(as_done, 3)
            pe.matmul(bank[1][:, 0:3], ones, asum[:, :], start=True, stop=True).then_inc(as_tot, 1)
            pe.wait_ge(ln_lo, B * KD)
            project_qk(0, 1)
            with pe.Fori(1, B) as b:
                project_qk(b, 0)
                project_qk(b, 1)

            def project_v(t):
                if t >= 2:
                    pe.wait_ge(v_out, t - 1)
                for i, (xt, w) in enumerate(((xT_hi, wv_hi), (xT_hi, wv_lo), (xT_lo, wv_hi))):
                    for k in range(KD):
                        last = pe.matmul(bank[V_BANKS[t % 2]][:, 0:DM], xt[:, k, t * P:(t + 1) * P], w[:, k, :],
                                         start=(i == 0 and k == 0), stop=(i == 2 and k == KD - 1))
                last.then_inc(v_mm, 1)

            pe.wait_ge(wa_lo, 2)
            pe.wait_ge(tot_out, 1)
            pe.wait_ge(bf_const, 2)
            pe.wait_ge(ks_ones, 1)
            pe.wait_ge(m3_zero, 1)

            def scores1(k, g):
                if g == 0:
                    pe.wait_ge(stack_in, (k + 1) * 12 * 16)
                r = at(k % 4, 1)
                for j, (to, its) in enumerate(P1_BANKS):
                    n = 12 * k + 3 * g + j
                    if not known(k) or n >= 3:
                        pe.wait_ge(p1_red, n - 2)
                    to, c = bank[to], 0
                    for it in its:
                        pe.matmul(to[:, c:c + (it + 1) * P], qs[0:KROWS, r, g, it * P:(it + 1) * P].rearrange("p o c -> p (o c)"),
                                  ks[0:KROWS, r, g, 0:(it + 1) * P].rearrange("p o c -> p (o c)"), start=True, stop=False,
                                  skip_group_check=True)
                        last = pe.matmul(to[:, c + it * P:c + (it + 1) * P], ident_b[:, :], mask_b[:, :], start=False, stop=True,
                                         skip_group_check=True)
                        c += (it + 1) * P
                    last.then_inc(p1_mm, 1)

            def scores2(k, g):
                if g == 0:
                    pe.wait_ge(m_in, (k + 1) * 16)
                r = at(k % 4, 1)
                for j, (to, jts) in enumerate(P2_BANKS):
                    n = 12 * k + 3 * g + j
                    if not known(k) or n >= 3:
                        pe.wait_ge(p2_exp, n - 2)
                    to, c = bank[to], 0
                    for jt in jts:
                        w = S - jt * P
                        pe.matmul(to[:, c:c + w], ks[0:KROWS + MROWS, r, g, jt * P:(jt + 1) * P].rearrange("p o c -> p (o c)"),
                                  qs[0:KROWS + MROWS, r, g, jt * P:S].rearrange("p o c -> p (o c)"), start=True, stop=False,
                                  skip_group_check=True)
                        last = pe.matmul(to[:, c:c + P], mask_b[:, :], ident_b[:, :], start=False, stop=True,
                                         skip_group_check=True)
                        c += w
                    last.then_inc(p2_mm, 1)

            def values(k, i, jt, heads):
                if jt == 0:
                    pe.wait_ge(p2_exp, 12 * k + 3 * heads[-1] + 3)
                if jt == 0 and heads[0] == 0:
                    pe.wait_ge(vg_set, k + 1)
                    if not known(k) or k >= 1:
                        pe.wait_ge(ot_copied, k)
                for g in heads:
                    w = S - jt * P
                    last = pe.matmul(bank[5][2 * DH * g:2 * DH * (g + 1), jt * P:S], vg[i][:, jt, g, :],
                                     PT[:, i, g, P2_AT[jt]:P2_AT[jt] + w], start=(jt == 0), stop=(jt == TB - 1),
                                     skip_group_check=True)
                if jt == TB - 1 and heads[-1] == 3:
                    last.then_inc(pv_mm, 1)

            def inverses(k, i):
                pe.wait_ge(inv_in, 16 * (k + 1))
                pe.wait_ge(m_copied, min(k + 5, NG) if known(k) else k + 5)
                if not known(k) or k >= 1:
                    pe.wait_ge(x_a, 2 * k)
                pe.matmul(bank[7][:, :], sel, OTs[:, i], start=True, stop=True).then_inc(inv_mm, 1)

            def transpose_max(k):
                pe.wait_ge(m_split, 4 * k + 4)
                if not known(k) or k >= 1:
                    pe.wait_ge(m_copied, k)
                if not known(k) or k >= 5:
                    pe.wait_ge(x_a, 2 * (k - 4))
                pe.transpose(bank[7].bitcast(BF16)[:, 0:P], m3[:, :], ident_b[:, :]).then_inc(m_tr, 1)

            def project_out(k, r):
                pe.wait_ge(ao_set, k + 1)
                if not known(k) or 2 * k + r >= 1:
                    pe.wait_ge(x_a, 2 * k + r)
                for t in range(2):
                    last = pe.matmul(bank[7][:, t * DM:(t + 1) * DM], aoT[:, (2 * r + t) * P:(2 * r + t + 1) * P],
                                     woa[:, at(k % 4, 1), :].rearrange("p o c -> p (o c)"), start=True, stop=True)
                last.then_inc(oa_mm, 1)

            def pe_group(k, i, v=None):
                for step in range(8):
                    if stage(k, -2) and step % 2 == 0:
                        scores1(k + 2, step // 2)
                    if v is not None:
                        project_v(v + step)
                    if stage(k, 0) and step % 2 == 1:
                        scores2(k, step // 2)
                    if stage(k, 1):
                        values(k - 1, 1 - i, step // 2, (0, 1) if step % 2 == 0 else (2, 3))
                    if stage(k, -1) and step == 0:
                        transpose_max(k + 1)
                    if stage(k, 3) and step == 2:
                        inverses(k - 3, 1 - i)
                    if stage(k, 3) and step in (4, 6):
                        project_out(k - 3, step // 2 - 2)

            pe.wait_ge(pj_rot, 2 * B)
            pe.wait_ge(pj_sem, 2 * B)
            pe.wait_ge(woa_in, 16)
            pe_group(-2, 0, v=0)
            pe_group(-1, 1, v=NT // 2)
            pe.wait_ge(v_out, NT)
            for k in range(4):
                pe_group(k, k % 2)
            with pe.Fori(2, NG // 2 - 1) as j:
                pe_group(2 * j, 0)
                pe_group(2 * j + 1, 1)
            for k in range(NG - 2, NG + 3):
                pe_group(k, k % 2)

            def ffn_up(f, n, b):
                if not known(n) or n >= 2:
                    pe.wait_ge(hid_set, n - 1)
                for w in range(2):
                    for i, xt in enumerate((xT_hi, xT_lo)):
                        for k in range(KD):
                            last = pe.matmul(bank[2 * w + f % 2][:, :], w12q[:, w, k, f * P:(f + 1) * P], xt[:, k, at(b * S, S)],
                                             start=(i == 0 and k == 0), stop=(i == 1 and k == KD - 1))
                    last.then_inc(up_mm, 1)

            def ffn_down(f, n, v):
                pe.wait_ge(lo_set, n + 1)
                if f == 0 and (not known(v) or v >= 1):
                    pe.wait_ge(x_f, 2 * v)
                for t in range(TB):
                    for i, part in enumerate((big_hi, big_lo)):
                        last = pe.matmul(bank[4 + t // 2][:, (t % 2) * DM:(t % 2 + 1) * DM],
                                         part[:, (f % 3) * S + t * P:(f % 3) * S + (t + 1) * P], w3q[:, f, :],
                                         start=(f == 0 and t % 2 == 0 and i == 0), stop=(f == NF - 1 and i == 1), skip_group_check=True)
                last.then_inc(dn_mm, 1)

            def ffn_pe(v, u, b, ln):
                pe.wait_ge(ln_lo, 2 * (u + 1))
                for f in range(NF):
                    n = NF * v + f
                    ffn_up(f, n, b)
                    if f >= 2:
                        ffn_down(f - 2, n - 2, v)
                    elif not known(b) or b:
                        ffn_down(f - 2 + NF, n - 2, v - 1)
                    if ln and f == 3:
                        ln_transpose(u + 1)
                if not ln:
                    for f in range(NF - 2, NF):
                        ffn_down(f, NF * v + f, v)

            def ffn_pe_all(first, u):
                ln_transpose(u)
                ffn_pe(first, u, 0, True)
                with pe.Fori(1, B - 1) as b:
                    ffn_pe(first + b, u + b, b, True)
                ffn_pe(first + B - 1, u + B - 1, B - 1, False)

            ffn_pe_all(0, B)

            def att_pe(h, b, nxt, cur, prv):
                u, p = B * h + b, b % 2
                bn = (b + 1) % B
                past = lambda n: not known(u) or u >= n

                def project_kqv():
                    if bn == 0:
                        pe.wait_ge(wb_lo, h + 2)
                    if past(0):
                        pe.wait_ge(vn_set, u + 1)
                    for t in range(TB):
                        tok = slice(bn * S + t * P, bn * S + (t + 1) * P)
                        for i, (xt, w) in enumerate(((xT_hi, big_hi), (xT_hi, big_lo), (xT_lo, big_hi))):
                            for k in range(KD):
                                last = pe.matmul(psum[:, t * 2 * DV:(t + 1) * 2 * DV], xt[:, k, tok], w[:, k * HW:k * HW + 2 * DV],
                                                 start=(i == 0 and k == 0), stop=(i == 2 and k == KD - 1))
                    last.then_inc(kqv_mm, 1)

                def project_gate():
                    if past(0):
                        pe.wait_ge(trl_out, u + 1)
                    for i, (w, xt) in enumerate(((big_hi, xT_hi), (big_lo, xT_hi), (big_hi, xT_lo))):
                        for k in range(KD):
                            last = pe.matmul(bank[2], w[:, k * HW + 2 * DV:(k + 1) * HW], xt[:, k, bn * S:(bn + 1) * S],
                                             start=(i == 0 and k == 0), stop=(i == 2 and k == KD - 1))
                    last.then_inc(gate_mm, 1)

                def transpose_kq():
                    pe.wait_ge(q_dup, u + 2)
                    if past(0):
                        pe.wait_ge(tr_out, u + 1)
                    for a in range(2):
                        for t in range(TB):
                            last = pe.transpose(bank[7].bitcast(F16)[:, (a * TB + t) * P:(a * TB + t + 1) * P],
                                                qk16[:, t, 2 * a:2 * a + 2, :].rearrange("p a d -> p (a d)"), ident_h[:, :])
                    last.then_inc(tr_mm, 1)
                    pe.wait_ge(silu_set, u + 2)
                    for t in range(TB):
                        last = pe.transpose(bank[2].bitcast(F16)[:, t * P:(t + 1) * P],
                                            qk16[:, t, 4:6, :].rearrange("p a d -> p (a d)"), ident_h[:, :])
                    last.then_inc(trl_mm, 1)

                def similarities(j):
                    n = TB * u + j
                    if j == 0:
                        pe.wait_ge(tr_out, u + 1)
                        pe.wait_ge(trl_out, u + 1)
                        if past(1):
                            pe.wait_ge(ssum_out, u)
                    if not known(n) or n >= 2:
                        pe.wait_ge(relu_set, n - 1)
                    k_t = kqT[p][:, 0, j * P:(j + 1) * P]
                    pe.matmul(bank[3 + j % 2], k_t, kqT[p][:, 1, :], start=True, stop=False)
                    pe.matmul(bank[3 + j % 2], k_t, qlT[p][:, :], start=False, stop=True).then_inc(sim_mm, 1)

                def aggregate(j):
                    pe.wait_ge(attn_set, TB * u + j + 1)
                    if j == 0:
                        pe.wait_ge(vn_set, u + 1)
                        if past(1):
                            pe.wait_ge(gated_set, u)
                    last = pe.matmul(bank[5], vn[p][:, j, :], attn[:, j], start=(j == 0), stop=(j == TB - 1))
                    if j == TB - 1:
                        last.then_inc(av_mm, 1)

                def sum_squares():
                    pe.wait_ge(agg2_set, u + 1)
                    pe.wait_ge(relu_set, TB * u + 3)
                    for t in range(TB):
                        last = pe.matmul(bank[3][:, t:t + 1], agg2[:, t * P:(t + 1) * P], ones[:, 0:1], start=True, stop=True)
                    last.then_inc(ssum_mm, 1)

                def project(r):
                    hp = h - (1 if b == 0 else 0)
                    pe.wait_ge(gated_set, u)
                    if r == 1 or past(2):
                        pe.wait_ge(x_b, 2 * (u - 1) + r)
                    for t in range(2):
                        last = pe.matmul(bank[6][:, t * DM:(t + 1) * DM], gated[:, (2 * r + t) * P:(2 * r + t + 1) * P],
                                         wob[:, at(hp, 1), :].rearrange("p o c -> p (o c)"), start=True, stop=True)
                    last.then_inc(ob_mm, 1)

                if nxt:
                    project_kqv()
                if cur:
                    similarities(0)
                    similarities(1)
                if nxt:
                    project_gate()
                if prv:
                    project(0)
                if cur:
                    aggregate(0)
                    similarities(2)
                    aggregate(1)
                    similarities(3)
                if prv:
                    project(1)
                if cur:
                    aggregate(2)
                    aggregate(3)
                if nxt:
                    transpose_kq()
                if cur:
                    sum_squares()

            with pe.Fori(0, B) as b:
                ln_transpose(2 * B + b)
            pe.wait_ge(ln_lo, 2 * 3 * B)
            pe.wait_ge(bf_const, 3)
            pe.wait_ge(wob_in, 16)
            att_pe(-1, 3, True, False, False)
            for b in range(B):
                att_pe(0, b, True, True, b > 0)
            with pe.Fori(1, H - 1) as h:
                for b in range(B):
                    att_pe(h, b, True, True, True)
            for b in range(B):
                att_pe(H - 1, b, b < 3, True, True)
            att_pe(H, 0, False, False, True)
            ffn_pe_all(B, 3 * B)


def laid_out(inputs):
    import numpy as np

    a = {k: np.asarray(v) for k, v in inputs.items()}
    half = DH // 2
    dim_major = np.array([h * half + d for d in range(half) for h in range(H)])
    swapped = np.array([h * half + (d + half // 2) % half for d in range(half) for h in range(H)])
    wqk = np.concatenate([a["L0_attn_a_Wq_sem"].T[:, dim_major], a["L0_attn_a_Wq_geo"].T[:, dim_major],
                          a["L0_attn_a_Wq_geo"].T[:, swapped], a["L0_attn_a_Wk_sem"].T[:, dim_major],
                          a["L0_attn_a_Wk_geo"].T[:, dim_major], a["L0_attn_a_Wk_geo"].T[:, swapped]], axis=1)
    wo = a["L0_attn_a_Wo"].T.reshape(4, 4, DH, DM)
    wo_a = np.zeros((4, 4, 2 * DH, DM), np.float32)
    wo_a[:, :, :DH] = wo
    wo_a = wo_a.reshape(4, P, DM).transpose(1, 0, 2)
    qg = a["L0_attn_b_Wqg"].reshape(DM, H, DK + DV)
    kv = a["L0_attn_b_Wkv"].reshape(DM, H, DK + DV)
    wb = np.concatenate([kv[:, :, :DK], qg[:, :, :DK], kv[:, :, DK:], qg[:, :, DK:]], axis=2)
    ls = np.broadcast_to(np.stack([a["L0_attn_b_ls_iaw"], a["L0_attn_b_ls_hws"]])[None], (P, 2, H))

    d = np.arange(P) // H
    inv_freq = (np.float32(1.0) / np.float32(10000.0) ** (np.arange(0, half, 2, dtype=np.float32) / np.float32(half))).astype(np.float32)
    angle = (np.arange(S, dtype=np.float32)[None, :] * inv_freq[d % (half // 2)][:, None]).astype(np.float32)
    sign = np.where(d < half // 2, -1.0, 1.0)[:, None]
    i = np.arange(P)
    sel = ((i[:, None] % 32 == DH) & (i[:, None] // 32 == i[None, :] // 32))
    consts = np.concatenate([np.eye(P), np.where(i[None, :] > i[:, None], MASKED, 0.0), sel, np.ones((P, P)),
                             np.cos(angle), np.sin(angle) * sign], axis=1)
    w12 = np.zeros((2, DM, FP), np.float32)
    w12[:, :, :FF] = a["L0_ffn_w1"].T, a["L0_ffn_w2"].T
    w3 = np.zeros((FP, DM), np.float32)
    w3[:FF] = a["L0_ffn_w3"].T
    arrays = {
        "x": a["L0_attn_a_x"].reshape(TOK, DM), "consts": consts.astype(np.float32), "wqk": wqk,
        "wv": a["L0_attn_a_Wv"].T, "wo_a": wo_a, "w12": w12,
        "w3": w3, "wb": wb, "wo_b": a["L0_attn_b_Wo"], "ls": ls,
    }
    return {k: np.ascontiguousarray(v) for k, v in arrays.items()}


def kernel(**inputs):
    import concourse.bacc as bacc
    from concourse.bass_utils import run_bass_kernel_spmd

    arrays = laid_out(inputs)
    nc = bacc.Bacc("TRN2", target_bir_lowering=False, num_devices=1)
    args = {k: nc.dram_tensor("in_" + k, v.shape, mybir.dt.from_np(v.dtype), kind="ExternalInput").ap() for k, v in arrays.items()}
    out = nc.dram_tensor("out_x", (TOK, DM), F32, kind="ExternalOutput").ap()
    program(nc, out=out, **args)
    r = run_bass_kernel_spmd(nc, [{"in_" + k: v for k, v in arrays.items()}], core_ids=[0])
    return r.results[0]["out_x"].reshape(B, S, DM)
```

```python
from contextlib import ExitStack

import concourse.bass as bass
from concourse import mybir

F32 = mybir.dt.float32
F32R = mybir.dt.float32r
BF16 = mybir.dt.bfloat16
F16 = mybir.dt.float16
ALU = mybir.AluOpType
ACT = mybir.ActivationFunctionType
AX = mybir.AxisListType

P = 128
B, S, DM = 4, 512, 256
TOK = B * S
NT = TOK // P
TB = S // P
KD = DM // P
H = 16
DH = 16
NG = B * H // 4
SLOTS = 6
KROWS = SLOTS * DH
STACK = ((0, 0, 0, 3), (0, 3, 0, 2), (0, 5, 0, 1), (1, 0, 0, 2), (1, 2, 0, 2), (1, 4, 0, 1), (1, 5, 2, 1))
MROWS = 3
DK, DV = 64, 128
HW = 2 * DK + 2 * DV
FF = 704
NF = -(-FF // P)
FP = NF * P
LN_EPS, Q_EPS, NORM_EPS = 1e-5, 1e-8, 1e-12
MASKED = -1e30


def at(start, n):
    return slice(start, start + n) if isinstance(start, int) else bass.ds(start, n)


def known(v):
    return isinstance(v, int)


def stage(k, behind):
    return not known(k) or 0 <= k - behind < NG


def through_dram(k):
    return not known(k) or k < NG - 2


def at_end(k):
    return known(k) and k >= NG - 3


def ffn_batches(first, u, batch, loop):
    batch(first, 0, u, ln=u + 1)
    if first:
        with loop(1, B - 1) as b:
            batch(first + b, b, u + b, ln=u + b + 1)
        batch(first + B - 1, B - 1, u + B - 1)
    else:
        with loop(1, B - 1) as b:
            batch(b, b, u + b, ln=2 * b + u, last=2 * b + u + 1)
        batch(B - 1, B - 1, u + 2 * B - 4, last=u + 2 * B - 2)


def program(nc, x, consts, wqk, wv, wo_a, w12, w3, wb, wo_b, ls, out):
    scratch = nc.dram_tensor("qk_parts", (2, 3, 2 * P, TOK), BF16, kind="Internal").ap()
    mscratch = nc.dram_tensor("max_parts", (2, MROWS, 4 * S), BF16, kind="Internal").ap()
    dscratch = nc.dram_tensor("denominators", (2, 2, 4, S), F32, kind="Internal").ap()
    ctx = ExitStack()
    with ctx:
        def sb(name, shape, dt=F32):
            return ctx.enter_context(nc.sbuf_tensor(name, shape, dt))

        def sem(name):
            return ctx.enter_context(nc.semaphore(name))

        xres = sb("xres", [P, NT, DM])
        xT_hi = sb("xT_hi", [P, KD, TOK], F32R)
        xT_lo = sb("xT_lo", [P, KD, TOK], F32R)
        big_hi = sb("big_hi", [P, 1536], F32R)
        big_lo = sb("big_lo", [P, 1536], F32R)
        wv_hi = sb("wv_hi", [P, KD, DM], F32R)
        wv_lo = sb("wv_lo", [P, KD, DM], F32R)
        w12q = sb("w12q", [P, 2, KD, FP], F32R)
        w3q = sb("w3q", [P, NF, DM], F32R)
        woa = sb("woa", [P, 4, DM])
        cst = sb("cst", [P, 5, P])
        ident, mask32, sel, ones = (cst[:, i, :] for i in range(4))
        ident_b = sb("ident_b", [P, P], BF16)
        mask_b = sb("mask_b", [P, P], BF16)
        stats = sb("stats", [P, TB, 6])
        mv = sb("mv", [P, TB, 2])
        lnw = sb("lnw", [P, 3, TB])
        neghalf = sb("neghalf", [P, 16])
        eps = sb("eps", [P, TB])
        hold = sb("hold", [P, 1])
        xn = sb("xn", [P, TB, DM])
        ident_h = sb("ident_h", [P, P], F16)
        ls_sb = sb("ls_sb", [P, 2, H])
        head = sb("head", [P, 4, H])
        region = ExitStack()

        def sa(name, shape, dt=F32):
            return region.enter_context(nc.sbuf_tensor(name, shape, dt))

        U1 = sa("U1", [P, 11264])
        wqk_raw = U1[:, 4096:5632]
        wv_raw = U1[:, 5632:6144]
        rot = U1[:, 6144:8192].rearrange("p (b y t) -> p b y t", b=2, y=2)
        parts = U1[:, 8192:11264].bitcast(BF16).rearrange("p (b a y t) -> p b a y t", b=2, a=3, y=2)
        PT = U1[:, 0:10240].rearrange("p (b g c) -> p b g c", b=2, g=4)
        U2 = sa("U2", [P, 8192])
        qs = U2[:, 0:4096].bitcast(BF16).rearrange("p (r g t) -> p r g t", r=4, g=4)
        ks = U2[:, 4096:8192].bitcast(BF16).rearrange("p (r g t) -> p r g t", r=4, g=4)
        w12_raw = U2[:, 0:2 * KD * FP].rearrange("p (w k f) -> p w k f", w=2, k=KD)
        w3_raw = U2[:, 3072:3072 + NF * DM].rearrange("p (f c) -> p f c", f=NF)
        rwide = U2[:, 4096:4096 + S]
        ao_last = U2[:, 6144:6144 + S]
        raw = (w12_raw[:, 0], w12_raw[:, 1], w3_raw)
        below = [region[:, start:start + KD * FP].rearrange("p (k f) -> p k f", k=k)
                 for region, start, k in ((U2, 4608, KD), (U2, 6144, KD), (U1, 0, NF))]
        junk = [U1[:, 1536:1536 + KD * FP].rearrange("p (k f) -> p k f", k=raw[w].shape[1]) for w in range(3)]
        trig = sa("trig", [P, 2, S])
        v_all = sa("v_all", [P, NG, TB, 4 * DH])
        vg = [sa(f"vg{i}", [P, TB, 4, 2 * DH]) for i in range(2)]
        OTs = sa("OTs", [P, 2, S])
        den = sa("den", [P, 4 * S // P])
        rden = sa("rden", [P, 4 * S // P])
        aoT = sa("aoT", [P, S])
        mx = sa("mx", [P, 16])
        mxr = sa("mxr", [P, 16])
        m3 = sa("m3", [P, P], BF16)
        mT = sa("mT", [MROWS * 16, P], BF16)
        asum = sa("asum", [P, 3])
        total = sa("total", [P, 3])
        thr = sa("thr", [P, 3, 3])
        region.close()
        wob = sb("wob", [P, H, DM])
        wb_raw = sb("wb_raw", [P, KD, HW])
        wob_hi = sb("wob_hi", [P, H, DM], F32R)
        wob_lo = sb("wob_lo", [P, H, DM], F32R)
        bias = sb("bias", [P, TB])
        sq = sb("sq", [P, TB, 2 * DV])
        ss = sb("ss", [P, 3 * TB])
        rs = sb("rs", [P, 3 * TB])
        sa2 = sb("sa2", [P, TB])
        ra = sb("ra", [P, TB])
        qk = sb("qk", [P, TB, 2, DK])
        qk16 = sb("qk16", [P, TB, 6, DK], F16)
        kqT = [sb(f"kqT{i}", [P, 2, S], F16) for i in range(2)]
        qlT = [sb(f"qlT{i}", [P, S], F16) for i in range(2)]
        vn = [sb(f"vn{i}", [P, TB, DV]) for i in range(2)]
        relu = sb("relu", [P, 2, S])
        attn = sb("attn", [P, TB, S])
        silu = sb("silu", [P, S])
        gate = [sb(f"gate{i}", [P, S]) for i in range(2)]
        agg2 = sb("agg2", [P, S])
        gated = sb("gated", [P, S])
        gated_hi = sb("gated_hi", [P, S], F32R)
        gated_lo = sb("gated_lo", [P, S], F32R)
        norm = sb("norm", [P, 3, TB])
        fsig = sb("fsig", [P, 2, S])
        hid = sb("hid", [P, 2, S])
        wb_h = sb("wb_h", [P, KD * HW], F32R)
        wb_l = sb("wb_l", [P, KD * HW], F32R)
        psum = ctx.enter_context(nc.psum_tensor("psum", [P, 8 * 512], F32))
        bank = [psum[:, i * 512:(i + 1) * 512] for i in range(8)]

        def ln_banks(u):
            return (0, 1) if known(u) and u == 3 * B else LN_BANKS

        def values_of(k):
            return ao_last if known(k) and k == NG - 1 else aoT[:, :]

        const_in, trig_in, wqk_in, wv_in, woa_in, ffn_in = (sem(n) for n in (
            "const_in", "trig_in", "wqk_in", "wv_in", "woa_in", "ffn_in"))
        x_in = [sem(f"x_in{b}") for b in range(B)]
        half_set, bf_const, wa_hi, wa_lo = (sem(n) for n in ("half_set", "bf_const", "wa_hi", "wa_lo"))
        as_done, as_tot, tot_out, thr_set, below_set, wq_set = (sem(n) for n in (
            "as_done", "as_tot", "tot_out", "thr_set", "below_set", "wq_set"))
        ln_stats, ln_mv, ln_eps, ln_rstd, ln_nmr, ln_xn, ln_tp, ln_hi, ln_lo = (sem(n) for n in (
            "ln_stats", "ln_mv", "ln_eps", "ln_rstd", "ln_nmr", "ln_xn", "ln_tp", "ln_hi", "ln_lo"))
        pj_mm, pj_sem, pj_t, pj_rot, pj_p1, pj_r1, pj_p2, pj_p3, v_mm, v_out = (sem(n) for n in (
            "pj_mm", "pj_sem", "pj_t", "pj_rot", "pj_p1", "pj_r1", "pj_p2", "pj_p3", "v_mm", "v_out"))
        pj_out = [sem(f"pj_out{i}") for i in range(2)]
        ks_ones, vg_pad, vg_set, stack_in = (sem(n) for n in ("ks_ones", "vg_pad", "vg_set", "stack_in"))
        p1_mm, p1_red, m_split, m_tr, m_copied, m_out, m_in = (sem(n) for n in (
            "p1_mm", "p1_red", "m_split", "m_tr", "m_copied", "m_out", "m_in"))
        p2_mm, p2_exp, pv_mm, ot_copied, den_mm, den_out, den_in, den_inv, inv_out, inv_in, inv_mm, rwide_set, ao_set, oa_mm, x_a = (sem(n) for n in (
            "p2_mm", "p2_exp", "pv_mm", "ot_copied", "den_mm", "den_out", "den_in", "den_inv", "inv_out", "inv_in", "inv_mm", "rwide_set", "ao_set", "oa_mm", "x_a"))
        y_out = sem("y_out")
        m3_zero = sem("m3_zero")
        up_mm, sig_set, hid_set, hi_set, lo_set, dn_mm, x_f = (sem(n) for n in (
            "up_mm", "sig_set", "hid_set", "hi_set", "lo_set", "dn_mm", "x_f"))
        wob_in, wob_high, wob_low, wb_in, ls_in, ra_set, ls_exp, r_set, wb_hi, wb_lo = (sem(n) for n in (
            "wob_in", "wob_high", "wob_low", "wb_in", "ls_in", "ra_set", "ls_exp", "r_set", "wb_hi", "wb_lo"))
        kqv_mm, sq_set, red_set, ss_set, rs_set, rq_set, qk_set, vn_set, q_hi, q_lo, q_dup = (sem(n) for n in (
            "kqv_mm", "sq_set", "red_set", "ss_set", "rs_set", "rq_set", "qk_set", "vn_set", "q_hi", "q_lo", "q_dup"))
        tr_mm, tr_out, trl_mm, trl_out, gate_mm, silu_set, gate_set = (sem(n) for n in (
            "tr_mm", "tr_out", "trl_mm", "trl_out", "gate_mm", "silu_set", "gate_set"))
        sim_mm, relu_set, attn_set, av_mm, agg2_set, gated_set, ghi_set, glo_set, ssum_mm, ssum_out = (sem(n) for n in (
            "sim_mm", "relu_set", "attn_set", "av_mm", "agg2_set", "gated_set", "ghi_set", "glo_set", "ssum_mm", "ssum_out"))
        kq_red_set, bias_set = sem("kq_red_set"), sem("bias_set")
        norm_set, tanh_set, factor_set, ob_mm, x_b = (sem(n) for n in (
            "norm_set", "tanh_set", "factor_set", "ob_mm", "x_b"))

        block = ctx.enter_context(nc.Block())

        P1_BANKS = [(0, (3,)), (1, (0, 2)), (6, (1,))]
        P2_BANKS = [(2, (0,)), (3, (1, 3)), (4, (2,))]
        INV_BANK, OUT_BANKS = (7, 3), ((7, 7), (7, 4))
        DEN_BANK = 2
        LN_BANKS = [5, 6]
        DOWN_BANKS = [4, 7]
        V_BANKS = [2, 3]
        P2_AT = [0, 512, 1024, 896]

        @block.sync
        def _(sp):
            def load_x(b):
                sp.dma_start(xres[:, b * TB:(b + 1) * TB, :],
                             x[b * S:(b + 1) * S, :].rearrange("(t p) c -> p t c", p=P)).then_inc(x_in[b], 16)

            load_x(0)
            sp.dma_start(cst[:, 0:4, :], consts[:, 0:4 * P].rearrange("p (i c) -> p i c", i=4)).then_inc(const_in, 16)
            load_x(1)
            sp.dma_start(wqk_raw.rearrange("p (k c) -> p k c", k=KD),
                         wqk.rearrange("(k p) c -> p k c", p=P)).then_inc(wqk_in, 16)
            load_x(2)
            load_x(3)
            sp.dma_start(trig[:, :, :], consts[:, 4 * P:4 * P + 2 * S].rearrange("p (i c) -> p i c", i=2)).then_inc(trig_in, 16)
            sp.dma_start(wv_raw.rearrange("p (k c) -> p k c", k=KD),
                         wv.rearrange("(k p) c -> p k c", p=P)).then_inc(wv_in, 16)
            for w in range(2):
                sp.dma_start(w12_raw[:, w], w12[w].rearrange("(k p) f -> p k f", p=P)).then_inc(ffn_in, 16)
            sp.dma_start(w3_raw, w3.rearrange("(f p) c -> p f c", p=P)).then_inc(ffn_in, 16)
            sp.dma_start(woa[:, :, :], wo_a).then_inc(woa_in, 16)
            sp.dma_start(ls_sb[:, :, :], ls).then_inc(ls_in, 16)
            def parts_out(b):
                for s in range(2):
                    sp.wait_ge(pj_p3, 2 * b + s + 1)
                    sp.dma_start(scratch[s].rearrange("a (y p) t -> p (a y) t", p=P)[:, :, b * S:(b + 1) * S],
                                 parts[:, s].rearrange("p a y t -> p (a y) t")).then_inc(pj_out[s], 16)

            def parts_written(b):
                for s in range(2):
                    sp.wait_ge(pj_out[s], (b + 1) * 16)

            def load_stack(k):
                slot_at, head_at, token_at, read, loaded = (
                    v if known(k) else sp.snap(v) for v in (k % 4, (k % 4) * 4, (k // 4) * S, 12 * (k - 3), k * len(STACK) * 16))
                if not known(k) or k >= 4:
                    sp.wait_ge(p2_mm, read)
                if not known(k) or k >= 1:
                    sp.wait_ge(stack_in, loaded)
                for s, slot, a, n in STACK:
                    rows = scratch[s, a:a + n].rearrange("a (r h) t -> (a r) h t", h=H)
                    sp.dma_start((qs, ks)[s][slot * DH:(slot + n) * DH, at(slot_at, 1), :, :].rearrange("p r g t -> p (r g) t"),
                                 rows[:, at(head_at, 4), at(token_at, S)]).then_inc(stack_in, 16)

            def move_max(k):
                half_at, slot_at, copied, written, read = (
                    v if known(k) else sp.snap(v) for v in (k % 2, k % 4, k + 1, (k + 1) * 2 * 16, k * 16))
                sp.wait_ge(m_copied, copied)
                for a, n in ((0, 1), (1, MROWS - 1)):
                    if a == 1 and (not known(k) or k >= 1):
                        sp.wait_ge(m_in, read)
                    sp.dma_start(mscratch[at(half_at, 1), a:a + n, :].rearrange("o a (r c) -> (o a r) c", c=P),
                                 mT[a * 16:(a + n) * 16, :]).then_inc(m_out, 16)
                sp.wait_ge(m_out, written)
                sp.dma_start(qs[KROWS:KROWS + MROWS, at(slot_at, 1), :, :].rearrange("p r g t -> p (r g t)"),
                             mscratch[at(half_at, 1), :, :].rearrange("o a n -> (o a) n")).then_inc(m_in, 16)

            parts_out(0)
            parts_written(0)
            parts_out(1)
            sp.wait_ge(wq_set, 3)
            load_stack(0)
            parts_out(2)
            parts_out(3)
            load_stack(1)
            load_stack(2)
            parts_written(B - 1)
            move_max(0)
            load_stack(3)
            with sp.Fori(1, NG - 3) as k:
                move_max(k)
                load_stack(k + 3)
            move_max(NG - 3)
            move_max(NG - 2)
            move_max(NG - 1)

            sp.wait_ge(pv_mm, NG)
            sp.dma_start(wob[:, :, :], wo_b.rearrange("(h p) c -> p h c", p=P)).then_inc(wob_in, 16)

            def load_head(h):
                if not known(h) or h:
                    sp.wait_ge(wb_lo, h)
                sp.dma_start(wb_raw[:, :, :], wb[:, at(h, 1), :].rearrange("(k p) o c -> p k (o c)", p=P)).then_inc(wb_in, 16)

            load_head(0)
            with sp.Fori(1, H) as h:
                load_head(h)

            for b in range(B):
                sp.wait_ge(x_f, 2 * (B + b + 1))
                sp.dma_start(out[b * S:(b + 1) * S, :].rearrange("(t p) c -> p t c", p=P),
                             xres[:, b * TB:(b + 1) * TB, :]).then_inc(y_out, 16)
            sp.wait_ge(y_out, B * 16)

        @block.gpsimd
        def _(pool):
            pool.memset(neghalf[:, :], -0.5).then_inc(half_set, 1)
            pool.memset(eps[:, :], LN_EPS).then_inc(half_set, 1)
            for i in range(2):
                pool.memset(vg[i][:, :, :, :], 0.0).then_inc(vg_pad, 1)
            pool.wait_ge(vg_pad, 2)
            for i in range(2):
                pool.memset(vg[i][:, :, :, DH:DH + 1], 1.0).then_inc(vg_pad, 1)

            def ln_rstd_of(u):
                pool.wait_ge(ln_mv, TB * (u + 1))
                pool.tensor_tensor(lnw[:, 0, :], mv[:, :, 1], eps[:, :], ALU.add).then_inc(ln_eps, 1)
                pool.wait_ge(ln_eps, u + 1)
                pool.tensor_tensor(lnw[:, 1, :], lnw[:, 0, :], neghalf[:, 0:TB], ALU.pow).then_inc(ln_rstd, 1)

            pool.wait_ge(half_set, 2)
            for u in range(B):
                ln_rstd_of(u)

            pool.wait_ge(tot_out, 1)
            pool.tensor_scalar(thr[:, 0, :], total[:, :], 1.0 / (FF * DM), Q_EPS, ALU.mult, ALU.add).then_inc(thr_set, 1)
            pool.wait_ge(thr_set, 1)
            pool.tensor_scalar(thr[:, 1, :], thr[:, 0, :], 0.5, None, ALU.mult).then_inc(thr_set, 1)
            pool.tensor_scalar(thr[:, 2, :], thr[:, 0, :], -0.5, None, ALU.mult).then_inc(thr_set, 1)
            pool.wait_ge(thr_set, 3)
            for w in range(3):
                pool.tensor_scalar(below[w], raw[w], thr[:, 2, w:w + 1], None, ALU.is_lt).then_inc(below_set, 1)
            pool.wait_ge(wq_set, 3)
            pool.memset(ks[KROWS:KROWS + MROWS, :, :, :], 1.0).then_inc(ks_ones, 1)
            pool.wait_ge(ks_ones, 1)
            pool.wait_ge(v_out, NT)
            pool.wait_ge(vg_pad, 4)

            def fill_vg(k, i):
                if not known(k) or k >= 2:
                    pool.wait_ge(pv_mm, k - 1)
                pool.tensor_copy(vg[i][:, :, :, 0:DH],
                                 v_all[:, at(k, 1), :, :].rearrange("p o j (g d) -> p (o j) g d", g=4)).then_inc(vg_set, 1)

            fill_vg(0, 0)
            fill_vg(1, 1)
            with pool.Fori(1, NG // 2) as j:
                fill_vg(2 * j, 0)
                fill_vg(2 * j + 1, 1)

            def low_weights(h):
                two = at(h, 2)
                pool.wait_ge(wob_high, 4)
                pool.tensor_tensor(wob_lo[:, two, :], wob[:, two, :], wob_hi[:, two, :].bitcast(F32), ALU.subtract).then_inc(wob_low, 1)

            ln_rstd_of(B)
            with pool.Fori(B + 1, 3 * B - 1) as u:
                ln_rstd_of(u)
                low_weights(2 * (u - B - 1))
            low_weights(H - 4)
            low_weights(H - 2)
            def inverse_norms(v):
                pool.wait_ge(ss_set, v + 1)
                if not known(v) or v >= 1:
                    pool.wait_ge(vn_set, v)
                pool.tensor_tensor(rs[:, :], ss[:, :], neghalf[:, 0:3 * TB], ALU.pow).then_inc(rs_set, 1)

            def inverse_aggregate(v):
                pool.wait_ge(ssum_out, v + 1)
                if not known(v) or v >= 1:
                    pool.wait_ge(factor_set, v)
                pool.tensor_tensor(ra[:, :], sa2[:, :], neghalf[:, 0:TB], ALU.pow).then_inc(ra_set, 1)

            def gated_low(v):
                pool.wait_ge(ghi_set, v + 1)
                if not known(v) or v >= 1:
                    pool.wait_ge(ob_mm, 2 * v)
                pool.tensor_tensor(gated_lo[:, :], gated[:, :], gated_hi[:, :].bitcast(F32), ALU.subtract).then_inc(glo_set, 1)

            inverse_norms(0)
            ln_rstd_of(3 * B - 1)
            inverse_norms(1)
            gated_low(0)
            inverse_aggregate(0)
            inverse_norms(2)
            with pool.Fori(2, B * H - 1) as u:
                gated_low(u - 1)
                inverse_aggregate(u - 1)
                inverse_norms(u + 1)
            for v in range(B * H - 2, B * H):
                if v == B * H - 2:
                    ln_rstd_of(3 * B)
                gated_low(v)
                inverse_aggregate(v)
            with pool.Fori(3 * B + 1, 4 * B) as u:
                ln_rstd_of(u)

        @block.scalar
        def _(act):
            act.preload_act_table(ACT.Exp)
            act.wait_ge(const_in, 16)
            act.activation(ident_b[:, :], ident, ACT.Copy).then_inc(bf_const, 1)
            act.activation(mask_b[:, :], mask32, ACT.Copy).then_inc(bf_const, 1)
            act.activation(ident_h[:, :], ident, ACT.Copy).then_inc(bf_const, 1)
            act.wait_ge(wqk_in, 16)
            act.activation(big_hi[:, :], wqk_raw, ACT.Copy).then_inc(wa_hi, 1)
            act.wait_ge(wv_in, 16)
            act.activation(wv_hi[:, :, :].rearrange("p k c -> p (k c)"), wv_raw, ACT.Copy).then_inc(wa_hi, 1)

            def ln_high(u, b):
                for k in range(KD):
                    act.wait_ge(ln_tp, 2 * u + k + 1)
                    act.activation(xT_hi[:, k, at(b * S, S)], bank[ln_banks(u)[k]], ACT.Copy).then_inc(ln_hi, 1)

            def sum_weights(w):
                act.activation(junk[w], raw[w], ACT.Abs, accum_out=asum[:, w:w + 1]).then_inc(as_done, 1)
                act.wait_ge(as_done, w + 1)

            for b in range(B - 1):
                ln_high(b, b)
            act.wait_ge(ffn_in, 3 * 16)
            sum_weights(0)
            sum_weights(1)
            ln_high(B - 1, B - 1)
            sum_weights(2)
            def parts_act(b):
                for s in range(2):
                    n = 2 * b + s
                    act.wait_ge(pj_mm, 3 * n + 1)
                    if not known(b) or b >= 1:
                        act.wait_ge(pj_p3, n - 1)
                    act.activation(rot[:, s, 0], bank[2 + 3 * s][:, :], ACT.Copy).then_inc(pj_sem, 1)
                    act.wait_ge(pj_rot, n + 1)
                    act.wait_ge(pj_sem, n + 1)
                    if not known(b) or b >= 1:
                        act.wait_ge(pj_out[s], b * 16)
                    act.activation(parts[:, s, 0], rot[:, s], ACT.Copy).then_inc(pj_p1, 1)
                    act.wait_ge(pj_r1, n + 1)
                    act.activation(parts[:, s, 1], rot[:, s], ACT.Copy).then_inc(pj_p2, 1)

            parts_act(0)
            act.wait_ge(as_tot, 1)
            act.activation(total[:, :], bank[1][:, 0:3], ACT.Copy).then_inc(tot_out, 1)
            with act.Fori(1, B) as b:
                parts_act(b)

            def values_out(tiles):
                for t in tiles:
                    act.wait_ge(v_mm, t + 1)
                    act.activation(v_all[:, t // TB * 4:t // TB * 4 + 4, t % TB, :],
                                   bank[V_BANKS[t % 2]][:, 0:DM].rearrange("p (g c) -> p g c", g=4), ACT.Copy).then_inc(v_out, 1)

            def ot_out(k, i):
                act.wait_ge(pv_mm, k + 1)
                if not known(k) or k >= 2:
                    act.wait_ge(ao_set, k - 1)
                act.activation(OTs[:, i], bank[5][:, :], ACT.Copy).then_inc(ot_copied, 1)

            def exps(k, i, g):
                for j in range(3):
                    act.wait_ge(p2_mm, 12 * k + 3 * g + j + 1)
                    if g == 0 and j == 0 and (not known(k) or k >= 2):
                        act.wait_ge(pv_mm, k - 1)
                    n = (512, 512, 256)[j]
                    act.activation(PT[:, i, g, 512 * j:512 * j + n], bank[2 + j][:, 0:n], ACT.Exp,
                                   scale=float(DH) ** -0.5).then_inc(p2_exp, 1)

            def max_out(k):
                act.wait_ge(m_tr, k + 1)
                if not known(k) or k >= 1:
                    act.wait_ge(m_out, k * 2 * 16)
                act.activation(mT[:, :], bank[7].bitcast(BF16)[0:MROWS * 16, 0:P], ACT.Copy).then_inc(m_copied, 1)

            def spread(k, i, step):
                rows = OTs[DH:P:2 * DH, i, :]
                if step == 0:
                    act.wait_ge(ot_copied, k + 1)
                    act.dma_start(dscratch[i, 0], rows).then_inc(den_out, 16)
                elif step == 1:
                    act.wait_ge(den_out, 16 * (k + 1))
                    act.dma_start(den[:, :], dscratch[i, 0].rearrange("g (c w) -> (g c) w", c=2 * DH)).then_inc(den_in, 16)
                elif step == 2:
                    act.wait_ge(den_inv, k + 1)
                    act.dma_start(dscratch[i, 1].rearrange("g (c w) -> (g c) w", c=2 * DH), rden[:, :]).then_inc(inv_out, 16)
                else:
                    act.wait_ge(inv_out, 16 * (k + 1))
                    act.dma_start(rows, dscratch[i, 1]).then_inc(inv_in, 16)

            def act_group(k, i):
                if stage(k, 2):
                    ot_out(k - 2, i)
                    if through_dram(k - 2):
                        spread(k - 2, i, 0)
                if stage(k, -1):
                    max_out(k + 1)
                for g in range(4):
                    if stage(k, 0):
                        exps(k, i, g)
                    if stage(k, 2) and g and through_dram(k - 2):
                        spread(k - 2, i, g)

            values_out(range(0, TB))
            act_group(-1, 1)
            values_out(range(TB, NT))
            for k in range(4):
                act_group(k, k % 2)
            with act.Fori(2, NG // 2 - 1) as j:
                act_group(2 * j, 0)
                act_group(2 * j + 1, 1)
            for k in range(NG - 2, NG + 1):
                act_group(k, k % 2)

            ot_out(NG - 1, (NG - 1) % 2)

            act.wait_ge(ls_in, 16)
            act.activation(head[:, 0, :], ls_sb[:, 0, :], ACT.Exp).then_inc(ls_exp, 1)
            act.activation(head[:, 3, :], ls_sb[:, 1, :], ACT.Exp).then_inc(ls_exp, 1)

            def ffn_high(f, n):
                act.wait_ge(hid_set, n + 1)
                if not known(n) or n >= 3:
                    act.wait_ge(dn_mm, n - 2)
                act.activation(big_hi[:, (f % 3) * S:(f % 3 + 1) * S], hid[:, f % 2], ACT.Copy).then_inc(hi_set, 1)

            def ffn_act(v, b, own, ln=None, last=None):
                for f in range(NF):
                    n = NF * v + f
                    act.wait_ge(up_mm, 2 * n + 1)
                    if not known(n) or n >= 2:
                        act.wait_ge(hid_set, n - 1)
                    act.activation(fsig[:, f % 2], bank[f % 2][:, :], ACT.Sigmoid).then_inc(sig_set, 1)
                    if f or not known(b) or b:
                        ffn_high((f - 1) % NF, n - 1)
                    if known(v) and v == B - 1 and f == 1:
                        head_high(0)
                    if known(v) and v == 0 and f >= 2:
                        four = slice(4 * (f - 2), 4 * (f - 1))
                        act.wait_ge(wob_in, 16)
                        act.activation(wob_hi[:, four, :], wob[:, four, :], ACT.Copy).then_inc(wob_high, 1)
                    if ln is not None and f == 3:
                        ln_high(ln, b + 1)
                    if last is not None and ln is not None and f == 5:
                        ln_high(last, b - 1)
                if ln is None:
                    ffn_high(NF - 1, n)

            def ffn_act_all(first, u):
                if first:
                    att_act(H, 0, False, False, True)
                act.preload_act_table(ACT.Sigmoid)
                if first == 0:
                    ln_high(u, 0)
                ffn_batches(first, u, ffn_act, act.Fori)

            def att_act(h, b, nxt, cur, prv, split=False, between=None):
                u, p = B * h + b, b % 2

                def scores_relu(j):
                    n = TB * u + j
                    act.wait_ge(sim_mm, n + 1)
                    if not known(n) or n >= 2:
                        act.wait_ge(attn_set, n - 1)
                    act.activation(relu[:, j % 2], bank[3 + j % 2], ACT.Relu, bias=bias[:, b:b + 1]).then_inc(relu_set, 1)

                if prv:
                    act.wait_ge(av_mm, u)
                    if not known(u) or u >= 2:
                        act.wait_ge(ssum_mm, u - 1)
                    act.activation(agg2[:, :], bank[5], ACT.Square).then_inc(agg2_set, 1)
                    act.wait_ge(gated_set, u)
                    if not known(u) or u >= 2:
                        act.wait_ge(ob_mm, 2 * (u - 1))
                    act.activation(gated_hi[:, :], gated[:, :], ACT.Copy).then_inc(ghi_set, 1)
                if nxt:
                    act.wait_ge(kqv_mm, u + 2)
                    if not known(u) or u >= 0:
                        act.wait_ge(red_set, u + 1)
                    act.activation(sq[:, :, :].rearrange("p t c -> p (t c)"), psum[:, 0:1024], ACT.Square).then_inc(sq_set, 1)
                if cur:
                    act.wait_ge(tr_mm, u + 1)
                    if not known(u) or u >= 2:
                        act.wait_ge(sim_mm, 4 * (u - 1))
                    act.activation(kqT[p][:, :, :].rearrange("p a t -> p (a t)"), bank[7].bitcast(F16), ACT.Copy).then_inc(tr_out, 1)
                    act.wait_ge(trl_mm, u + 1)
                    act.activation(qlT[p][:, :], bank[4].bitcast(F16)[:, 0:S], ACT.Copy).then_inc(trl_out, 1)
                if prv:
                    act.wait_ge(norm_set, u)
                    act.activation(norm[:, 1, :], norm[:, 0, :], ACT.Tanh).then_inc(tanh_set, 1)
                if nxt:
                    act.wait_ge(gate_mm, u + 2)
                    act.activation(silu[:, :], bank[2], ACT.Silu).then_inc(silu_set, 1)
                if known(u) and u <= 0:
                    ln_high(3 * B - 1 + u, B - 1 + u)
                if cur:
                    act.wait_ge(bias_set, u + 1)
                    scores_relu(0)
                    scores_relu(1)
                if split:
                    head_high(h + 1)
                if cur:
                    scores_relu(2)
                    scores_relu(3)
                if between:
                    between()
                if nxt:
                    act.wait_ge(silu_set, u + 2)
                    if not known(u) or u >= 1:
                        act.wait_ge(gated_set, u)
                    act.activation(gate[1 - p][:, :], silu[:, :], ACT.Tanh).then_inc(gate_set, 1)
                    act.wait_ge(qk_set, u + 2)
                    if not known(u) or u >= 0:
                        act.wait_ge(trl_mm, u + 1)
                    act.activation(qk16[:, :, 0:4:2, :], qk[:, :, :, :], ACT.Copy).then_inc(q_hi, 1)

            def head_high(h):
                act.wait_ge(wb_in, 16 * (h + 1))
                if not known(h) or h >= 1:
                    act.wait_ge(gate_mm, B * h)
                act.activation(wb_h[:, :], wb_raw[:, :, :].rearrange("p k c -> p (k c)"),
                               ACT.Copy).then_inc(wb_hi, 1)

            ffn_act_all(0, B)
            act.wait_ge(r_set, 3)
            act.preload_act_table(ACT.Silu)
            att_act(-1, 3, True, False, False)
            for b in range(B):
                att_act(0, b, True, True, b > 0, b == 2)
            with act.Fori(1, H - 1) as h:
                for b in range(B):
                    att_act(h, b, True, True, True, b == 2)
            for b in range(B):
                att_act(H - 1, b, b < 3, True, True, between=(lambda: ln_high(3 * B, 0)) if b == 3 else None)
            ffn_act_all(B, 3 * B)

        @block.vector
        def _(dve):
            dve.memset(m3[:, :], 0.0).then_inc(m3_zero, 1)

            def ln_stat(u, b):
                for t in range(TB):
                    dve.bn_stats(stats[:, t, :], xres[:, at(b * TB + t, 1), :].rearrange("p o c -> p (o c)")).then_inc(ln_stats, 1)
                dve.wait_ge(ln_stats, TB * (u + 1))
                if not known(u):
                    dve.memset(hold[:, :], 0.0)
                for t in range(TB):
                    dve.bn_aggr(mv[:, t, :], stats[:, t, :]).then_inc(ln_mv, 1)

            def ln_norm(u, b):
                dve.wait_ge(ln_rstd, u + 1)
                dve.scalar_tensor_tensor(lnw[:, 2, :], mv[:, :, 0], -1.0, lnw[:, 1, :], ALU.mult, ALU.mult).then_inc(ln_nmr, 1)
                dve.wait_ge(ln_nmr, u + 1)
                if not known(u) or u >= 1:
                    dve.wait_ge(ln_tp, 2 * u)
                for t in range(TB):
                    dve.tensor_scalar(xn[:, t, :], xres[:, at(b * TB + t, 1), :].rearrange("p o c -> p (o c)"),
                                      lnw[:, 1, t:t + 1], lnw[:, 2, t:t + 1], ALU.mult, ALU.add).then_inc(ln_xn, 1)

            def ln_low(u, b):
                for k in range(KD):
                    dve.wait_ge(ln_hi, 2 * u + k + 1)
                    dve.tensor_tensor(xT_lo[:, k, at(b * S, S)], bank[ln_banks(u)[k]],
                                      xT_hi[:, k, at(b * S, S)].bitcast(F32), ALU.subtract).then_inc(ln_lo, 1)

            def weights_low():
                dve.wait_ge(wa_hi, 1)
                dve.tensor_tensor(big_lo[:, :], wqk_raw, big_hi[:, :].bitcast(F32), ALU.subtract).then_inc(wa_lo, 1)
                dve.wait_ge(wa_hi, 2)
                dve.tensor_tensor(wv_lo[:, :, :].rearrange("p k c -> p (k c)"), wv_raw,
                                  wv_hi[:, :, :].rearrange("p k c -> p (k c)").bitcast(F32), ALU.subtract).then_inc(wa_lo, 1)

            dve.wait_ge(x_in[0], 16)
            ln_stat(0, 0)
            for b in range(B):
                ln_norm(b, b)
                if b < B - 1:
                    dve.wait_ge(x_in[b + 1], 16)
                    ln_stat(b + 1, b + 1)
                if b == 0:
                    weights_low()
                ln_low(b, b)

            dve.wait_ge(trig_in, 16)

            def third_part(n, s):
                dve.wait_ge(pj_p2, n + 1)
                dve.tensor_tensor(parts[:, s, 2], rot[:, s], parts[:, s, 1], ALU.subtract).then_inc(pj_p3, 1)

            def rope_and_parts(b):
                for s in range(2):
                    n = 2 * b + s
                    if not known(b) or b >= 1:
                        dve.wait_ge(pj_p3, n - 1)
                    dve.wait_ge(pj_mm, 3 * n + 2)
                    dve.tensor_tensor(rot[:, s, 1], bank[3 + 3 * s][:, :], trig[:, 0], ALU.mult).then_inc(pj_t, 1)
                    dve.wait_ge(pj_mm, 3 * n + 3)
                    dve.tensor_tensor(OTs[:, 0], bank[4 + 3 * s][:, :], trig[:, 1], ALU.mult).then_inc(pj_t, 1)
                    dve.wait_ge(pj_t, 2 * n + 2)
                    dve.tensor_tensor(rot[:, s, 1], rot[:, s, 1], OTs[:, 0], ALU.add).then_inc(pj_rot, 1)
                    if not known(b) or n >= 1:
                        third_part(n - 1, 1 - s)
                    dve.wait_ge(pj_p1, n + 1)
                    dve.tensor_tensor(rot[:, s], rot[:, s], parts[:, s, 0], ALU.subtract).then_inc(pj_r1, 1)

            rope_and_parts(0)
            rope_and_parts(1)
            for w, q in enumerate((w12q[:, 0], w12q[:, 1], w3q[:, :, :])):
                dve.wait_ge(below_set, w + 1)
                dve.scalar_tensor_tensor(q, raw[w], thr[:, 1, w:w + 1], below[w], ALU.is_gt, ALU.subtract).then_inc(wq_set, 1)
            with dve.Fori(2, B) as b:
                rope_and_parts(b)
            third_part(2 * B - 1, 1)

            def row_max(k, g):
                for j, (to, its) in enumerate(P1_BANKS):
                    n = 12 * k + 3 * g + j
                    dve.wait_ge(p1_mm, n + 1)
                    if g == 0 and j == 0 and (not known(k) or k >= 1):
                        dve.wait_ge(m_split, 4 * k)
                    c = 0
                    for it in its:
                        last = dve.reduce_max(mx[:, 4 * g + it:4 * g + it + 1],
                                              bank[to][:, c:c + (it + 1) * P], AX.X)
                        c += (it + 1) * P
                    last.then_inc(p1_red, 1)

            def split_max(k):
                dve.wait_ge(p1_red, 12 * k + 12)
                if not known(k) or k >= 1:
                    dve.wait_ge(m_tr, k)
                dve.tensor_scalar(m3[:, 0:16], mx[:, :], -1.0, None, ALU.mult).then_inc(m_split, 1)
                dve.wait_ge(m_split, 4 * k + 1)
                dve.scalar_tensor_tensor(mxr[:, :], mx[:, :], -1.0, m3[:, 0:16], ALU.mult, ALU.subtract).then_inc(m_split, 1)
                dve.wait_ge(m_split, 4 * k + 2)
                dve.tensor_copy(m3[:, 16:32], mxr[:, :]).then_inc(m_split, 1)
                dve.wait_ge(m_split, 4 * k + 3)
                dve.tensor_tensor(m3[:, 32:48], mxr[:, :], m3[:, 16:32], ALU.subtract).then_inc(m_split, 1)

            def invert(k):
                dve.wait_ge(den_in, 16 * (k + 1))
                if not known(k) or k >= 1:
                    dve.wait_ge(inv_out, 16 * k)
                dve.reciprocal(rden[:, :], den[:, :]).then_inc(den_inv, 1)

            def normalise(k, i):
                if through_dram(k):
                    dve.wait_ge(inv_mm, k + 1)
                    inverse = bank[INV_BANK[at_end(k)]][:, :]
                else:
                    dve.wait_ge(rwide_set, k - NG + 3)
                    inverse = rwide
                if not known(k) or k >= 1:
                    dve.wait_ge(oa_mm, 2 * k)
                dve.tensor_tensor(values_of(k), OTs[:, i], inverse, ALU.mult).then_inc(ao_set, 1)

            def add_out(k, r):
                dve.wait_ge(oa_mm, 2 * k + r + 1)
                if not known(k) or 2 * k + r >= 1:
                    dve.wait_ge(x_a, 2 * k + r)
                rows = xres[:, at((k // 4) * TB + 2 * r, 2), :]
                dve.tensor_tensor(rows, bank[OUT_BANKS[at_end(k)][r]][:, :].rearrange("p (t c) -> p t c", t=2), rows,
                                  ALU.add).then_inc(x_a, 1)

            def invert_wide(k):
                dve.wait_ge(den_mm, k - NG + 3)
                if k == NG - 1:
                    dve.wait_ge(ao_set, k)
                dve.reciprocal(rwide, bank[DEN_BANK][:, :]).then_inc(rwide_set, 1)

            def dve_group(k, i):
                if stage(k, -2):
                    row_max(k + 2, 0)
                    row_max(k + 2, 1)
                if stage(k, 3):
                    normalise(k - 3, 1 - i)
                if stage(k, -2):
                    row_max(k + 2, 2)
                if stage(k, 3):
                    add_out(k - 3, 0)
                if stage(k, 2) and through_dram(k - 2):
                    invert(k - 2)
                if stage(k, -2):
                    row_max(k + 2, 3)
                    split_max(k + 2)
                if stage(k, 3):
                    add_out(k - 3, 1)

            for k in range(-2, 4):
                dve_group(k, k % 2)
            with dve.Fori(2, NG // 2 - 1) as j:
                dve_group(2 * j, 0)
                dve_group(2 * j + 1, 1)
            dve_group(NG - 2, NG % 2)
            ln_stat(B, 0)
            dve_group(NG - 1, (NG - 1) % 2)
            ln_norm(B, 0)
            invert_wide(NG - 2)
            dve_group(NG, NG % 2)
            normalise(NG - 2, NG % 2)
            invert_wide(NG - 1)
            ln_low(B, 0)
            add_out(NG - 2, 0)
            add_out(NG - 2, 1)
            normalise(NG - 1, (NG - 1) % 2)

            def ffn_low(f, n):
                dve.wait_ge(hi_set, n + 1)
                dve.tensor_tensor(big_lo[:, (f % 3) * S:(f % 3 + 1) * S], hid[:, f % 2],
                                  big_hi[:, (f % 3) * S:(f % 3 + 1) * S].bitcast(F32), ALU.subtract).then_inc(lo_set, 1)

            def ffn_add(v, b):
                dve.wait_ge(dn_mm, NF * (v + 1))
                for r in range(2):
                    rows = xres[:, at(b * TB + 2 * r, 2), :]
                    dve.tensor_tensor(rows, bank[DOWN_BANKS[r]].rearrange("p (t c) -> p t c", t=2), rows, ALU.add).then_inc(x_f, 1)

            def ffn_dve(v, b, own, ln=None, last=None):
                if known(v) and v == B:
                    att_dve(H, 0, False, False, True, halves=(0,))
                if ln is not None:
                    ln_stat(ln, b + 1)
                for f in range(NF):
                    n = NF * v + f
                    dve.wait_ge(sig_set, n + 1)
                    dve.wait_ge(up_mm, 2 * n + 2)
                    if not known(n) or n >= 2:
                        dve.wait_ge(lo_set, n - 1)
                    dve.tensor_tensor(hid[:, f % 2], bank[2 + f % 2][:, :], fsig[:, f % 2], ALU.mult).then_inc(hid_set, 1)
                    if f or not known(b) or b:
                        ffn_low((f - 1) % NF, n - 1)
                    if known(v) and v == B and f == 1:
                        att_dve(H, 0, False, False, True, halves=(1,))
                        dve.wait_ge(x_b, 2 * B * H)
                    if f == 1 and (not known(b) or b):
                        ffn_add(v - 1, b - 1)
                    if f == 2 and known(v) and v == B - 1:
                        head_low(0)
                    if f == 1 and known(v) and v == 0:
                        add_out(NG - 1, 0)
                        add_out(NG - 1, 1)
                        dve.wait_ge(x_a, 2 * NG)
                    if ln is not None and f == 2:
                        ln_norm(ln, b + 1)
                    if last is not None and f == 2:
                        dve.wait_ge(x_f, 2 * v)
                        dve.memset(hold[:, :], 0.0)
                        ln_stat(last, b - 1)
                    if ln is not None and f == 4:
                        ln_low(ln, b + 1)
                    if last is not None and f == 4:
                        ln_norm(last, b - 1)
                    if last is not None and ln is not None and f == 5:
                        ln_low(last, b - 1)
                if ln is None:
                    ffn_low(NF - 1, n)
                if ln is None and v > B:
                    ffn_add(v, b)

            dve.wait_ge(ls_exp, 2)
            dve.tensor_scalar(head[:, 0, :], head[:, 0, :], 1.0, None, ALU.add).then_inc(r_set, 1)
            dve.wait_ge(r_set, 1)
            dve.reciprocal(head[:, 1, :], head[:, 0, :]).then_inc(r_set, 1)
            dve.wait_ge(r_set, 2)
            dve.tensor_scalar(head[:, 2, :], head[:, 1, :], -1.0, 1.0, ALU.mult, ALU.add).then_inc(r_set, 1)
            dve.wait_ge(x_a, 2 * NG - 2)
            def head_low(h):
                dve.wait_ge(wb_hi, h + 1)
                dve.tensor_tensor(wb_l[:, :], wb_raw[:, :, :].rearrange("p k c -> p (k c)"),
                                  wb_h[:, :].bitcast(F32), ALU.subtract).then_inc(wb_lo, 1)

            proj = psum[:, 0:1024].rearrange("p (t c) -> p t c", t=TB)

            def att_dve(h, b, nxt, cur, prv, split=False, between=None, halves=(0, 1)):
                u, p = B * h + b, b % 2
                past = lambda n: not known(u) or u >= n

                def square(j):
                    dve.wait_ge(relu_set, TB * u + j + 1)
                    if j == 0 and past(1):
                        dve.wait_ge(av_mm, u)
                    dve.tensor_tensor(attn[:, j], relu[:, j % 2], relu[:, j % 2], ALU.mult).then_inc(attn_set, 1)

                def add_head(r):
                    dve.wait_ge(ob_mm, 2 * (u - 1) + r + 1)
                    for t in range(2):
                        row = xres[:, ((b - 1) % B) * TB + 2 * r + t, :]
                        last = dve.scalar_tensor_tensor(row, bank[6][:, t * DM:(t + 1) * DM], norm[:, 2, 2 * r + t:2 * r + t + 1],
                                                        row, ALU.mult, ALU.add)
                    last.then_inc(x_b, 1)

                if cur:
                    dve.tensor_copy(bias[:, b:b + 1], head[:, 2, at(h, 1)]).then_inc(bias_set, 1)
                if prv and 0 in halves:
                    dve.wait_ge(agg2_set, u)
                    dve.wait_ge(gate_set, u)
                    if past(2):
                        dve.wait_ge(glo_set, u - 1)
                    dve.tensor_tensor(gated[:, :], bank[5], gate[1 - p][:, :], ALU.mult).then_inc(gated_set, 1)
                if cur:
                    dve.wait_ge(q_hi, u + 1)
                    dve.tensor_tensor(qk16[:, :, 1:5:3, :], qk[:, :, :, :], qk16[:, :, 0:4:2, :], ALU.subtract).then_inc(q_lo, 1)
                    dve.wait_ge(q_lo, u + 1)
                    dve.tensor_copy(qk16[:, :, 3:6:2, :], qk16[:, :, 2:5:2, :]).then_inc(q_dup, 1)
                if prv and 0 in halves:
                    dve.wait_ge(ssum_mm, u)
                    dve.tensor_scalar(sa2[:, :], bank[3][:, 0:TB], NORM_EPS ** 2, None, ALU.max).then_inc(ssum_out, 1)
                if known(u) and u == 0:
                    ln_norm(3 * B - 1, B - 1)
                if nxt:
                    dve.wait_ge(sq_set, u + 2)
                    if past(0):
                        dve.wait_ge(rs_set, u + 1)
                    dve.tensor_reduce(ss[:, 0:8].rearrange("p (t a) -> p t a", t=TB),
                                      sq[:, :, 0:2 * DK].rearrange("p t (a d) -> p t a d", a=2), AX.X, ALU.add).then_inc(kq_red_set, 1)
                    dve.tensor_reduce(ss[:, 8:12], sq[:, :, 2 * DK:], AX.X, ALU.add).then_inc(red_set, 1)
                    dve.wait_ge(red_set, u + 2)
                    dve.tensor_scalar(ss[:, :], ss[:, :], NORM_EPS ** 2, None, ALU.max).then_inc(ss_set, 1)
                if prv and 0 in halves:
                    hp = h - (1 if b == 0 else 0)
                    dve.wait_ge(ra_set, u)
                    dve.tensor_tensor(norm[:, 0, :], sa2[:, :], ra[:, :], ALU.mult).then_inc(norm_set, 1)
                    dve.wait_ge(tanh_set, u)
                    dve.scalar_tensor_tensor(norm[:, 2, :], norm[:, 1, :], head[:, 3, at(hp, 1)], ra[:, :],
                                             ALU.mult, ALU.mult).then_inc(factor_set, 1)
                    dve.wait_ge(factor_set, u)
                    add_head(0)
                if known(u) and u == 0:
                    ln_low(3 * B - 1, B - 1)
                if cur:
                    square(0)
                    square(1)
                if between:
                    between()
                if nxt:
                    hn = h + (b + 1) // 4
                    dve.wait_ge(rs_set, u + 2)
                    inv_q = rs[:, 0:8].rearrange("p (t a) -> p t a", t=TB)[:, :, 1]
                    dve.tensor_scalar(inv_q, inv_q, head[:, 1, at(hn, 1)], None, ALU.mult).then_inc(rq_set, 1)
                    dve.wait_ge(rq_set, u + 2)
                    dve.tensor_tensor(qk[:, :, :, :], proj[:, :, 0:2 * DK].rearrange("p t (a d) -> p t a d", a=2),
                                      rs[:, 0:8].rearrange("p (t a o) -> p t a o", t=TB, o=1).broadcast_to([P, TB, 2, DK]),
                                      ALU.mult).then_inc(qk_set, 1)
                if cur:
                    square(2)
                if nxt:
                    dve.tensor_tensor(vn[1 - p][:, :, :], proj[:, :, 2 * DK:],
                                      rs[:, 8:12].rearrange("p (t o) -> p t o", o=1).broadcast_to([P, TB, DV]),
                                      ALU.mult).then_inc(vn_set, 1)
                if cur:
                    square(3)
                if split:
                    head_low(h + 1)
                if prv and 1 in halves:
                    add_head(1)

            def last_sums():
                ln_low(3 * B - 2, B - 2)
                ffn_add(B - 1, B - 1)

            ffn_batches(0, B, ffn_dve, dve.Fori)
            att_dve(-1, 3, True, False, False, between=last_sums)
            dve.wait_ge(x_f, 2 * B)
            ln_stat(3 * B - 1, B - 1)
            for b in range(B):
                att_dve(0, b, True, True, b > 0, b == 2)
            with dve.Fori(1, H - 1) as h:
                for b in range(B):
                    att_dve(h, b, True, True, True, b == 2)
            att_dve(H - 1, 0, True, True, True)
            att_dve(H - 1, 1, True, True, True)
            dve.wait_ge(x_b, 2 * (B * (H - 1) + 1))
            ln_stat(3 * B, 0)
            att_dve(H - 1, 2, True, True, True)
            ln_norm(3 * B, 0)
            att_dve(H - 1, 3, False, True, True)
            ln_low(3 * B, 0)
            ffn_batches(B, 3 * B, ffn_dve, dve.Fori)

        @block.tensor
        def _(pe):
            def ln_transpose(u):
                for k in range(KD):
                    pe.wait_ge(ln_xn, TB * (u + 1))
                    if not known(u) or u >= 1:
                        pe.wait_ge(ln_lo, 2 * u - 1 + k)
                    for t in range(TB):
                        last = pe.transpose(bank[ln_banks(u)[k]][:, t * P:(t + 1) * P], xn[:, t, k * P:(k + 1) * P], ident)
                    last.then_inc(ln_tp, 1)

            def project_qk(b, s):
                n = 2 * b + s
                if not known(b) or b >= 1:
                    pe.wait_ge(pj_rot, n - 1)
                    pe.wait_ge(pj_sem, n - 1)
                for m in range(3):
                    c = (3 * s + m) * P
                    for i, (w, xt) in enumerate(((big_hi, xT_hi), (big_hi, xT_lo), (big_lo, xT_hi))):
                        for k in range(KD):
                            last = pe.matmul(bank[2 + 3 * s + m][:, :], w[:, k * 768 + c:k * 768 + c + P],
                                             xt[:, k, at(b * S, S)], start=(i == 0 and k == 0), stop=(i == 2 and k == KD - 1))
                    last.then_inc(pj_mm, 1)

            pe.wait_ge(const_in, 16)
            for u in range(B - 1):
                ln_transpose(u)
            pe.wait_ge(wa_lo, 1)
            project_qk(0, 0)
            ln_transpose(B - 1)
            pe.wait_ge(ln_lo, B * KD)
            project_qk(0, 1)
            pe.wait_ge(as_done, 3)
            pe.matmul(bank[1][:, 0:3], ones, asum[:, :], start=True, stop=True).then_inc(as_tot, 1)
            with pe.Fori(1, B) as b:
                project_qk(b, 0)
                project_qk(b, 1)

            def project_v(t):
                if t >= 2:
                    pe.wait_ge(v_out, t - 1)
                for i, (xt, w) in enumerate(((xT_hi, wv_hi), (xT_hi, wv_lo), (xT_lo, wv_hi))):
                    for k in range(KD):
                        last = pe.matmul(bank[V_BANKS[t % 2]][:, 0:DM], xt[:, k, t * P:(t + 1) * P], w[:, k, :],
                                         start=(i == 0 and k == 0), stop=(i == 2 and k == KD - 1))
                last.then_inc(v_mm, 1)

            pe.wait_ge(wa_lo, 2)
            pe.wait_ge(tot_out, 1)
            pe.wait_ge(bf_const, 2)
            pe.wait_ge(ks_ones, 1)
            pe.wait_ge(m3_zero, 1)

            def scores1(k, g):
                if g == 0:
                    pe.wait_ge(stack_in, (k + 1) * len(STACK) * 16)
                r = at(k % 4, 1)
                for j, (to, its) in enumerate(P1_BANKS):
                    n = 12 * k + 3 * g + j
                    if not known(k) or n >= 3:
                        pe.wait_ge(p1_red, n - 2)
                    to, c = bank[to], 0
                    for it in its:
                        pe.matmul(to[:, c:c + (it + 1) * P], qs[0:KROWS, r, g, it * P:(it + 1) * P].rearrange("p o c -> p (o c)"),
                                  ks[0:KROWS, r, g, 0:(it + 1) * P].rearrange("p o c -> p (o c)"), start=True, stop=False,
                                  skip_group_check=True)
                        last = pe.matmul(to[:, c + it * P:c + (it + 1) * P], ident_b[:, :], mask_b[:, :], start=False, stop=True,
                                         skip_group_check=True)
                        c += (it + 1) * P
                    last.then_inc(p1_mm, 1)

            def scores2(k, g):
                if g == 0:
                    pe.wait_ge(m_in, (k + 1) * 16)
                r = at(k % 4, 1)
                for j, (to, jts) in enumerate(P2_BANKS):
                    n = 12 * k + 3 * g + j
                    if not known(k) or n >= 3:
                        pe.wait_ge(p2_exp, n - 2)
                    to, c = bank[to], 0
                    for jt in jts:
                        w = S - jt * P
                        pe.matmul(to[:, c:c + w], ks[0:KROWS + MROWS, r, g, jt * P:(jt + 1) * P].rearrange("p o c -> p (o c)"),
                                  qs[0:KROWS + MROWS, r, g, jt * P:S].rearrange("p o c -> p (o c)"), start=True, stop=False,
                                  skip_group_check=True)
                        last = pe.matmul(to[:, c:c + P], mask_b[:, :], ident_b[:, :], start=False, stop=True,
                                         skip_group_check=True)
                        c += w
                    last.then_inc(p2_mm, 1)

            def values(k, i, jt, heads):
                if jt == 0:
                    pe.wait_ge(p2_exp, 12 * k + 3 * heads[-1] + 3)
                if jt == 0 and heads[0] == 0:
                    pe.wait_ge(vg_set, k + 1)
                    if not known(k) or k >= 1:
                        pe.wait_ge(ot_copied, k)
                for g in heads:
                    w = S - jt * P
                    last = pe.matmul(bank[5][2 * DH * g:2 * DH * (g + 1), jt * P:S], vg[i][:, jt, g, :],
                                     PT[:, i, g, P2_AT[jt]:P2_AT[jt] + w], start=(jt == 0), stop=(jt == TB - 1),
                                     skip_group_check=True)
                if jt == TB - 1 and heads[-1] == 3:
                    last.then_inc(pv_mm, 1)

            def inverses(k, i):
                pe.wait_ge(inv_in, 16 * (k + 1))
                if at_end(k):
                    pe.wait_ge(p2_exp, 12 * NG)
                    pe.wait_ge(ao_set, k)
                else:
                    pe.wait_ge(m_copied, min(k + 5, NG) if known(k) else k + 5)
                    if not known(k) or k >= 1:
                        pe.wait_ge(x_a, 2 * k)
                pe.matmul(bank[INV_BANK[at_end(k)]][:, :], sel, OTs[:, i], start=True, stop=True).then_inc(inv_mm, 1)

            def denominators(k, i):
                pe.wait_ge(ot_copied, k + 1)
                if k == NG - 1:
                    pe.wait_ge(rwide_set, 1)
                pe.wait_ge(p2_exp, 12 * NG)
                pe.matmul(bank[DEN_BANK][:, :], sel, OTs[:, i], start=True, stop=True).then_inc(den_mm, 1)

            def transpose_max(k):
                pe.wait_ge(m_split, 4 * k + 4)
                if not known(k) or k >= 1:
                    pe.wait_ge(m_copied, k)
                if not known(k) or k >= 5:
                    pe.wait_ge(x_a, 2 * (k - 4))
                pe.transpose(bank[7].bitcast(BF16)[:, 0:P], m3[:, :], ident_b[:, :]).then_inc(m_tr, 1)

            def project_out(k, r):
                pe.wait_ge(ao_set, k + 1)
                if not known(k) or 2 * k + r >= 1:
                    pe.wait_ge(x_a, 2 * k - 1 + r if at_end(k) and at_end(k - 1) else 2 * k + r)
                for t in range(2):
                    last = pe.matmul(bank[OUT_BANKS[at_end(k)][r]][:, t * DM:(t + 1) * DM], values_of(k)[:, (2 * r + t) * P:(2 * r + t + 1) * P],
                                     woa[:, at(k % 4, 1), :].rearrange("p o c -> p (o c)"), start=True, stop=True)
                last.then_inc(oa_mm, 1)

            def pe_group(k, i, v=None):
                for step in range(8):
                    if stage(k, -2) and step % 2 == 0:
                        scores1(k + 2, step // 2)
                    if v is not None and step % 2 == 0:
                        project_v(v + step // 2)
                    if stage(k, 0) and step % 2 == 1:
                        scores2(k, step // 2)
                    if stage(k, 1):
                        values(k - 1, 1 - i, step // 2, (0, 1) if step % 2 == 0 else (2, 3))
                    if stage(k, -1) and step == 0:
                        transpose_max(k + 1)
                    if stage(k, 3) and step == 2 and through_dram(k - 3):
                        inverses(k - 3, 1 - i)
                    if stage(k, 3) and step in (4, 6):
                        project_out(k - 3, step // 2 - 2)

            pe.wait_ge(pj_rot, 2 * B)
            pe.wait_ge(pj_sem, 2 * B)
            pe.wait_ge(woa_in, 16)
            pe_group(-2, 0, v=0)
            pe_group(-1, 1, v=TB)
            for t in range(2 * TB, NT):
                project_v(t)
            pe.wait_ge(v_out, NT)
            for k in range(4):
                pe_group(k, k % 2)
            with pe.Fori(2, NG // 2 - 1) as j:
                pe_group(2 * j, 0)
                pe_group(2 * j + 1, 1)
            for k in range(NG - 2, NG):
                pe_group(k, k % 2)
            denominators(NG - 2, NG % 2)
            pe_group(NG, NG % 2)
            denominators(NG - 1, (NG - 1) % 2)
            ln_transpose(B)
            for r in range(2):
                project_out(NG - 2, r)

            def ffn_up(f, n, b):
                if not known(n) or n >= 2:
                    pe.wait_ge(hid_set, n - 1)
                for w in range(2):
                    for i, xt in enumerate((xT_hi, xT_lo)):
                        for k in range(KD):
                            last = pe.matmul(bank[2 * w + f % 2][:, :], w12q[:, w, k, f * P:(f + 1) * P], xt[:, k, at(b * S, S)],
                                             start=(i == 0 and k == 0), stop=(i == 1 and k == KD - 1))
                    last.then_inc(up_mm, 1)

            def ffn_down(f, n, v):
                pe.wait_ge(lo_set, n + 1)
                if f == 0 and known(v) and v == 0:
                    pe.wait_ge(x_a, 2 * NG)
                elif f == 0:
                    pe.wait_ge(x_f, 2 * v)
                for t in range(TB):
                    for i, part in enumerate((big_hi, big_lo)):
                        last = pe.matmul(bank[DOWN_BANKS[t // 2]][:, (t % 2) * DM:(t % 2 + 1) * DM],
                                         part[:, (f % 3) * S + t * P:(f % 3) * S + (t + 1) * P], w3q[:, f, :],
                                         start=(f == 0 and t % 2 == 0 and i == 0), stop=(f == NF - 1 and i == 1), skip_group_check=True)
                last.then_inc(dn_mm, 1)

            def ffn_pe(v, b, own, ln=None, last=None):
                pe.wait_ge(ln_lo, 2 * (own + 1))
                for f in range(NF):
                    n = NF * v + f
                    if known(v) and v == B and f == 1:
                        pe.wait_ge(ssum_out, B * H)
                    ffn_up(f, n, b)
                    if known(v) and v == 0 and f == 1:
                        project_out(NG - 1, 0)
                        project_out(NG - 1, 1)
                    if known(v) and v == B and f < 2:
                        att_pe(H, 0, False, False, True, halves=(f,))
                    if f >= 2:
                        ffn_down(f - 2, n - 2, v)
                    elif not known(b) or b:
                        ffn_down(f - 2 + NF, n - 2, v - 1)
                    if ln is not None and f == 3:
                        ln_transpose(ln)
                    if known(v) and v == B - 1 and f == 5:
                        pe.wait_ge(sig_set, NF * B)
                        pe.wait_ge(hid_set, NF * B - 1)
                        att_pe(-1, 3, True, False, False)
                    if last is not None and f == 5:
                        ln_transpose(last)
                if ln is None:
                    for f in range(NF - 2, NF):
                        ffn_down(f, NF * v + f, v)

            def att_pe(h, b, nxt, cur, prv, between=None, halves=(0, 1)):
                u, p = B * h + b, b % 2
                bn = (b + 1) % B
                past = lambda n: not known(u) or u >= n

                def project_kqv():
                    if bn == 0:
                        pe.wait_ge(wb_lo, h + 2)
                    if past(0):
                        pe.wait_ge(vn_set, u + 1)
                    for t in range(TB):
                        tok = slice(bn * S + t * P, bn * S + (t + 1) * P)
                        for i, (xt, w) in enumerate(((xT_hi, wb_h), (xT_hi, wb_l), (xT_lo, wb_h))):
                            for k in range(KD):
                                last = pe.matmul(psum[:, t * 2 * DV:(t + 1) * 2 * DV], xt[:, k, tok], w[:, k * HW:k * HW + 2 * DV],
                                                 start=(i == 0 and k == 0), stop=(i == 2 and k == KD - 1))
                    last.then_inc(kqv_mm, 1)

                def project_gate():
                    if past(0):
                        pe.wait_ge(silu_set, u + 1)
                    for i, (w, xt) in enumerate(((wb_h, xT_hi), (wb_l, xT_hi), (wb_h, xT_lo))):
                        for k in range(KD):
                            last = pe.matmul(bank[2], w[:, k * HW + 2 * DV:(k + 1) * HW], xt[:, k, bn * S:(bn + 1) * S],
                                             start=(i == 0 and k == 0), stop=(i == 2 and k == KD - 1))
                    last.then_inc(gate_mm, 1)

                def transpose_kq():
                    pe.wait_ge(q_dup, u + 1)
                    if past(1):
                        pe.wait_ge(tr_out, u)
                    for a in range(2):
                        for t in range(TB):
                            last = pe.transpose(bank[7].bitcast(F16)[:, (a * TB + t) * P:(a * TB + t + 1) * P],
                                                qk16[:, t, 2 * a:2 * a + 2, :].rearrange("p a d -> p (a d)"), ident_h[:, :])
                    last.then_inc(tr_mm, 1)
                    if past(1):
                        pe.wait_ge(relu_set, TB * u)
                    for t in range(TB):
                        last = pe.transpose(bank[4].bitcast(F16)[:, t * P:(t + 1) * P],
                                            qk16[:, t, 4:6, :].rearrange("p a d -> p (a d)"), ident_h[:, :])
                    last.then_inc(trl_mm, 1)

                def similarities(j):
                    n = TB * u + j
                    if j == 0:
                        pe.wait_ge(tr_out, u + 1)
                        pe.wait_ge(trl_out, u + 1)
                        if past(1):
                            pe.wait_ge(ssum_out, u)
                    if not known(n) or n >= 2:
                        pe.wait_ge(relu_set, n - 1)
                    k_t = kqT[p][:, 0, j * P:(j + 1) * P]
                    pe.matmul(bank[3 + j % 2], k_t, kqT[p][:, 1, :], start=True, stop=False)
                    pe.matmul(bank[3 + j % 2], k_t, qlT[p][:, :], start=False, stop=True).then_inc(sim_mm, 1)

                def aggregate(j):
                    pe.wait_ge(attn_set, TB * u + j + 1)
                    if j == 0:
                        pe.wait_ge(vn_set, u + 1)
                        if past(1):
                            pe.wait_ge(gated_set, u)
                    last = pe.matmul(bank[5], vn[p][:, j, :], attn[:, j], start=(j == 0), stop=(j == TB - 1))
                    if j == TB - 1:
                        last.then_inc(av_mm, 1)

                def sum_squares():
                    pe.wait_ge(agg2_set, u)
                    pe.wait_ge(relu_set, TB * u - 1)
                    for t in range(TB):
                        last = pe.matmul(bank[3][:, t:t + 1], agg2[:, t * P:(t + 1) * P], ones[:, 0:1], start=True, stop=True)
                    last.then_inc(ssum_mm, 1)

                def project(r):
                    hp = h - (1 if b == 0 else 0)
                    pe.wait_ge(glo_set, u)
                    if r == 1 or past(2):
                        pe.wait_ge(x_b, 2 * (u - 1) + r)
                    for t in range(2):
                        for i, (g, w) in enumerate(((gated_hi, wob_hi), (gated_hi, wob_lo), (gated_lo, wob_hi))):
                            last = pe.matmul(bank[6][:, t * DM:(t + 1) * DM], g[:, (2 * r + t) * P:(2 * r + t + 1) * P],
                                             w[:, at(hp, 1), :].rearrange("p o c -> p (o c)"), start=(i == 0), stop=(i == 2))
                    last.then_inc(ob_mm, 1)

                if nxt:
                    project_kqv()
                if prv and 0 in halves:
                    sum_squares()
                if cur:
                    transpose_kq()
                if prv and 0 in halves:
                    project(0)
                if nxt:
                    project_gate()
                if between:
                    between()
                if cur:
                    similarities(0)
                    similarities(1)
                if prv and 1 in halves:
                    project(1)
                if cur:
                    similarities(2)
                    aggregate(0)
                    similarities(3)
                    aggregate(1)
                    aggregate(2)
                    aggregate(3)

            pe.wait_ge(rwide_set, 2)
            pe.wait_ge(ao_set, NG - 2)
            ffn_batches(0, B, ffn_pe, pe.Fori)
            pe.wait_ge(bf_const, 3)
            for b in range(B):
                if b == 0:
                    pe.wait_ge(ln_lo, 2 * (3 * B - 1))
                elif b == 1:
                    pe.wait_ge(wob_low, H // 2)
                elif b == 2:
                    pe.wait_ge(ln_lo, 2 * 3 * B)
                att_pe(0, b, True, True, b > 0, between=(lambda: ln_transpose(3 * B - 1)) if b == 0 else None)
            with pe.Fori(1, H - 1) as h:
                for b in range(B):
                    att_pe(h, b, True, True, True)
            for b in range(B):
                att_pe(H - 1, b, b < 3, True, True, between=(lambda: ln_transpose(3 * B)) if b == 3 else None)
            ffn_batches(B, 3 * B, ffn_pe, pe.Fori)


def laid_out(inputs):
    import numpy as np

    a = {k: np.asarray(v) for k, v in inputs.items()}
    half = DH // 2
    dim_major = np.array([h * half + d for d in range(half) for h in range(H)])
    swapped = np.array([h * half + (d + half // 2) % half for d in range(half) for h in range(H)])
    wqk = np.concatenate([a["L0_attn_a_Wq_sem"].T[:, dim_major], a["L0_attn_a_Wq_geo"].T[:, dim_major],
                          a["L0_attn_a_Wq_geo"].T[:, swapped], a["L0_attn_a_Wk_sem"].T[:, dim_major],
                          a["L0_attn_a_Wk_geo"].T[:, dim_major], a["L0_attn_a_Wk_geo"].T[:, swapped]], axis=1)
    wo = a["L0_attn_a_Wo"].T.reshape(4, 4, DH, DM)
    wo_a = np.zeros((4, 4, 2 * DH, DM), np.float32)
    wo_a[:, :, :DH] = wo
    wo_a = wo_a.reshape(4, P, DM).transpose(1, 0, 2)
    qg = a["L0_attn_b_Wqg"].reshape(DM, H, DK + DV)
    kv = a["L0_attn_b_Wkv"].reshape(DM, H, DK + DV)
    wb = np.concatenate([kv[:, :, :DK], qg[:, :, :DK], kv[:, :, DK:], qg[:, :, DK:]], axis=2)
    ls = np.broadcast_to(np.stack([a["L0_attn_b_ls_iaw"], a["L0_attn_b_ls_hws"]])[None], (P, 2, H))

    d = np.arange(P) // H
    inv_freq = (np.float32(1.0) / np.float32(10000.0) ** (np.arange(0, half, 2, dtype=np.float32) / np.float32(half))).astype(np.float32)
    angle = (np.arange(S, dtype=np.float32)[None, :] * inv_freq[d % (half // 2)][:, None]).astype(np.float32)
    sign = np.where(d < half // 2, -1.0, 1.0)[:, None]
    i = np.arange(P)
    sel = ((i[:, None] % 32 == DH) & (i[:, None] // 32 == i[None, :] // 32))
    consts = np.concatenate([np.eye(P), np.where(i[None, :] > i[:, None], MASKED, 0.0), sel, np.ones((P, P)),
                             np.cos(angle), np.sin(angle) * sign], axis=1)
    w12 = np.zeros((2, DM, FP), np.float32)
    w12[:, :, :FF] = a["L0_ffn_w1"].T, a["L0_ffn_w2"].T
    w3 = np.zeros((FP, DM), np.float32)
    w3[:FF] = a["L0_ffn_w3"].T
    arrays = {
        "x": a["L0_attn_a_x"].reshape(TOK, DM), "consts": consts.astype(np.float32), "wqk": wqk,
        "wv": a["L0_attn_a_Wv"].T, "wo_a": wo_a, "w12": w12,
        "w3": w3, "wb": wb, "wo_b": a["L0_attn_b_Wo"], "ls": ls,
    }
    return {k: np.ascontiguousarray(v) for k, v in arrays.items()}


def kernel(**inputs):
    import concourse.bacc as bacc
    from concourse.bass_utils import run_bass_kernel_spmd

    arrays = laid_out(inputs)
    nc = bacc.Bacc("TRN2", target_bir_lowering=False, num_devices=1)
    args = {k: nc.dram_tensor("in_" + k, v.shape, mybir.dt.from_np(v.dtype), kind="ExternalInput").ap() for k, v in arrays.items()}
    out = nc.dram_tensor("out_x", (TOK, DM), F32, kind="ExternalOutput").ap()
    program(nc, out=out, **args)
    r = run_bass_kernel_spmd(nc, [{"in_" + k: v for k, v in arrays.items()}], core_ids=[0])
    return r.results[0]["out_x"].reshape(B, S, DM)
```
